# Optimizing a Trainium2 kernel written in Bass

```python
import numpy as np
import jax
import jax.numpy as jnp

def _softmax(x, axis=-1):
    return jax.nn.softmax(x, axis=axis)

def _gelu(x):
    return jax.nn.gelu(x, approximate=True)

def _silu(x):
    return jax.nn.silu(x)

def _sigmoid(x):
    return jax.nn.sigmoid(x)

def _layernorm(x, axis=-1, eps=1e-05):
    m = jnp.mean(x, axis=axis, keepdims=True)
    v = jnp.var(x, axis=axis, keepdims=True)
    return (x - m) / jnp.sqrt(v + eps)

def _scatter_add(tgt, idx, src, axis=0):
    return tgt.at[idx].add(src)

def _segment_sum(src, seg, n):
    return jax.ops.segment_sum(src, seg, n)
kernel_name = 'mk_audio_tower_d4_tok_audfeat256_r4_3212f0'

def setup_inputs(seed: int=0):
    np.random.seed(seed)
    _w = jnp.asarray

    def _rec_inputs():
        import jax
        import jax.numpy as jnp
        _rk = jax.random.key(seed)
        x = -0.000392918 + 0.999932 * jax.random.normal(jax.random.fold_in(_rk, 1), (64, 750, 16), jnp.float32)
        return x
    x = _rec_inputs()

    def _L0_tok_setup():
        import jax, jax.numpy as jnp
        import numpy as np
        PATCH = 16
        STRIDE = 8
        EPS = 1e-05
        key = jax.random.key(seed)
        k1, k2, k3 = jax.random.split(key, 3)
        B, S, F, D = (128, 2048, 16, 64)
        in_dim = F * PATCH
        x = jax.random.normal(k1, (B, S, F), dtype=jnp.float32)
        bound = 1.0 / np.sqrt(in_dim)
        W = jax.random.uniform(k2, (D, in_dim), minval=-bound, maxval=bound, dtype=jnp.float32)
        b = jax.random.uniform(k3, (D,), minval=-bound, maxval=bound, dtype=jnp.float32)
        gamma = jnp.ones((D,), dtype=jnp.float32)
        beta = jnp.zeros((D,), dtype=jnp.float32)
        return {'x': x, 'W': W, 'b': b, 'gamma': gamma, 'beta': beta}
    _L0_tok_all = _L0_tok_setup()
    _L0_tok_in = {k: v for k, v in _L0_tok_all.items() if k in ('W', 'b', 'gamma', 'beta')}
    del _L0_tok_all

    def _L0_attn_setup():
        import jax, jax.numpy as jnp
        import numpy as np
        S, B, D, H, DH = (128, 32, 64, 8, 32)
        LN_EPS = 1e-05

        def elu_p1(x):
            return jax.nn.elu(x) + 1.0

        def sum_norm(x):
            return x / jnp.sum(x, axis=-1, keepdims=True)

        def layer_norm(x, g, b):
            mu = jnp.mean(x, axis=-1, keepdims=True)
            var = jnp.mean(jnp.square(x - mu), axis=-1, keepdims=True)
            return (x - mu) * jax.lax.rsqrt(var + LN_EPS) * g + b

        def _fast_rnn_forward(x, slow_W, out_W, ln_g, ln_b):
            slen, bsz, _ = x.shape
            o = layer_norm(x, ln_g, ln_b)
            qkv = jnp.einsum('sbd,ed->sbe', o, slow_W)
            qkv = qkv.reshape(slen, bsz, H, 5 * DH + 2)
            q, k, v, rk, rv, beta, rbeta = jnp.split(qkv, [DH, 2 * DH, 3 * DH, 4 * DH, 5 * DH, 5 * DH + 1], axis=-1)
            beta = jax.nn.sigmoid(beta)
            rbeta = jax.nn.sigmoid(rbeta)
            q = sum_norm(elu_p1(q))
            k = sum_norm(elu_p1(k))
            rk = jax.nn.softmax(rk, axis=-1)

            def ff_step(W, inp):
                qt, kt, vt, bt = inp
                v_old = jnp.einsum('bhij,bhj->bhi', W, kt)
                W = W + (bt * (vt - v_old))[..., :, None] * kt[..., None, :]
                z = jnp.einsum('bhij,bhj->bhi', W, qt)
                return (W, z)
            W0 = jnp.zeros((bsz, H, DH, DH), x.dtype)
            _, z = jax.lax.scan(ff_step, W0, (q, k, v, beta))

            def rec_step(carry, inp):
                R, h = carry
                zt, kt, vt, bt = inp
                q_rec = jax.nn.softmax(h, axis=-1)
                v_old = jnp.einsum('bhij,bhj->bhi', R, kt)
                R = R + (bt * (vt - v_old))[..., :, None] * kt[..., None, :]
                h = zt + jnp.einsum('bhij,bhj->bhi', R, q_rec)
                return ((R, h), h)
            R0 = jnp.zeros((bsz, H, DH, DH), x.dtype)
            h0 = jnp.zeros((bsz, H, DH), x.dtype)
            _, hs = jax.lax.scan(rec_step, (R0, h0), (z, rk, rv, rbeta))
            out = hs.reshape(slen, bsz, H * DH)
            out = jnp.einsum('sbe,de->sbd', out, out_W)
            return x + out
        key = jax.random.key(seed)
        k1, k2, k3 = jax.random.split(key, 3)
        x = jax.random.normal(k1, (S, B, D), jnp.float32)
        slow_W = jax.random.normal(k2, (H * (5 * DH + 2), D), jnp.float32) * 0.02
        out_W = jax.random.normal(k3, (D, H * DH), jnp.float32) * 0.02
        ln_g = jnp.ones((D,), jnp.float32)
        ln_b = jnp.zeros((D,), jnp.float32)
        return {'x': x, 'slow_W': slow_W, 'out_W': out_W, 'ln_g': ln_g, 'ln_b': ln_b}
    _L0_attn_all = _L0_attn_setup()
    _L0_attn_in = {k: v for k, v in _L0_attn_all.items() if k in ('slow_W', 'out_W', 'ln_g', 'ln_b')}
    del _L0_attn_all

    def _L0_ffn_setup():
        import jax, jax.numpy as jnp
        import numpy as np
        B, S, D = (8, 1024, 64)
        H = 4 * D
        CAPACITY = 0.5
        key = jax.random.key(seed)
        ks = jax.random.split(key, 6)
        x = jax.random.normal(ks[0], (B, S, D), dtype=jnp.float32)
        attention_mask = jnp.zeros((B, 1, 1, S), dtype=jnp.float32)
        wr = jax.random.normal(ks[1], (D, 1), dtype=jnp.float32) * 0.02
        br = jnp.zeros((1,), dtype=jnp.float32)
        w1 = jax.random.normal(ks[2], (D, H), dtype=jnp.float32) * 0.02
        b1 = jnp.zeros((H,), dtype=jnp.float32)
        w2 = jax.random.normal(ks[3], (H, D), dtype=jnp.float32) * 0.02
        b2 = jnp.zeros((D,), dtype=jnp.float32)
        return {'x': x, 'attention_mask': attention_mask, 'wr': wr, 'br': br, 'w1': w1, 'b1': b1, 'w2': w2, 'b2': b2}
    _L0_ffn_all = _L0_ffn_setup()
    _L0_ffn_in = {k: v for k, v in _L0_ffn_all.items() if k in ('attention_mask', 'wr', 'br', 'w1', 'b1', 'w2', 'b2')}
    del _L0_ffn_all

    def _L1_attn_setup():
        import jax, jax.numpy as jnp
        import numpy as np
        DIM = 64
        WINDOW = 8
        SHIFT = 4
        HEADS = 8
        key = jax.random.key(seed)
        k_x, k_qw, k_qb, k_pw, k_pb, k_rb = jax.random.split(key, 6)
        B, T, D = (8, 2048, DIM)
        x = jax.random.normal(k_x, (B, T, D), dtype=jnp.float32)
        qkv_w = jax.random.normal(k_qw, (D, 3 * D), dtype=jnp.float32) * (1.0 / np.sqrt(D))
        qkv_b = jax.random.normal(k_qb, (3 * D,), dtype=jnp.float32) * 0.02
        proj_w = jax.random.normal(k_pw, (D, D), dtype=jnp.float32) * (1.0 / np.sqrt(D))
        proj_b = jax.random.normal(k_pb, (D,), dtype=jnp.float32) * 0.02
        rel_bias = jax.random.normal(k_rb, (2 * WINDOW - 1, HEADS), dtype=jnp.float32) * 0.02
        return {'x': x, 'qkv_w': qkv_w, 'qkv_b': qkv_b, 'proj_w': proj_w, 'proj_b': proj_b, 'rel_bias': rel_bias}
    _L1_attn_all = _L1_attn_setup()
    _L1_attn_in = {k: v for k, v in _L1_attn_all.items() if k in ('qkv_w', 'qkv_b', 'proj_w', 'proj_b', 'rel_bias')}
    del _L1_attn_all

    def _L1_ffn_setup():
        import jax, jax.numpy as jnp
        import numpy as np
        B, K, D = (128, 16, 64)
        E = 32
        H = int(D * 0.25)
        key = jax.random.key(seed)
        ks = jax.random.split(key, 7)
        d_rs = D ** (-0.5)
        h_rs = H ** (-0.5)
        x = jax.random.normal(ks[0], (B, K, D), dtype=jnp.float32)
        router_w = jax.random.uniform(ks[1], (E, D), jnp.float32, -d_rs, d_rs)
        router_b = jax.random.uniform(ks[2], (E,), jnp.float32, -d_rs, d_rs)
        W1 = jax.random.uniform(ks[3], (E, D, H), jnp.float32, -h_rs, h_rs)
        b1 = jax.random.uniform(ks[4], (E, H), jnp.float32, -h_rs, h_rs)
        W2 = jax.random.uniform(ks[5], (E, H, D), jnp.float32, -d_rs, d_rs)
        b2 = jax.random.uniform(ks[6], (E, D), jnp.float32, -d_rs, d_rs)
        return {'x': x, 'router_w': router_w, 'router_b': router_b, 'W1': W1, 'b1': b1, 'W2': W2, 'b2': b2}
    _L1_ffn_all = _L1_ffn_setup()
    _L1_ffn_in = {k: v for k, v in _L1_ffn_all.items() if k in ('router_w', 'router_b', 'W1', 'b1', 'W2', 'b2')}
    del _L1_ffn_all

    def _L2_attn_setup():
        import jax, jax.numpy as jnp
        import numpy as np
        D_ATT = 64
        D_GROUP = 32
        N_GROUP = D_ATT // D_GROUP
        key = jax.random.key(seed)
        ks = jax.random.split(key, 6)
        B, L = (4, 128)
        import math
        s = 1.0 / math.sqrt(D_ATT)
        return {'x': jax.random.normal(ks[0], (B, L, D_ATT), dtype=jnp.float32), 'Wq': jax.random.normal(ks[1], (D_ATT, D_ATT), dtype=jnp.float32) * s * 0.06, 'Wk': jax.random.normal(ks[2], (D_ATT, D_ATT), dtype=jnp.float32) * s * 0.06, 'Wv': jax.random.normal(ks[3], (D_ATT, D_ATT), dtype=jnp.float32) * s * 0.06, 'w_mlp': jax.random.normal(ks[4], (D_GROUP,), dtype=jnp.float32) * 0.1, 'b_mlp': jax.random.normal(ks[5], (1,), dtype=jnp.float32) * 0.1}
    _L2_attn_all = _L2_attn_setup()
    _L2_attn_in = {k: v for k, v in _L2_attn_all.items() if k in ('Wq', 'Wk', 'Wv', 'w_mlp', 'b_mlp')}
    del _L2_attn_all

    def _L2_ffn_setup():
        import jax, jax.numpy as jnp
        import numpy as np
        C = 64
        HID = 256
        E = 8
        TEMP = 1.0
        key = jax.random.key(seed)
        ks = jax.random.split(key, 7)
        x = jax.random.normal(ks[0], (8, 4096, C), dtype=jnp.float32)
        W1 = jax.random.normal(ks[1], (C, HID), dtype=jnp.float32) * 0.02
        b1 = jnp.zeros((HID,), dtype=jnp.float32)
        Wg = jax.random.normal(ks[2], (HID, E), dtype=jnp.float32) * 0.02
        bg = jnp.zeros((E,), dtype=jnp.float32)
        Wd = jax.random.normal(ks[3], (E, HID, C), dtype=jnp.float32) * 0.02
        bd = jnp.zeros((E, C), dtype=jnp.float32)
        return {'x': x, 'W1': W1, 'b1': b1, 'Wg': Wg, 'bg': bg, 'Wd': Wd, 'bd': bd}
    _L2_ffn_all = _L2_ffn_setup()
    _L2_ffn_in = {k: v for k, v in _L2_ffn_all.items() if k in ('W1', 'b1', 'Wg', 'bg', 'Wd', 'bd')}
    del _L2_ffn_all

    def _L3_attn_setup():
        import jax, jax.numpy as jnp
        import numpy as np
        D_MODEL = 64
        N_BRANCH = 4
        PH = 16
        KMAX = 15
        REL_HID = 64
        B, T = (2, 512)
        REL_IN = KMAX + 2
        SCALE_ACT = float(np.pi / np.sqrt(3.0))

        def _rope_tables(t_len, dim):
            inv = 1.0 / 10000.0 ** (np.arange(0, dim, 2, dtype=np.float32) / dim)
            f = np.outer(np.arange(t_len, dtype=np.float32), inv)
            return (jnp.asarray(np.cos(f)), jnp.asarray(np.sin(f)))

        def _rope(x, cos, sin):
            x1 = x[..., 0::2]
            x2 = x[..., 1::2]
            y1 = x1 * cos - x2 * sin
            y2 = x1 * sin + x2 * cos
            return jnp.stack((y1, y2), axis=-1).reshape(x.shape)

        def _l2n(v):
            n = jnp.linalg.norm(v, axis=-1, keepdims=True)
            return v / jnp.maximum(n, 1e-12)

        def _mlp(x, W1, b1, W2, b2):
            h = x @ W1 + b1
            h = h * jax.nn.sigmoid(SCALE_ACT * h)
            return h @ W2 + b2

        def _grid_sample_border(pal, g):
            D, H, W = pal.shape
            gx = jnp.clip((g[..., 0] + 1.0) * 0.5 * (W - 1), 0.0, W - 1.0)
            gy = jnp.clip((g[..., 1] + 1.0) * 0.5 * (H - 1), 0.0, H - 1.0)
            x0 = jnp.floor(gx)
            y0 = jnp.floor(gy)
            wx = gx - x0
            wy = gy - y0
            x0i = x0.astype(jnp.int32)
            y0i = y0.astype(jnp.int32)
            x1i = jnp.minimum(x0i + 1, W - 1)
            y1i = jnp.minimum(y0i + 1, H - 1)
            v00 = pal[:, y0i, x0i]
            v01 = pal[:, y0i, x1i]
            v10 = pal[:, y1i, x0i]
            v11 = pal[:, y1i, x1i]
            out = v00 * (1 - wx) * (1 - wy) + v01 * wx * (1 - wy) + v10 * (1 - wx) * wy + v11 * wx * wy
            return jnp.moveaxis(out, 0, -1)
        key = jax.random.key(seed)
        ks = jax.random.split(key, 12)
        D, BR, H = (D_MODEL, N_BRANCH, REL_HID)
        s = D ** (-0.5)
        return {'x': jax.random.normal(ks[0], (B, T, D), jnp.float32), 'Wi': jax.random.normal(ks[1], (D, BR * D), jnp.float32) * s, 'Wp': jax.random.normal(ks[2], (D, D), jnp.float32) * s, 'W1': jax.random.normal(ks[3], (REL_IN, H), jnp.float32) * REL_IN ** (-0.5), 'b1': jnp.zeros((H,), jnp.float32), 'W2': jax.random.normal(ks[4], (H, H), jnp.float32) * H ** (-0.5), 'b2': jnp.zeros((H,), jnp.float32), 'Wc': jax.random.normal(ks[5], (H, 2), jnp.float32) * H ** (-0.5), 'bc': jnp.zeros((2,), jnp.float32), 'Wm': jax.random.normal(ks[6], (H, 1), jnp.float32) * H ** (-0.5), 'bm': jnp.zeros((1,), jnp.float32), 'palette': jax.random.normal(ks[7], (D, PH, PH), jnp.float32) * s, 'Wo': jax.random.normal(ks[8], (BR, D, D), jnp.float32) * s}
    _L3_attn_all = _L3_attn_setup()
    _L3_attn_in = {k: v for k, v in _L3_attn_all.items() if k in ('Wi', 'Wp', 'W1', 'b1', 'W2', 'b2', 'Wc', 'bc', 'Wm', 'bm', 'palette', 'Wo')}
    del _L3_attn_all

    def _L3_ffn_setup():
        import jax, jax.numpy as jnp
        import numpy as np
        TOP_K = 2
        key = jax.random.key(seed)
        ks = jax.random.split(key, 4)
        B, L, D, H, E = (8, 1024, 64, 256, 8)
        s = 0.02
        return {'x': jax.random.normal(ks[0], (B, L, D), jnp.float32), 'Wg': jax.random.normal(ks[1], (D, E), jnp.float32) * s, 'bg': jnp.zeros((E,), jnp.float32), 'W1': jax.random.normal(ks[2], (E, D, H), jnp.float32) * s, 'b1': jnp.zeros((E, H), jnp.float32), 'W2': jax.random.normal(ks[3], (E, H, D), jnp.float32) * s, 'b2': jnp.zeros((E, D), jnp.float32)}
    _L3_ffn_all = _L3_ffn_setup()
    _L3_ffn_in = {k: v for k, v in _L3_ffn_all.items() if k in ('Wg', 'bg', 'W1', 'b1', 'W2', 'b2')}
    del _L3_ffn_all
    return {'x': x, 'L0_tok_W': _L0_tok_in['W'], 'L0_tok_b': _L0_tok_in['b'], 'L0_tok_gamma': _L0_tok_in['gamma'], 'L0_tok_beta': _L0_tok_in['beta'], 'L0_attn_slow_W': _L0_attn_in['slow_W'], 'L0_attn_out_W': _L0_attn_in['out_W'], 'L0_attn_ln_g': _L0_attn_in['ln_g'], 'L0_attn_ln_b': _L0_attn_in['ln_b'], 'L0_ffn_attention_mask': _L0_ffn_in['attention_mask'], 'L0_ffn_wr': _L0_ffn_in['wr'], 'L0_ffn_br': _L0_ffn_in['br'], 'L0_ffn_w1': _L0_ffn_in['w1'], 'L0_ffn_b1': _L0_ffn_in['b1'], 'L0_ffn_w2': _L0_ffn_in['w2'], 'L0_ffn_b2': _L0_ffn_in['b2'], 'L1_attn_qkv_w': _L1_attn_in['qkv_w'], 'L1_attn_qkv_b': _L1_attn_in['qkv_b'], 'L1_attn_proj_w': _L1_attn_in['proj_w'], 'L1_attn_proj_b': _L1_attn_in['proj_b'], 'L1_attn_rel_bias': _L1_attn_in['rel_bias'], 'L1_ffn_router_w': _L1_ffn_in['router_w'], 'L1_ffn_router_b': _L1_ffn_in['router_b'], 'L1_ffn_W1': _L1_ffn_in['W1'], 'L1_ffn_b1': _L1_ffn_in['b1'], 'L1_ffn_W2': _L1_ffn_in['W2'], 'L1_ffn_b2': _L1_ffn_in['b2'], 'L2_attn_Wq': _L2_attn_in['Wq'], 'L2_attn_Wk': _L2_attn_in['Wk'], 'L2_attn_Wv': _L2_attn_in['Wv'], 'L2_attn_w_mlp': _L2_attn_in['w_mlp'], 'L2_attn_b_mlp': _L2_attn_in['b_mlp'], 'L2_ffn_W1': _L2_ffn_in['W1'], 'L2_ffn_b1': _L2_ffn_in['b1'], 'L2_ffn_Wg': _L2_ffn_in['Wg'], 'L2_ffn_bg': _L2_ffn_in['bg'], 'L2_ffn_Wd': _L2_ffn_in['Wd'], 'L2_ffn_bd': _L2_ffn_in['bd'], 'L3_attn_Wi': _L3_attn_in['Wi'], 'L3_attn_Wp': _L3_attn_in['Wp'], 'L3_attn_W1': _L3_attn_in['W1'], 'L3_attn_b1': _L3_attn_in['b1'], 'L3_attn_W2': _L3_attn_in['W2'], 'L3_attn_b2': _L3_attn_in['b2'], 'L3_attn_Wc': _L3_attn_in['Wc'], 'L3_attn_bc': _L3_attn_in['bc'], 'L3_attn_Wm': _L3_attn_in['Wm'], 'L3_attn_bm': _L3_attn_in['bm'], 'L3_attn_palette': _L3_attn_in['palette'], 'L3_attn_Wo': _L3_attn_in['Wo'], 'L3_ffn_Wg': _L3_ffn_in['Wg'], 'L3_ffn_bg': _L3_ffn_in['bg'], 'L3_ffn_W1': _L3_ffn_in['W1'], 'L3_ffn_b1': _L3_ffn_in['b1'], 'L3_ffn_W2': _L3_ffn_in['W2'], 'L3_ffn_b2': _L3_ffn_in['b2']}

def reference(x, L0_tok_W, L0_tok_b, L0_tok_gamma, L0_tok_beta, L0_attn_slow_W, L0_attn_out_W, L0_attn_ln_g, L0_attn_ln_b, L0_ffn_attention_mask, L0_ffn_wr, L0_ffn_br, L0_ffn_w1, L0_ffn_b1, L0_ffn_w2, L0_ffn_b2, L1_attn_qkv_w, L1_attn_qkv_b, L1_attn_proj_w, L1_attn_proj_b, L1_attn_rel_bias, L1_ffn_router_w, L1_ffn_router_b, L1_ffn_W1, L1_ffn_b1, L1_ffn_W2, L1_ffn_b2, L2_attn_Wq, L2_attn_Wk, L2_attn_Wv, L2_attn_w_mlp, L2_attn_b_mlp, L2_ffn_W1, L2_ffn_b1, L2_ffn_Wg, L2_ffn_bg, L2_ffn_Wd, L2_ffn_bd, L3_attn_Wi, L3_attn_Wp, L3_attn_W1, L3_attn_b1, L3_attn_W2, L3_attn_b2, L3_attn_Wc, L3_attn_bc, L3_attn_Wm, L3_attn_bm, L3_attn_palette, L3_attn_Wo, L3_ffn_Wg, L3_ffn_bg, L3_ffn_W1, L3_ffn_b1, L3_ffn_W2, L3_ffn_b2):
    import jax
    import jax.numpy as jnp

    def _L0_tok_ref(x, W, b, gamma, beta):
        import jax, jax.numpy as jnp
        import numpy as np
        PATCH = 16
        STRIDE = 8
        EPS = 1e-05
        B, S, F = x.shape
        starts = jnp.arange(0, S - PATCH + 1, STRIDE)
        idx = starts[:, None] + jnp.arange(PATCH)[None, :]
        patches = x[:, idx, :].reshape(B, idx.shape[0], PATCH * F)
        y = jnp.einsum('bpi,di->bpd', patches, W) + b
        mu = jnp.mean(y, axis=-1, keepdims=True)
        var = jnp.mean(jnp.square(y - mu), axis=-1, keepdims=True)
        return (y - mu) * jax.lax.rsqrt(var + EPS) * gamma + beta

    def _L0_attn_ref(x, slow_W, out_W, ln_g, ln_b):
        import jax, jax.numpy as jnp
        import numpy as np
        S, B, D, H, DH = (128, 32, 64, 8, 32)
        LN_EPS = 1e-05

        def elu_p1(x):
            return jax.nn.elu(x) + 1.0

        def sum_norm(x):
            return x / jnp.sum(x, axis=-1, keepdims=True)

        def layer_norm(x, g, b):
            mu = jnp.mean(x, axis=-1, keepdims=True)
            var = jnp.mean(jnp.square(x - mu), axis=-1, keepdims=True)
            return (x - mu) * jax.lax.rsqrt(var + LN_EPS) * g + b

        def _fast_rnn_forward(x, slow_W, out_W, ln_g, ln_b):
            slen, bsz, _ = x.shape
            o = layer_norm(x, ln_g, ln_b)
            qkv = jnp.einsum('sbd,ed->sbe', o, slow_W)
            qkv = qkv.reshape(slen, bsz, H, 5 * DH + 2)
            q, k, v, rk, rv, beta, rbeta = jnp.split(qkv, [DH, 2 * DH, 3 * DH, 4 * DH, 5 * DH, 5 * DH + 1], axis=-1)
            beta = jax.nn.sigmoid(beta)
            rbeta = jax.nn.sigmoid(rbeta)
            q = sum_norm(elu_p1(q))
            k = sum_norm(elu_p1(k))
            rk = jax.nn.softmax(rk, axis=-1)

            def ff_step(W, inp):
                qt, kt, vt, bt = inp
                v_old = jnp.einsum('bhij,bhj->bhi', W, kt)
                W = W + (bt * (vt - v_old))[..., :, None] * kt[..., None, :]
                z = jnp.einsum('bhij,bhj->bhi', W, qt)
                return (W, z)
            W0 = jnp.zeros((bsz, H, DH, DH), x.dtype)
            _, z = jax.lax.scan(ff_step, W0, (q, k, v, beta))

            def rec_step(carry, inp):
                R, h = carry
                zt, kt, vt, bt = inp
                q_rec = jax.nn.softmax(h, axis=-1)
                v_old = jnp.einsum('bhij,bhj->bhi', R, kt)
                R = R + (bt * (vt - v_old))[..., :, None] * kt[..., None, :]
                h = zt + jnp.einsum('bhij,bhj->bhi', R, q_rec)
                return ((R, h), h)
            R0 = jnp.zeros((bsz, H, DH, DH), x.dtype)
            h0 = jnp.zeros((bsz, H, DH), x.dtype)
            _, hs = jax.lax.scan(rec_step, (R0, h0), (z, rk, rv, rbeta))
            out = hs.reshape(slen, bsz, H * DH)
            out = jnp.einsum('sbe,de->sbd', out, out_W)
            return x + out
        return _fast_rnn_forward(x, slow_W, out_W, ln_g, ln_b)

    def _L0_ffn_ref(x, attention_mask, wr, br, w1, b1, w2, b2):
        import jax, jax.numpy as jnp
        import numpy as np
        B, S, D = (8, 1024, 64)
        H = 4 * D
        CAPACITY = 0.5
        b, s, d = x.shape
        weights = (jnp.einsum('bsd,do->bso', x, wr) + br)[..., 0]
        k = max(1, int(CAPACITY * s))
        kk = k - 1 if k > 1 else 1
        _, idx = jax.lax.top_k(weights, k)
        sel_idx = idx[:, :kk]
        sel = jnp.take_along_axis(x, sel_idx[:, :, None], axis=1)
        h = jax.nn.gelu(jnp.einsum('bkd,dh->bkh', sel, w1) + b1)
        y = jnp.einsum('bkh,hd->bkd', h, w2) + b2
        w_sel = jnp.take_along_axis(weights, sel_idx, axis=1)
        y = y * w_sel[..., None]
        batch_idx = jnp.arange(b)[:, None]
        processed = jnp.zeros_like(x).at[batch_idx, sel_idx].set(y)
        return processed + x

    def _L1_attn_ref(x, qkv_w, qkv_b, proj_w, proj_b, rel_bias):
        import jax, jax.numpy as jnp
        import numpy as np
        DIM = 64
        WINDOW = 8
        SHIFT = 4
        HEADS = 8
        B, T, D = x.shape
        ws, shift, heads = (WINDOW, SHIFT, HEADS)
        hd = D // heads
        pad_len = (ws - T % ws) % ws
        if pad_len:
            x = jnp.pad(x, ((0, 0), (0, pad_len), (0, 0)))
        T_pad = T + pad_len
        if shift > 0:
            x = jnp.roll(x, -shift, axis=1)
        n_win = T_pad // ws
        win = x.reshape(B * n_win, ws, D)
        qkv = win @ qkv_w + qkv_b
        qkv = qkv.reshape(B * n_win, ws, 3, heads, hd)
        qkv = jnp.transpose(qkv, (2, 0, 3, 1, 4))
        q, k, v = (qkv[0], qkv[1], qkv[2])
        scale = hd ** (-0.5)
        scores = jnp.einsum('whqd,whkd->whqk', q, k) * scale
        coords = jnp.arange(ws)
        rel = coords[None, :] - coords[:, None] + (ws - 1)
        bias = rel_bias[rel]
        scores = scores + jnp.transpose(bias, (2, 0, 1))[None]
        probs = jax.nn.softmax(scores, axis=-1)
        attn = jnp.einsum('whqk,whkd->whqd', probs, v)
        attn = jnp.transpose(attn, (0, 2, 1, 3)).reshape(B * n_win, ws, D)
        out = attn @ proj_w + proj_b
        out = out.reshape(B, T_pad, D)
        if shift > 0:
            out = jnp.roll(out, shift, axis=1)
        return out[:, :T, :]

    def _L1_ffn_ref(x, router_w, router_b, W1, b1, W2, b2):
        import jax, jax.numpy as jnp
        import numpy as np
        B, K, D = (128, 16, 64)
        E = 32
        H = int(D * 0.25)
        xf = x.reshape(-1, D)
        logits = xf @ router_w.T + router_b
        idx = jnp.argmax(logits, axis=-1)
        w1t = jnp.take(W1, idx, axis=0)
        h = jnp.einsum('nd,ndh->nh', xf, w1t) + jnp.take(b1, idx, axis=0)
        h = jax.nn.relu(h)
        w2t = jnp.take(W2, idx, axis=0)
        out = jnp.einsum('nh,nhd->nd', h, w2t) + jnp.take(b2, idx, axis=0)
        out = jax.nn.relu(out)
        return out.reshape(x.shape)

    def _L2_attn_ref(x, Wq, Wk, Wv, w_mlp, b_mlp):
        import jax, jax.numpy as jnp
        import numpy as np
        D_ATT = 64
        D_GROUP = 32
        N_GROUP = D_ATT // D_GROUP
        B, L, d_att = x.shape
        G, Dg = (N_GROUP, D_GROUP)
        Q = x @ Wq.T
        K = x @ Wk.T
        V = x @ Wv.T
        Qg = Q.reshape(B, L, 1, G, Dg)
        Kg = K.reshape(B, 1, L, G, Dg)
        diff = Qg - Kg
        attn = jnp.einsum('bqkgd,d->bqkg', jax.nn.relu(diff), w_mlp) + b_mlp[0]
        attn = jax.nn.relu(attn)
        attn = jax.nn.softmax(attn, axis=2)
        Vg = V.reshape(B, L, Dg, G)
        out = jnp.einsum('bqkg,bkdg->bqdg', attn, Vg)
        return out.reshape(B, L, d_att)

    def _L2_ffn_ref(x, W1, b1, Wg, bg, Wd, bd):
        import jax, jax.numpy as jnp
        import numpy as np
        C = 64
        HID = 256
        E = 8
        TEMP = 1.0
        orig_shape = x.shape
        xf = x.reshape(-1, orig_shape[-1])
        H = jax.nn.gelu(xf @ W1 + b1, approximate=False)
        probs = jax.nn.softmax((H @ Wg + bg) / TEMP, axis=-1)
        assign = jnp.argmax(probs, axis=-1)
        out = jnp.zeros_like(xf)
        for e in range(Wd.shape[0]):
            y = H @ Wd[e] + bd[e]
            sel = (assign == e)[:, None]
            out = out + jnp.where(sel, probs[:, e:e + 1] * y, 0.0)
        return out.reshape(orig_shape)

    def _L3_attn_ref(x, Wi, Wp, W1, b1, W2, b2, Wc, bc, Wm, bm, palette, Wo):
        import jax, jax.numpy as jnp
        import numpy as np
        D_MODEL = 64
        N_BRANCH = 4
        PH = 16
        KMAX = 15
        REL_HID = 64
        B, T = (2, 512)
        REL_IN = KMAX + 2
        SCALE_ACT = float(np.pi / np.sqrt(3.0))

        def _rope_tables(t_len, dim):
            inv = 1.0 / 10000.0 ** (np.arange(0, dim, 2, dtype=np.float32) / dim)
            f = np.outer(np.arange(t_len, dtype=np.float32), inv)
            return (jnp.asarray(np.cos(f)), jnp.asarray(np.sin(f)))

        def _rope(x, cos, sin):
            x1 = x[..., 0::2]
            x2 = x[..., 1::2]
            y1 = x1 * cos - x2 * sin
            y2 = x1 * sin + x2 * cos
            return jnp.stack((y1, y2), axis=-1).reshape(x.shape)

        def _l2n(v):
            n = jnp.linalg.norm(v, axis=-1, keepdims=True)
            return v / jnp.maximum(n, 1e-12)

        def _mlp(x, W1, b1, W2, b2):
            h = x @ W1 + b1
            h = h * jax.nn.sigmoid(SCALE_ACT * h)
            return h @ W2 + b2

        def _grid_sample_border(pal, g):
            D, H, W = pal.shape
            gx = jnp.clip((g[..., 0] + 1.0) * 0.5 * (W - 1), 0.0, W - 1.0)
            gy = jnp.clip((g[..., 1] + 1.0) * 0.5 * (H - 1), 0.0, H - 1.0)
            x0 = jnp.floor(gx)
            y0 = jnp.floor(gy)
            wx = gx - x0
            wy = gy - y0
            x0i = x0.astype(jnp.int32)
            y0i = y0.astype(jnp.int32)
            x1i = jnp.minimum(x0i + 1, W - 1)
            y1i = jnp.minimum(y0i + 1, H - 1)
            v00 = pal[:, y0i, x0i]
            v01 = pal[:, y0i, x1i]
            v10 = pal[:, y1i, x0i]
            v11 = pal[:, y1i, x1i]
            out = v00 * (1 - wx) * (1 - wy) + v01 * wx * (1 - wy) + v10 * (1 - wx) * wy + v11 * wx * wy
            return jnp.moveaxis(out, 0, -1)
        Bn, Tn, D = x.shape
        BR = Wo.shape[0]
        K = KMAX
        scale = D ** (-0.5)
        cos, sin = _rope_tables(Tn, D)
        I = (x @ Wi).reshape(Bn, Tn, BR, D).transpose(0, 2, 1, 3)
        P = x @ Wp
        I = _rope(I, cos, sin)
        P = _rope(P, cos, sin)
        logits = jnp.einsum('brtd,bsd->brts', I, P) * scale
        causal = jnp.tril(jnp.ones((Tn, Tn), bool))
        logits = jnp.where(causal, logits, -jnp.inf)
        topk_val, topk_idx = jax.lax.top_k(logits, K)
        keep = jnp.isfinite(topk_val)
        keep_f = keep.astype(x.dtype)
        P_sel = jax.vmap(lambda p, i: p[i])(P, topk_idx)
        P_sel_n = _l2n(P_sel) * keep_f[..., None]
        I_n = _l2n(I)[:, :, :, None, :]
        feat_a = jnp.clip(jnp.sum(I_n * P_sel_n, -1), -1.0, 1.0) * keep_f
        G = jnp.clip(jnp.einsum('brtkd,brtjd->brtkj', P_sel_n, P_sel_n), -1.0, 1.0)
        G = G * keep_f[..., :, None] * keep_f[..., None, :]
        t_rng = jnp.arange(Tn)[None, None, :, None]
        delta = jnp.maximum((t_rng - topk_idx).astype(x.dtype), 0.0) / max(1.0, float(Tn))
        delta = delta * keep_f
        rel = jnp.concatenate([G, feat_a[..., None], delta[..., None]], -1)
        h = _mlp(rel, W1, b1, W2, b2)
        z = jnp.tanh(h @ Wc + bc)
        mix = jnp.where(keep, (h @ Wm + bm)[..., 0], -jnp.inf)
        w = jnp.nan_to_num(jax.nn.softmax(mix, axis=-1), nan=0.0)
        samples = _grid_sample_border(palette, z)
        V = jnp.sum(samples * w[..., None], axis=3)
        y = jnp.einsum('brtd,rdm->brtm', V, Wo).mean(axis=1)
        return y

    def _L3_ffn_ref(x, Wg, bg, W1, b1, W2, b2):
        import jax, jax.numpy as jnp
        import numpy as np
        TOP_K = 2
        B, L, D = x.shape
        E = W1.shape[0]
        xf = x.reshape(-1, D)
        gate_logits = xf @ Wg + bg
        top_w, top_i = jax.lax.top_k(gate_logits, TOP_K)
        top_w = jax.nn.softmax(top_w, axis=-1)
        w_dense = jnp.sum(jax.nn.one_hot(top_i, E, dtype=xf.dtype) * top_w[..., None], axis=1)
        out = jnp.zeros_like(xf)
        for e in range(E):
            h = jax.nn.gelu(xf @ W1[e] + b1[e], approximate=False)
            out = out + w_dense[:, e:e + 1] * (h @ W2[e] + b2[e])
        return out.reshape(B, L, D)
    h = _L0_tok_ref(x, L0_tok_W, L0_tok_b, L0_tok_gamma, L0_tok_beta)
    h = h + _L0_attn_ref(_layernorm(h, axis=-1), L0_attn_slow_W, L0_attn_out_W, L0_attn_ln_g, L0_attn_ln_b)
    h = h + _L0_ffn_ref(_layernorm(h, axis=-1), L0_ffn_attention_mask, L0_ffn_wr, L0_ffn_br, L0_ffn_w1, L0_ffn_b1, L0_ffn_w2, L0_ffn_b2)
    h = h + _L1_attn_ref(_layernorm(h, axis=-1), L1_attn_qkv_w, L1_attn_qkv_b, L1_attn_proj_w, L1_attn_proj_b, L1_attn_rel_bias)
    h = h + _L1_ffn_ref(_layernorm(h, axis=-1), L1_ffn_router_w, L1_ffn_router_b, L1_ffn_W1, L1_ffn_b1, L1_ffn_W2, L1_ffn_b2)
    h = h + _L2_attn_ref(_layernorm(h, axis=-1), L2_attn_Wq, L2_attn_Wk, L2_attn_Wv, L2_attn_w_mlp, L2_attn_b_mlp)
    h = h + _L2_ffn_ref(_layernorm(h, axis=-1), L2_ffn_W1, L2_ffn_b1, L2_ffn_Wg, L2_ffn_bg, L2_ffn_Wd, L2_ffn_bd)
    h = h + _L3_attn_ref(_layernorm(h, axis=-1), L3_attn_Wi, L3_attn_Wp, L3_attn_W1, L3_attn_b1, L3_attn_W2, L3_attn_b2, L3_attn_Wc, L3_attn_bc, L3_attn_Wm, L3_attn_bm, L3_attn_palette, L3_attn_Wo)
    h = h + _L3_ffn_ref(_layernorm(h, axis=-1), L3_ffn_Wg, L3_ffn_bg, L3_ffn_W1, L3_ffn_b1, L3_ffn_W2, L3_ffn_b2)
    return h

_drawn_inputs = setup_inputs


def setup_inputs(seed=0):
    import zlib

    import numpy as np

    out = dict(_drawn_inputs(seed))
    spreads = {'L0_tok_gamma': (1.0, 0.2),
     'L0_tok_beta': (0.0, 0.1),
     'L0_attn_ln_g': (1.0, 0.6),
     'L0_attn_ln_b': (0.0, 0.8),
     'L0_ffn_b1': (0.0, 0.8),
     'L0_ffn_b2': (0.0, 0.8),
     'L2_ffn_b1': (0.0, 0.8),
     'L2_ffn_bg': (0.0, 0.8),
     'L2_ffn_bd': (0.0, 0.8),
     'L3_attn_b1': (0.0, 0.8),
     'L3_attn_b2': (0.0, 0.8),
     'L3_attn_bc': (0.0, 0.8),
     'L3_ffn_bg': (0.0, 0.406),
     'L3_ffn_b1': (0.0, 0.8),
     'L3_ffn_b2': (0.0, 0.342)}
    factors = {'L0_attn_slow_W': 8.0,
     'L0_attn_out_W': 8.0,
     'L0_ffn_wr': 8.0,
     'L0_ffn_w1': 8.0,
     'L0_ffn_w2': 8.0,
     'L1_attn_qkv_b': 6.084,
     'L1_attn_proj_b': 6.867,
     'L1_attn_rel_bias': 8.0,
     'L1_ffn_b1': 8.0,
     'L1_ffn_b2': 3.543,
     'L2_attn_Wq': 8.0,
     'L2_attn_Wk': 8.0,
     'L2_attn_Wv': 8.0,
     'L2_attn_w_mlp': 8.0,
     'L2_ffn_W1': 8.0,
     'L2_ffn_Wg': 8.0,
     'L2_ffn_Wd': 8.0,
     'L3_attn_Wi': 8.0,
     'L3_attn_Wp': 8.0,
     'L3_attn_W1': 8.0,
     'L3_attn_W2': 8.0,
     'L3_attn_Wc': 8.0,
     'L3_attn_Wm': 8.0,
     'L3_attn_palette': 7.912,
     'L3_attn_Wo': 8.0,
     'L3_ffn_Wg': 2.938,
     'L3_ffn_W1': 8.0,
     'L3_ffn_W2': 8.0}
    for name, (base, spread) in spreads.items():
        noise = np.random.default_rng([zlib.crc32(name.encode()), seed]).standard_normal(out[name].shape)
        drawn = base * np.exp(spread * noise) if base else spread * noise
        out[name] = jnp.asarray(drawn.astype(out[name].dtype))
    for name, factor in factors.items():
        out[name] = (out[name] * factor).astype(out[name].dtype)
    return out
```

```python
from contextlib import ExitStack

import numpy as np
import concourse.bass as bass
from concourse import mybir
from concourse.alu_op_type import AluOpType as ALU

F32 = mybir.dt.float32
BF16 = mybir.dt.bfloat16
U32 = mybir.dt.uint32
ACT = mybir.ActivationFunctionType
X = mybir.AxisListType.X

B = 64
T = 92
D = 64
F = B * D
PATCH_COLS = 128
ROWS = T + 1
G = 4
NG = B // G
GT = G * T
EPS = 1e-5


class Layer(ExitStack):

    def __init__(self, nc):
        super().__init__()
        self.nc, self.semaphores = nc, []

    def enter_context(self, cm):
        got = super().enter_context(cm)
        if isinstance(got, bass.SemaphoreHandle):
            self.semaphores.append(got)
        return got

    def block(self):
        self.callback(self.clear)
        return super().enter_context(self.nc.Block())

    def clear(self):
        numbers = sorted(s.num for s in self.semaphores)
        while numbers:
            n = 1
            while n < len(numbers) and numbers[n] == numbers[0] + n:
                n += 1
            self.nc.gpsimd.sem_clear(range(numbers[0], numbers[0] + n))
            numbers = numbers[n:]


class Chain:

    def __init__(self, eng, sem, gap=None):
        self.eng, self.sem, self.gap = eng, sem, gap
        self.before, self.n, self.i, self.per = 0, 0, 0, 0

    def begin(self, i, per, first=0):
        self.before += self.n
        self.i, self.per, self.n, self.first = i, per, 0, first

    def end(self, times):
        assert self.n == self.per, f"{self.sem.name}: {self.n} steps in a body, {self.per} said"
        self.before += self.per * times
        self.i, self.per, self.n = 0, 0, 0

    def __call__(self, ins, gap=False):
        ins.then_inc(self.sem, 1)
        self.n += 1
        at = self.before + self.n
        if self.per:
            at = (self.i - self.first) * self.per + at if self.first else self.i * self.per + at
        self.eng.wait_ge(self.sem, at)
        if gap:
            self.eng.sem_inc(self.gap, 1)


def inner(ap, n):
    return ap.unsqueeze(len(ap.shape)).broadcast_to(list(ap.shape) + [n])


def outer(ap, n, axis=1):
    shape = list(ap.shape)
    shape.insert(axis, n)
    return ap.unsqueeze(axis).broadcast_to(shape)


def tokens(nc, m, c):
    with Layer(nc) as ctx:
        rows = ctx.enter_context(nc.sbuf_tensor("tok_rows", [128, 2, G * ROWS], F32))
        w = ctx.enter_context(nc.sbuf_tensor("tok_w_sb", [128, 2 * D], F32))
        b = ctx.enter_context(nc.sbuf_tensor("tok_b_sb", [1, D], F32))
        weights = ctx.enter_context(nc.semaphore("tok_weights"))
        rows0 = ctx.enter_context(nc.semaphore("tok_rows0"))
        rows1 = ctx.enter_context(nc.semaphore("tok_rows1"))
        rows_free = ctx.enter_context(nc.semaphore("tok_rows_free"))
        done = ctx.enter_context(nc.semaphore("tok_done"))
        psum_free = ctx.enter_context(nc.semaphore("tok_psum_free"))
        block = ctx.block()
        rows_loaded = [rows0, rows1]

        @block.sync
        def _(sp):
            sp.dma_start(w[:, :], c["tok_w"]).then_inc(weights, 16)
            sp.dma_start(b[:, :], c["tok_b"]).then_inc(weights, 16)
            sp.dma_start(m.ident[:, :], c["ident"]).then_inc(weights, 16)
            sp.dma_start(m.ones[:, :], c["ones"]).then_inc(weights, 16)
            with sp.Fori(0, NG // 2) as i:
                for u in range(2):
                    sp.wait_ge(rows_free, i * 2 + u + 1)
                    sp.dma_start(rows[:, u, :], c["tok_rows"][:, bass.ds((i * 2 + u) * (G * ROWS), G * ROWS)]).then_inc(rows_loaded[u], 16)

        @block.tensor
        def _(pe):
            pe.sem_inc(rows_free, 2)
            pe.wait_ge(weights, 64)
            with pe.Fori(0, NG // 2) as i:
                for u in range(2):
                    pe.wait_ge(rows_loaded[u], i * 16 + 16)
                    pe.wait_ge(psum_free, i * 2 + u + 1)
                    for q in range(G):
                        out = m.ps[0:T, u * 512 + q * D:u * 512 + (q + 1) * D]
                        at = q * ROWS
                        nc.tensor.matmul(out, rows[:, u, at:at + T], w[:, 0:D], start=True, stop=False)
                        nc.tensor.matmul(out, rows[:, u, at + 1:at + 1 + T], w[:, D:2 * D], start=False, stop=False)
                        last = nc.tensor.matmul(out, m.ones[0:1, 0:T], b[0:1, :], start=False, stop=True)
                    last.then_inc(done, 1)
                    pe.wait_ge(done, i * 2 + u + 1)
                    pe.sem_inc(rows_free, 1)

        @block.scalar
        def _(act):
            act.sem_inc(psum_free, 2)
            with act.Fori(0, NG // 2) as i:
                for u in range(2):
                    act.wait_ge(done, i * 2 + u + 1)
                    nc.scalar.activation(m.h[:, bass.ds((i * 2 + u) * (G * D), G * D)], m.ps[0:T, u * 512:u * 512 + G * D], ACT.Copy).then_inc(psum_free, 1)


def layer_norm(nc, m, src, dst, tag, gain=None, shift=None):
    with Layer(nc) as ctx:
        sq = ctx.enter_context(nc.sbuf_tensor(f"{tag}_sq", [T, F], F32))
        total = ctx.enter_context(nc.sbuf_tensor(f"{tag}_sum", [T, B], F32))
        mean = ctx.enter_context(nc.sbuf_tensor(f"{tag}_mean", [T, B], F32))
        var = ctx.enter_context(nc.sbuf_tensor(f"{tag}_var", [T, B], F32))
        std = ctx.enter_context(nc.sbuf_tensor(f"{tag}_std", [T, B], F32))
        rstd = ctx.enter_context(nc.sbuf_tensor(f"{tag}_rstd", [T, B], F32))
        affine = ctx.enter_context(nc.sbuf_tensor(f"{tag}_gain", [T, 2, D], F32))
        affine_loaded = ctx.enter_context(nc.semaphore(f"{tag}_affine_loaded"))
        centred = ctx.enter_context(nc.semaphore(f"{tag}_centred"))
        squared = ctx.enter_context(nc.semaphore(f"{tag}_squared"))
        var_ready = ctx.enter_context(nc.semaphore(f"{tag}_var_ready"))
        std_ready = ctx.enter_context(nc.semaphore(f"{tag}_std_ready"))
        steps = ctx.enter_context(nc.semaphore(f"{tag}_steps"))
        block = ctx.block()
        v3 = lambda ap: ap.rearrange("p (b d) -> p b d", d=D)

        @block.sync
        def _(sp):
            if gain is not None:
                sp.dma_start(affine[:, 0, :], gain.broadcast_to([T, D])).then_inc(affine_loaded, 16)
                sp.dma_start(affine[:, 1, :], shift.broadcast_to([T, D])).then_inc(affine_loaded, 16)

        @block.vector
        def _(dve):
            step = Chain(dve, steps)
            step(nc.vector.tensor_reduce(total[:, :], v3(src), X, ALU.add))
            step(nc.vector.tensor_scalar(mean[:, :], total[:, :], 1.0 / D, None, ALU.mult))
            nc.vector.tensor_tensor(v3(dst), v3(src), inner(mean[:, :], D), ALU.subtract).then_inc(centred, 1)
            dve.wait_ge(squared, 1)
            step(nc.vector.tensor_reduce(total[:, :], v3(sq[:, :]), X, ALU.add))
            nc.vector.tensor_scalar(var[:, :], total[:, :], 1.0 / D, EPS, ALU.mult, ALU.add).then_inc(var_ready, 1)
            dve.wait_ge(std_ready, 1)
            step(nc.vector.reciprocal(rstd[:, :], std[:, :]))
            step(nc.vector.tensor_tensor(v3(dst), v3(dst), inner(rstd[:, :], D), ALU.mult))
            if gain is not None:
                dve.wait_ge(affine_loaded, 32)
                step(nc.vector.tensor_tensor(v3(dst), v3(dst), outer(affine[:, 0, :], B), ALU.mult))
                step(nc.vector.tensor_tensor(v3(dst), v3(dst), outer(affine[:, 1, :], B), ALU.add))

        @block.scalar
        def _(act):
            act.wait_ge(centred, 1)
            nc.scalar.activation(sq[:, :], dst, ACT.Square).then_inc(squared, 1)
            act.wait_ge(var_ready, 1)
            nc.scalar.activation(std[:, :], var[:, :], ACT.Sqrt).then_inc(std_ready, 1)


HEADS = 8
DH = 32
UNIT = 2 * DH * DH
DVE_GROUPS = [(0, 2), (2, 2), (4, 1)]
POOL_GROUPS = [(5, 1), (6, 2)]


def fast_weights(nc, m, c):
    CUTS = [(0, 512), (512, 1024), (1024, 1296)]
    QK, RK, VV, RV, BB = 0, 512, 768, 1024, 1280
    IN_BANK, H_BANK, QOUT = 0, 512, 1024
    KOUT = {first: 512 * (3 + k) for k, (first, _) in enumerate(DVE_GROUPS + POOL_GROUPS)}
    with Layer(nc) as ctx:
        state = ctx.enter_context(nc.sbuf_tensor("fw_state", [T, HEADS * UNIT], F32))
        growth = ctx.enter_context(nc.sbuf_tensor("fw_growth", [T, UNIT], F32))
        prod_q = ctx.enter_context(nc.sbuf_tensor("fw_prod_q", [T, 2 * UNIT], F32))
        prod_k = ctx.enter_context(nc.sbuf_tensor("fw_prod_k", [T, 2 * UNIT], F32))
        pool_q = ctx.enter_context(nc.sbuf_tensor("fw_pool_q", [T, 2 * UNIT], F32))
        pool_k = ctx.enter_context(nc.sbuf_tensor("fw_pool_k", [T, 2 * UNIT], F32))
        w = ctx.enter_context(nc.sbuf_tensor("fw_w", [D, 1296], F32))
        w_out = ctx.enter_context(nc.sbuf_tensor("fw_w_out", [128, 2 * D], F32))
        raw = ctx.enter_context(nc.sbuf_tensor("fw_raw", [T, 1296], F32))
        o = ctx.enter_context(nc.sbuf_tensor("fw_o", [T, 2, D], F32))
        oT = ctx.enter_context(nc.sbuf_tensor("fw_oT", [D, T], F32))
        neg = ctx.enter_context(nc.sbuf_tensor("fw_neg", [T, 512], F32))
        small = ctx.enter_context(nc.sbuf_tensor("fw_small", [T, 8, 16], F32))
        be = ctx.enter_context(nc.sbuf_tensor("fw_be", [T, 2, 16], F32))
        K = ctx.enter_context(nc.sbuf_tensor("fw_K", [T, 2, 512], F32))
        V = ctx.enter_context(nc.sbuf_tensor("fw_V", [T, 2, 512], F32))
        Q = ctx.enter_context(nc.sbuf_tensor("fw_Q", [T, 2, 512], F32))
        beta = ctx.enter_context(nc.sbuf_tensor("fw_beta", [T, 2, 16], F32))
        dv = ctx.enter_context(nc.sbuf_tensor("fw_dv", [T, 512], F32))
        hs = ctx.enter_context(nc.sbuf_tensor("fw_h", [T, 256], F32))
        hx = ctx.enter_context(nc.sbuf_tensor("fw_hx", [T, 256], F32))
        he = ctx.enter_context(nc.sbuf_tensor("fw_he", [T, 256], F32))
        hT = ctx.enter_context(nc.sbuf_tensor("fw_hT", [128, 2 * T], F32))
        weights = ctx.enter_context(nc.semaphore("fw_weights"))
        zeroed = ctx.enter_context(nc.semaphore("fw_zeroed"))
        o_staged = ctx.enter_context(nc.semaphore("fw_o_staged"))
        o_turned = ctx.enter_context(nc.semaphore("fw_o_turned"))
        oT_ready = ctx.enter_context(nc.semaphore("fw_oT_ready"))
        qkv_ready = ctx.enter_context(nc.semaphore("fw_qkv_ready"))
        qkv_read = ctx.enter_context(nc.semaphore("fw_qkv_read"))
        neg_ready = ctx.enter_context(nc.semaphore("fw_neg_ready"))
        exp_ready = ctx.enter_context(nc.semaphore("fw_exp_ready"))
        rk_ready = ctx.enter_context(nc.semaphore("fw_rk_ready"))
        rke_ready = ctx.enter_context(nc.semaphore("fw_rke_ready"))
        be_ready = ctx.enter_context(nc.semaphore("fw_be_ready"))
        v_ready = ctx.enter_context(nc.semaphore("fw_v_ready"))
        k_ready = ctx.enter_context(nc.semaphore("fw_k_ready"))
        q_ready = ctx.enter_context(nc.semaphore("fw_q_ready"))
        dv_ready = ctx.enter_context(nc.semaphore("fw_dv_ready"))
        hx_ready = ctx.enter_context(nc.semaphore("fw_hx_ready"))
        he_ready = ctx.enter_context(nc.semaphore("fw_he_ready"))
        h_ready = ctx.enter_context(nc.semaphore("fw_h_ready"))
        h_turned = ctx.enter_context(nc.semaphore("fw_h_turned"))
        hT_ready = ctx.enter_context(nc.semaphore("fw_hT_ready"))
        proj_done = ctx.enter_context(nc.semaphore("fw_proj_done"))
        stored = ctx.enter_context(nc.semaphore("fw_stored"))
        dve_prod_q = ctx.enter_context(nc.semaphore("fw_dve_prod_q"))
        dve_prod_k = ctx.enter_context(nc.semaphore("fw_dve_prod_k"))
        pool_prod_q = ctx.enter_context(nc.semaphore("fw_pool_prod_q"))
        pool_prod_k = ctx.enter_context(nc.semaphore("fw_pool_prod_k"))
        pool_updated = ctx.enter_context(nc.semaphore("fw_pool_updated"))
        dve_q_summed = ctx.enter_context(nc.semaphore("fw_dve_q_summed"))
        dve_k_summed = ctx.enter_context(nc.semaphore("fw_dve_k_summed"))
        pool_q_summed = ctx.enter_context(nc.semaphore("fw_pool_q_summed"))
        pool_k_summed = ctx.enter_context(nc.semaphore("fw_pool_k_summed"))
        pe_gap = ctx.enter_context(nc.semaphore("fw_pe_gap"))
        dve_steps = ctx.enter_context(nc.semaphore("fw_dve_steps"))
        pool_steps = ctx.enter_context(nc.semaphore("fw_pool_steps"))
        block = ctx.block()
        def heads2(ap, first, n, w=DH):
            return ap[:, first * 2 * w:(first + n) * 2 * w].rearrange("p (u j) -> p u j", j=w)

        def grid(ap, first, n):
            return ap[:, first * UNIT:(first + n) * UNIT].rearrange("p (u i j) -> p u i j", i=DH, j=DH)

        def part(ap, which):
            return ap.rearrange("p (h w j) -> p h w j", w=2, j=DH)[:, :, which, :]

        def per_head(ap):
            return ap.rearrange("p (h j) -> p h j", j=DH)

        ps = m.ps
        NDG, NPG = len(DVE_GROUPS), len(POOL_GROUPS)

        @block.sync
        def _(sp):
            sp.dma_start(w[:, :], c["fw_w"]).then_inc(weights, 16)
            sp.dma_start(w_out[:, :], c["fw_w_out"]).then_inc(weights, 16)

        @block.vector
        def _(dve):
            step = Chain(dve, dve_steps)

            def features(s, p):
                dve.wait_ge(qkv_read, 3 * s + 6)
                nc.vector.tensor_scalar(neg[:, :], raw[:, QK:QK + 512], 0.0, None, ALU.min).then_inc(neg_ready, 1)
                step(nc.vector.tensor_reduce(small[:, 0, 0:8], per_head(raw[:, RK:RK + 256]), X, ALU.max))
                nc.vector.tensor_tensor(per_head(raw[:, RK:RK + 256]), per_head(raw[:, RK:RK + 256]), inner(small[:, 0, 0:8], DH), ALU.subtract).then_inc(rk_ready, 1)
                dve.wait_ge(exp_ready, s + 1)
                step(nc.vector.scalar_tensor_tensor(raw[:, QK:QK + 512], raw[:, QK:QK + 512], 0.0, neg[:, :], ALU.max, ALU.add))
                step(nc.vector.tensor_reduce(small[:, 1, :], per_head(raw[:, QK:QK + 512]), X, ALU.add))
                step(nc.vector.reciprocal(small[:, 2, :], small[:, 1, :]))
                dve.wait_ge(rke_ready, s + 1)
                step(nc.vector.tensor_reduce(small[:, 3, 0:8], per_head(raw[:, RK:RK + 256]), X, ALU.add))
                step(nc.vector.reciprocal(small[:, 4, 0:8], small[:, 3, 0:8]))
                dve.wait_ge(be_ready, s + 1)
                step(nc.vector.tensor_scalar(be[:, 1, :], be[:, 0, :], 1.0, None, ALU.add))
                nc.vector.reciprocal(beta[:, p, :], be[:, 1, :])
                nc.vector.tensor_tensor(part(Q[:, p, :], 0), per_head(raw[:, QK:QK + 256]), inner(small[:, 2, 0:8], DH), ALU.mult)
                nc.vector.tensor_tensor(part(K[:, p, :], 0), per_head(raw[:, QK + 256:QK + 512]), inner(small[:, 2, 8:16], DH), ALU.mult)
                ins = nc.vector.tensor_tensor(part(K[:, p, :], 1), per_head(raw[:, RK:RK + 256]), inner(small[:, 4, 0:8], DH), ALU.mult)
                ins.then_inc(k_ready, 1)
                dve.wait_ge(k_ready, s + 1)

            def delta(first, n, p):
                a, b = first * 64, (first + n) * 64
                step(nc.vector.tensor_tensor(dv[:, a:b], V[:, p, a:b], ps[0:T, KOUT[first]:KOUT[first] + b - a], ALU.subtract))
                return nc.vector.tensor_tensor(heads2(dv, first, n), heads2(dv, first, n), inner(beta[:, p, 2 * first:2 * (first + n)], DH), ALU.mult)

            def pool_delta(s, g, p):
                dve.wait_ge(pool_k_summed, s * NPG + g + 1)
                delta(*POOL_GROUPS[g], p).then_inc(dv_ready, 1)

            def update(s, g, p):
                first, n = DVE_GROUPS[g]
                dve.wait_ge(dve_k_summed, s * NDG + g + 1)
                step(delta(first, n, p))
                for k in range(first, first + n):
                    step(nc.vector.tensor_tensor(grid(growth, 0, 1), inner(heads2(dv, k, 1), DH), outer(heads2(K[:, p, :], k, 1), DH, 2), ALU.mult))
                    step(nc.vector.tensor_tensor(grid(state, k, 1), grid(state, k, 1), grid(growth, 0, 1), ALU.add))

            def times_q(s, g, p):
                first, n = DVE_GROUPS[g]
                dve.wait_ge(dve_q_summed, s * NDG + g + NDG)
                nc.vector.tensor_tensor(grid(prod_q, 0, n), grid(state, first, n), outer(heads2(Q[:, p, :], first, n), DH, 2), ALU.mult).then_inc(dve_prod_q, 1)

            def times_k(s, g, p):
                first, n = DVE_GROUPS[g]
                dve.wait_ge(dve_k_summed, s * NDG + g + NDG)
                nc.vector.tensor_tensor(grid(prod_k, 0, n), grid(state, first, n), outer(heads2(K[:, p, :], first, n), DH, 2), ALU.mult).then_inc(dve_prod_k, 1)

            def outputs(s):
                dve.wait_ge(dve_q_summed, (s + 1) * NDG)
                dve.wait_ge(pool_q_summed, (s + 1) * NPG)
                dve.wait_ge(h_turned, s + 1)
                both = ps[0:T, QOUT:QOUT + 512].rearrange("p (h w j) -> p h j w", w=2, j=DH)
                ins = nc.vector.tensor_reduce(per_head(hs[:, :]), both, X, ALU.add)
                ins.then_inc(h_ready, 1)
                dve.wait_ge(h_ready, s + 1)

            def soft_query(s, p):
                outputs(s)
                step(nc.vector.tensor_reduce(small[:, 5, 0:8], per_head(hs[:, :]), X, ALU.max))
                nc.vector.tensor_tensor(per_head(hx[:, :]), per_head(hs[:, :]), inner(small[:, 5, 0:8], DH), ALU.subtract).then_inc(hx_ready, 1)
                dve.wait_ge(he_ready, s + 1)
                step(nc.vector.tensor_reduce(small[:, 6, 0:8], per_head(he[:, :]), X, ALU.add))
                step(nc.vector.reciprocal(small[:, 7, 0:8], small[:, 6, 0:8]))
                nc.vector.tensor_tensor(part(Q[:, p, :], 1), per_head(he[:, :]), inner(small[:, 7, 0:8], DH), ALU.mult).then_inc(q_ready, 1)
                dve.wait_ge(q_ready, s + 1)

            def whole_step(s, p, last=False):
                if not last:
                    dve.wait_ge(pool_updated, s * NPG + 1)
                    dve.wait_ge(pool_q_summed, (s + 1) * NPG)
                    features(s + 1, 1 - p)
                dve.wait_ge(v_ready, s + 1)
                for g in range(NDG):
                    update(s, g, p)
                    if g == 0:
                        pool_delta(s, 0, p)
                        soft_query(s, p)
                    times_q(s, g, p)
                    if not last:
                        times_k(s, g, 1 - p)
                    if g + 1 < NPG:
                        pool_delta(s, g + 1, p)

            nc.vector.memset(state[:, 0:POOL_GROUPS[0][0] * UNIT], 0.0)
            for at in KOUT.values():
                nc.vector.memset(ps[0:T, at:at + 128], 0.0)
            step(nc.vector.memset(ps[0:T, QOUT:QOUT + 512], 0.0))
            dve.sem_inc(zeroed, 1)
            dve.sem_inc(pool_updated, 1)
            dve.sem_inc(dve_q_summed, NDG)
            dve.sem_inc(dve_k_summed, NDG)
            dve.sem_inc(pool_q_summed, NPG)
            dve.sem_inc(pool_k_summed, NPG)
            dve.sem_inc(h_turned, 1)
            features(0, 0)
            N = 28
            with dve.Fori(0, B // 2 - 1) as i:
                step.begin(i, 2 * N)
                for u in range(2):
                    whole_step(i * 2 + u, u)
                step.end(B // 2 - 1)
            whole_step(B - 2, 0)
            whole_step(B - 1, 1, last=True)
            outputs(B)
            dve.wait_ge(stored, B + 2)
            step(nc.vector.tensor_tensor(m.h[:, :], m.h[:, :], m.xn[:, D:D + F], ALU.add))

        @block.gpsimd
        def _(pool):
            step = Chain(pool, pool_steps)

            def times_k(s, g, p):
                first, n = POOL_GROUPS[g]
                nc.gpsimd.tensor_tensor(grid(pool_k, 0, n), grid(state, first, n), outer(heads2(K[:, p, :], first, n), DH, 2), ALU.mult).then_inc(pool_prod_k, 1)

            def whole_step(s, p, last=False):
                for g in range(NPG):
                    first, n = POOL_GROUPS[g]
                    pool.wait_ge(dv_ready, s * NPG + g + 1)
                    pool.wait_ge(pool_q_summed, s * NPG + g + NPG)
                    step(nc.gpsimd.tensor_tensor(grid(pool_q, 0, n), inner(heads2(dv, first, n), DH), outer(heads2(K[:, p, :], first, n), DH, 2), ALU.mult))
                    ins = nc.gpsimd.tensor_tensor(grid(state, first, n), grid(state, first, n), grid(pool_q, 0, n), ALU.add)
                    ins.then_inc(pool_updated, 1)
                    pool.wait_ge(pool_updated, s * NPG + g + 2)
                    pool.wait_ge(q_ready, s + 1)
                    nc.gpsimd.tensor_tensor(grid(pool_q, 0, n), grid(state, first, n), outer(heads2(Q[:, p, :], first, n), DH, 2), ALU.mult).then_inc(pool_prod_q, 1)
                    if not last:
                        pool.wait_ge(k_ready, s + 2)
                        pool.wait_ge(pool_k_summed, s * NPG + g + NPG)
                        times_k(s, g, 1 - p)

            nc.gpsimd.memset(state[:, POOL_GROUPS[0][0] * UNIT:], 0.0).then_inc(zeroed, 1)
            pool.wait_ge(zeroed, 2)
            N = 2
            with pool.Fori(0, B // 2 - 1) as i:
                step.begin(i, 2 * N)
                for u in range(2):
                    whole_step(i * 2 + u, u)
                step.end(B // 2 - 1)
            whole_step(B - 2, 0)
            whole_step(B - 1, 1, last=True)

        @block.tensor
        def _(pe):
            def turn_and_project(s):
                pe.wait_ge(o_staged, s + 1)
                pe.wait_ge(qkv_read, 3 * s + 3)
                pe.sem_inc(pe_gap, 1)
                nc.tensor.transpose(ps[0:D, IN_BANK:IN_BANK + T], o[:, 0, :], m.ident[0:T, 0:T]).then_inc(o_turned, 1)
                pe.wait_ge(oT_ready, s + 1)
                for k, (a, b) in enumerate(CUTS):
                    if k == 1 and not (type(s) is int and s == 0):
                        pe.wait_ge(stored, s)
                    if k == 2:
                        pe.wait_ge(qkv_read, 3 * s + 4)
                    at = (IN_BANK, H_BANK)[k % 2]
                    nc.tensor.matmul(ps[0:T, at:at + b - a], oT[:, :], w[:, a:b], start=True, stop=True).then_inc(qkv_ready, 1)

            def sum_rows(products, at, n):
                v = products[:, 0:n * UNIT].rearrange("p (r j) -> p r j", j=DH)
                for j in range(DH):
                    ins = nc.tensor.matmul(ps[0:T, at:at + n * 2 * DH], m.ident[0:T, 0:T], v[:, :, j], start=(j == 0), stop=(j == DH - 1))
                return ins

            def project_h(s, bank_used=True):
                pe.wait_ge(h_ready, s + 1)
                pe.wait_ge(hT_ready, s + 1)
                pe.wait_ge(stored, s + 1)
                if bank_used:
                    pe.wait_ge(qkv_read, 3 * s + 8)
                for k in range(2):
                    ins = nc.tensor.transpose(ps[:, H_BANK + k * T:H_BANK + (k + 1) * T], hs[:, k * 128:(k + 1) * 128], m.ident[0:T, 0:T])
                ins.then_inc(h_turned, 1)
                pe.wait_ge(hT_ready, s + 2)
                nc.tensor.matmul(ps[0:T, H_BANK + 256:H_BANK + 256 + D], hT[:, 0:T], w_out[:, 0:D], start=True, stop=False)
                nc.tensor.matmul(ps[0:T, H_BANK + 256:H_BANK + 256 + D], hT[:, T:2 * T], w_out[:, D:2 * D], start=False, stop=True).then_inc(proj_done, 1)

            def whole_step(s, p, last=False, more=True):
                for g in range(NDG):
                    first, n = DVE_GROUPS[g]
                    pe.wait_ge(dve_prod_q, s * NDG + g + 1)
                    if g == 0:
                        pe.wait_ge(h_ready, s + 1)
                    sum_rows(prod_q, QOUT + first * 2 * DH, n).then_inc(dve_q_summed, 1)
                    if not last:
                        pe.wait_ge(dve_prod_k, s * NDG + g + 1)
                        sum_rows(prod_k, KOUT[first], n).then_inc(dve_k_summed, 1)
                    if g < NPG:
                        first, n = POOL_GROUPS[g]
                        pe.wait_ge(pool_prod_q, s * NPG + g + 1)
                        sum_rows(pool_q, QOUT + first * 2 * DH, n).then_inc(pool_q_summed, 1)
                        if not last:
                            pe.wait_ge(pool_prod_k, s * NPG + g + 1)
                            sum_rows(pool_k, KOUT[first], n).then_inc(pool_k_summed, 1)
                    if g == 0:
                        project_h(s, bank_used=not last)
                    if g == 1 and more:
                        turn_and_project(s + 2)

            pe.wait_ge(weights, 32)
            pe.wait_ge(zeroed, 2)
            turn_and_project(0)
            turn_and_project(1)
            with pe.Fori(0, B // 2 - 1) as i:
                for u in range(2):
                    whole_step(i * 2 + u, u)
            whole_step(B - 2, 0, more=False)
            whole_step(B - 1, 1, last=True, more=False)
            project_h(B, bank_used=False)

        @block.scalar
        def _(act):
            def stage(s):
                act.wait_ge(o_turned, s + 1)
                nc.scalar.activation(o[:, 0, :], m.xn[:, bass.ds((s + 1) * D, D)], ACT.Copy).then_inc(o_staged, 1)
                act.wait_ge(o_turned, s + 2)
                nc.scalar.activation(oT[:, :], ps[0:D, IN_BANK:IN_BANK + T], ACT.Copy).then_inc(oT_ready, 1)
                if not (type(s) is int and s == 0):
                    act.wait_ge(k_ready, s)
                for k, (a, b) in enumerate(CUTS):
                    act.wait_ge(qkv_ready, 3 * s + k + 1)
                    at = (IN_BANK, H_BANK)[k % 2]
                    nc.scalar.activation(raw[:, a:b], ps[0:T, at:at + b - a], ACT.Copy).then_inc(qkv_read, 1)

            def features(s, p):
                act.wait_ge(neg_ready, s + 1)
                nc.scalar.activation(neg[:, :], neg[:, :], ACT.Exp).then_inc(exp_ready, 1)
                act.wait_ge(rk_ready, s + 1)
                nc.scalar.activation(raw[:, RK:RK + 256], raw[:, RK:RK + 256], ACT.Exp).then_inc(rke_ready, 1)
                nc.scalar.activation(be[:, 0, :].rearrange("p (h w) -> p w h", w=2), raw[:, BB:BB + 16].rearrange("p (w h) -> p w h", w=2), ACT.Exp, scale=-1.0).then_inc(be_ready, 1)
                nc.scalar.activation(part(V[:, p, :], 0), per_head(raw[:, VV:VV + 256]), ACT.Copy)
                nc.scalar.activation(part(V[:, p, :], 1), per_head(raw[:, RV:RV + 256]), ACT.Copy).then_inc(v_ready, 1)

            def soft(s):
                act.wait_ge(hx_ready, s + 1)
                nc.scalar.activation(he[:, :], hx[:, :], ACT.Exp).then_inc(he_ready, 1)

            def finish(s):
                act.wait_ge(h_turned, s + 2)
                act.wait_ge(proj_done, s + 1)
                nc.scalar.activation(hT[:, :], ps[:, H_BANK:H_BANK + 2 * T], ACT.Copy).then_inc(hT_ready, 1)
                act.wait_ge(proj_done, s + 2)
                nc.scalar.activation(m.xn[:, bass.ds(s * D, D)], ps[0:T, H_BANK + 256:H_BANK + 256 + D], ACT.Copy).then_inc(stored, 1)

            def whole_step(s, p, last=False, more=True):
                if not last:
                    features(s + 1, 1 - p)
                soft(s)
                finish(s)
                if more:
                    stage(s + 2)

            act.sem_inc(qkv_read, 3)
            act.sem_inc(o_turned, 1)
            act.sem_inc(hT_ready, 1)
            act.sem_inc(stored, 1)
            act.sem_inc(proj_done, 1)
            stage(0)
            features(0, 0)
            stage(1)
            with act.Fori(0, B // 2 - 1) as i:
                for u in range(2):
                    whole_step(i * 2 + u, u)
            whole_step(B - 2, 0, more=False)
            whole_step(B - 1, 1, last=True, more=False)
            finish(B)


class Turned:

    def __init__(self, nc, m, ctx, tag):
        self.nc, self.m = nc, m
        self.staged = ctx.enter_context(nc.sbuf_tensor(f"{tag}_staged", [T, 2, G * D], F32))
        self.xT = ctx.enter_context(nc.sbuf_tensor(f"{tag}_xT", [D + 1, 2, GT], F32))
        self.x_staged = ctx.enter_context(nc.semaphore(f"{tag}_x_staged"))
        self.x_turned = ctx.enter_context(nc.semaphore(f"{tag}_x_turned"))
        self.x_ready = ctx.enter_context(nc.semaphore(f"{tag}_x_ready"))
        self.x_used = ctx.enter_context(nc.semaphore(f"{tag}_x_used"))
        self.gap = ctx.enter_context(nc.semaphore(f"{tag}_gap"))
        self.ones_set = ctx.enter_context(nc.semaphore(f"{tag}_ones_set"))

    def credits(self, pool):
        self.nc.gpsimd.memset(self.xT[D:D + 1, :, :], 1.0).then_inc(self.ones_set, 1)
        pool.wait_ge(self.ones_set, 1)
        pool.sem_inc(self.x_turned, 2)
        pool.sem_inc(self.x_ready, 1)
        pool.sem_inc(self.x_used, 2)

    def copy_in(self, pool, n, u):
        pool.wait_ge(self.x_turned, n + 1)
        self.nc.gpsimd.tensor_copy(self.staged[:, u, :], self.m.xn[:, bass.ds(n * (G * D), G * D)]).then_inc(self.x_staged, 1)

    def turn(self, pe, n, u):
        pe.wait_ge(self.x_staged, n + 1)
        pe.wait_ge(self.x_ready, n + 1)
        pe.sem_inc(self.gap, 1)
        for q in range(G):
            ins = self.nc.tensor.transpose(self.m.ps[0:D, q * T:(q + 1) * T], self.staged[:, u, q * D:(q + 1) * D], self.m.ident[0:T, 0:T])
        ins.then_inc(self.x_turned, 1)
        pe.wait_ge(self.x_ready, n + 2)

    def take_out(self, act, n, u):
        act.wait_ge(self.x_turned, n + 3)
        act.wait_ge(self.x_used, n + 1)
        self.nc.scalar.activation(self.xT[0:D, u, :], self.m.ps[0:D, 0:GT], ACT.Copy).then_inc(self.x_ready, 1)

    def columns(self, u, q):
        return self.xT[:, u, q * T:(q + 1) * T]


GONE = -3.0e38
HID = 4 * D
KEPT = max(1, T // 2) - 1


def depth_ffn(nc, m, c):
    with Layer(nc) as ctx:
        w1 = ctx.enter_context(nc.sbuf_tensor("mod_w1_sb", [D, HID], F32))
        b1 = ctx.enter_context(nc.sbuf_tensor("mod_b1_sb", [128, 2], F32))
        w2 = ctx.enter_context(nc.sbuf_tensor("mod_w2_sb", [128, 2 * D], F32))
        b2 = ctx.enter_context(nc.sbuf_tensor("mod_b2_sb", [1, D], F32))
        wr = ctx.enter_context(nc.sbuf_tensor("mod_wr_sb", [T, D], F32))
        br = ctx.enter_context(nc.sbuf_tensor("mod_br_sb", [T, 1], F32))
        y = ctx.enter_context(nc.sbuf_tensor("mod_y", [T, F], F32))
        rating = ctx.enter_context(nc.sbuf_tensor("mod_rating", [T, B], F32))
        rated = ctx.enter_context(nc.sbuf_tensor("mod_rated", [T, B], F32))
        ratingT = ctx.enter_context(nc.sbuf_tensor("mod_ratingT", [B, T], F32))
        left = ctx.enter_context(nc.sbuf_tensor("mod_left", [B, T], F32))
        top = ctx.enter_context(nc.sbuf_tensor("mod_top", [B, 8], F32))
        keptT = ctx.enter_context(nc.sbuf_tensor("mod_keptT", [B, T], F32))
        kept = ctx.enter_context(nc.sbuf_tensor("mod_kept", [T, B], F32))
        g = ctx.enter_context(nc.sbuf_tensor("mod_g", [128, 2, 2, GT], F32))
        weights = ctx.enter_context(nc.semaphore("mod_weights"))
        rating_ready = ctx.enter_context(nc.semaphore("mod_rating_ready"))
        rating_turned = ctx.enter_context(nc.semaphore("mod_rating_turned"))
        kept_ready = ctx.enter_context(nc.semaphore("mod_kept_ready"))
        kept_turned = ctx.enter_context(nc.semaphore("mod_kept_turned"))
        hidden_ready = ctx.enter_context(nc.semaphore("mod_hidden_ready"))
        act_ready = ctx.enter_context(nc.semaphore("mod_act_ready"))
        y_ready = ctx.enter_context(nc.semaphore("mod_y_ready"))
        y_read = ctx.enter_context(nc.semaphore("mod_y_read"))
        steps = ctx.enter_context(nc.semaphore("mod_steps"))
        t = Turned(nc, m, ctx, "mod")
        block = ctx.block()
        ps = m.ps

        @block.sync
        def _(sp):
            sp.dma_start(w1[:, :], c["mod_w1"]).then_inc(weights, 16)
            sp.dma_start(b1[:, :], c["mod_b1"]).then_inc(weights, 16)
            sp.dma_start(w2[:, :], c["mod_w2"]).then_inc(weights, 16)
            sp.dma_start(b2[:, :], c["mod_b2"]).then_inc(weights, 16)
            sp.dma_start(wr[:, :], c["mod_wr"].broadcast_to([T, D])).then_inc(weights, 16)
            sp.dma_start(br[:, :], c["mod_br"].broadcast_to([T, 1])).then_inc(weights, 16)

        @block.gpsimd
        def _(pool):
            t.credits(pool)
            with pool.Fori(0, NG // 2) as i:
                for u in range(2):
                    t.copy_in(pool, i * 2 + u, u)

        @block.vector
        def _(dve):
            step = Chain(dve, steps)
            dve.sem_inc(y_read, 2)
            dve.wait_ge(weights, 96)
            y3 = y[:, :].rearrange("p (b d) -> p b d", d=D)
            step(nc.vector.tensor_tensor(y3, m.xn[:, 0:F].rearrange("p (b d) -> p b d", d=D), outer(wr[:, :], B), ALU.mult))
            step(nc.vector.tensor_reduce(rating[:, :], y3, X, ALU.add))
            nc.vector.tensor_scalar(rated[:, :], rating[:, :], br[:, 0:1], None, ALU.add).then_inc(rating_ready, 1)
            dve.wait_ge(rating_turned, 1)
            step(nc.vector.tensor_copy(ratingT[:, :], ps[0:B, 3584:3584 + T]))
            step(nc.vector.tensor_copy(left[:, :], ratingT[:, :]))
            for k in range(0, KEPT, 8):
                step(nc.vector.max(top[:, :], left[:, :]))
                if KEPT - k < 8:
                    step(nc.vector.memset(top[:, KEPT - k:8], GONE))
                step(nc.vector.match_replace(left[:, :], top[:, :], left[:, :], GONE))
            nc.vector.scalar_tensor_tensor(keptT[:, :], left[:, :], GONE, ratingT[:, :], ALU.is_equal, ALU.mult).then_inc(kept_ready, 1)
            dve.wait_ge(kept_turned, 1)
            step(nc.vector.tensor_copy(kept[:, :], ps[0:T, 3584:3584 + B]))
            with dve.Fori(0, NG // 2) as i:
                for u in range(2):
                    n = i * 2 + u
                    dve.wait_ge(y_ready, n + 3)
                    nc.vector.tensor_tensor(y[:, bass.ds(n * (G * D), G * D)].rearrange("p (b d) -> p b d", d=D),
                                            ps[0:T, 1536 + u * 512:1536 + u * 512 + G * D].rearrange("p (b d) -> p b d", d=D),
                                            inner(kept[:, bass.ds(n * G, G)], D), ALU.mult).then_inc(y_read, 1)
            dve.wait_ge(y_read, NG + 2)
            step(nc.vector.tensor_tensor(m.h[:, :], m.h[:, :], m.xn[:, 0:F], ALU.add))
            step(nc.vector.tensor_tensor(m.h[:, :], m.h[:, :], y[:, :], ALU.add))

        @block.tensor
        def _(pe):
            pe.sem_inc(y_ready, 2)
            pe.wait_ge(rating_ready, 1)
            nc.tensor.transpose(ps[0:B, 3584:3584 + T], rated[:, :], m.ident[0:T, 0:T]).then_inc(rating_turned, 1)
            pe.wait_ge(kept_ready, 1)
            nc.tensor.transpose(ps[0:T, 3584:3584 + B], keptT[:, :], m.ident[0:B, 0:B]).then_inc(kept_turned, 1)
            pe.wait_ge(weights, 96)
            pe.wait_ge(t.ones_set, 1)
            with pe.Fori(0, NG // 2) as i:
                for u in range(2):
                    n = i * 2 + u
                    t.turn(pe, n, u)
                    pe.wait_ge(act_ready, n + 1)
                    for k in range(2):
                        ins = nc.tensor.matmul(ps[:, 512 * (1 + k):512 * (1 + k) + GT], w1[:, k * 128:(k + 1) * 128], t.xT[0:D, u, :], start=True, stop=True)
                    ins.then_inc(hidden_ready, 1)
                    pe.wait_ge(act_ready, n + 2)
                    pe.sem_inc(t.x_used, 1)
                    pe.wait_ge(y_read, n + 1)
                    for q in range(G):
                        out = ps[0:T, 1536 + u * 512 + q * D:1536 + u * 512 + (q + 1) * D]
                        for k in range(2):
                            nc.tensor.matmul(out, g[:, u, k, q * T:(q + 1) * T], w2[:, k * D:(k + 1) * D], start=(k == 0), stop=False)
                        ins = nc.tensor.matmul(out, m.ones[0:1, 0:T], b2[0:1, :], start=False, stop=True)
                    ins.then_inc(y_ready, 1)

        @block.scalar
        def _(act):
            act.sem_inc(act_ready, 1)
            act.wait_ge(weights, 96)
            act.wait_ge(kept_turned, 1)
            with act.Fori(0, NG // 2) as i:
                for u in range(2):
                    n = i * 2 + u
                    t.take_out(act, n, u)
                    act.wait_ge(hidden_ready, n + 1)
                    act.wait_ge(y_ready, n + 1)
                    for k in range(2):
                        ins = nc.scalar.activation(g[:, u, k, :], ps[:, 512 * (1 + k):512 * (1 + k) + GT], ACT.Gelu_apprx_tanh, bias=b1[:, k:k + 1])
                    ins.then_inc(act_ready, 1)


WIN = 8
SHIFT = 4
TP = -(-T // WIN) * WIN
NWIN = B * TP // WIN
WH = 8
WD = D // WH


def window_attention(nc, m, c):
    qkv_dram = nc.dram_tensor("win_qkv_scratch", (B, TP, 3 * D), F32).ap()
    out_dram = nc.dram_tensor("win_out_scratch", (B, TP, D), F32).ap()
    window_products(nc, m, c, qkv_dram)
    window_heads(nc, m, c, qkv_dram, out_dram)
    window_projection(nc, m, c, out_dram)


def window_products(nc, m, c, qkv_dram):
    with Layer(nc) as ctx:
        w = ctx.enter_context(nc.sbuf_tensor("winp_w_sb", [D + 1, 3 * D], F32))
        out = ctx.enter_context(nc.sbuf_tensor("winp_out", [T, 2, G * 3 * D], F32))
        weights = ctx.enter_context(nc.semaphore("winp_weights"))
        padded = ctx.enter_context(nc.semaphore("winp_padded"))
        ready = ctx.enter_context(nc.semaphore("winp_ready"))
        copied = ctx.enter_context(nc.semaphore("winp_copied"))
        stored0 = ctx.enter_context(nc.semaphore("winp_stored0"))
        stored1 = ctx.enter_context(nc.semaphore("winp_stored1"))
        t = Turned(nc, m, ctx, "winp")
        block = ctx.block()
        stored = [stored0, stored1]

        @block.sync
        def _(sp):
            sp.dma_start(w[:, :], c["win_w"]).then_inc(weights, 16)
            sp.dma_start(qkv_dram[:, T - SHIFT:TP - SHIFT, :], c["win_w"][D:D + 1, :].unsqueeze(1).broadcast_to([B, TP - T, 3 * D])).then_inc(padded, 16)
            with sp.Fori(0, NG // 2) as i:
                for u in range(2):
                    n = i * 2 + u
                    sp.wait_ge(copied, n + 3)
                    to = qkv_dram[bass.ds(n * G, G), :, :]
                    src = out[:, u, :].rearrange("t (b e) -> t b e", e=3 * D)
                    sp.dma_start(to[:, 0:T - SHIFT, :].rearrange("b t e -> t b e"), src[SHIFT:T]).then_inc(stored[u], 16)
                    sp.dma_start(to[:, TP - SHIFT:TP, :].rearrange("b t e -> t b e"), src[0:SHIFT]).then_inc(stored[u], 16)
            sp.wait_ge(stored[0], 16 * NG + 1)
            sp.wait_ge(stored[1], 16 * NG + 1)
            sp.wait_ge(padded, 16)

        @block.gpsimd
        def _(pool):
            t.credits(pool)
            with pool.Fori(0, NG // 2) as i:
                for u in range(2):
                    t.copy_in(pool, i * 2 + u, u)

        @block.tensor
        def _(pe):
            pe.wait_ge(weights, 16)
            pe.wait_ge(t.ones_set, 1)
            with pe.Fori(0, NG // 2) as i:
                for u in range(2):
                    n = i * 2 + u
                    t.turn(pe, n, u)
                    pe.wait_ge(copied, n + 1)
                    for q in range(G):
                        at = 512 * (1 + 2 * u + q // 2) + (q % 2) * 3 * D
                        ins = nc.tensor.matmul(m.ps[0:T, at:at + 3 * D], t.columns(u, q), w[:, :], start=True, stop=True)
                    ins.then_inc(ready, 1)
                    pe.wait_ge(ready, n + 1)
                    pe.sem_inc(t.x_used, 1)

        @block.scalar
        def _(act):
            with act.Fori(0, NG // 2) as i:
                for u in range(2):
                    t.take_out(act, i * 2 + u, u)

        @block.vector
        def _(dve):
            dve.sem_inc(copied, 2)
            dve.sem_inc(stored0, 1)
            dve.sem_inc(stored1, 1)
            with dve.Fori(0, NG // 2) as i:
                for u in range(2):
                    n = i * 2 + u
                    dve.wait_ge(ready, n + 1)
                    dve.wait_ge(stored[u], i * 32 + 1)
                    src = m.ps[0:T, 512 * (1 + 2 * u):512 * (3 + 2 * u)].rearrange("t (k e) -> t k e", k=2)[:, :, 0:6 * D]
                    nc.vector.tensor_copy(out[:, u, :].rearrange("t (k e) -> t k e", k=2), src).then_inc(copied, 1)


def window_heads(nc, m, c, qkv_dram, out_dram):
    tiles = NWIN // 128
    SC = WH * WIN * WIN
    qkv_rows = qkv_dram.rearrange("b (w t) e -> (b w) (t e)", t=WIN)
    out_rows = out_dram.rearrange("b (w t) e -> (b w) (t e)", t=WIN)
    with Layer(nc) as ctx:
        rows = ctx.enter_context(nc.sbuf_tensor("winh_in", [128, 2, WIN * 3 * D], F32))
        bias = ctx.enter_context(nc.sbuf_tensor("winh_bias", [128, SC], F32))
        prod = ctx.enter_context(nc.sbuf_tensor("winh_prod", [128, SC * WD], F32))
        scores = ctx.enter_context(nc.sbuf_tensor("winh_scores", [128, SC], F32))
        biased = ctx.enter_context(nc.sbuf_tensor("winh_biased", [128, SC], F32))
        probs = ctx.enter_context(nc.sbuf_tensor("winh_probs", [128, SC], F32))
        most = ctx.enter_context(nc.sbuf_tensor("winh_max", [128, WH * WIN], F32))
        total = ctx.enter_context(nc.sbuf_tensor("winh_sum", [128, WH * WIN], F32))
        inv = ctx.enter_context(nc.sbuf_tensor("winh_inv", [128, WH * WIN], F32))
        out = ctx.enter_context(nc.sbuf_tensor("winh_out", [128, 2, WIN * D], F32))
        bias_loaded = ctx.enter_context(nc.semaphore("winh_bias_loaded"))
        loaded0 = ctx.enter_context(nc.semaphore("winh_loaded0"))
        loaded1 = ctx.enter_context(nc.semaphore("winh_loaded1"))
        stored0 = ctx.enter_context(nc.semaphore("winh_stored0"))
        stored1 = ctx.enter_context(nc.semaphore("winh_stored1"))
        centred = ctx.enter_context(nc.semaphore("winh_centred"))
        exp_ready = ctx.enter_context(nc.semaphore("winh_exp_ready"))
        out_ready = ctx.enter_context(nc.semaphore("winh_out_ready"))
        steps = ctx.enter_context(nc.semaphore("winh_steps"))
        block = ctx.block()
        loaded, stored = [loaded0, loaded1], [stored0, stored1]

        @block.sync
        def _(sp):
            sp.dma_start(bias[:, :], c["win_bias"].broadcast_to([128, SC])).then_inc(bias_loaded, 16)
            with sp.Fori(0, tiles // 2) as i:
                for u in range(2):
                    sp.wait_ge(out_ready, i * 2 + u + 1)
                    sp.dma_start(rows[:, u, :], qkv_rows[bass.ds((i * 2 + u) * 128, 128), :]).then_inc(loaded[u], 16)

        @block.vector
        def _(dve):
            step = Chain(dve, steps)
            dve.sem_inc(out_ready, 2)
            dve.sem_inc(stored0, 1)
            dve.sem_inc(stored1, 1)
            dve.wait_ge(bias_loaded, 16)
            N = 8
            with dve.Fori(0, tiles // 2) as i:
                step.begin(i, 2 * N)
                for u in range(2):
                    row = rows[:, u, :].rearrange("p (t s h d) -> p t s h d", t=WIN, s=3, h=WH)
                    heads = prod[:, :].rearrange("p (h a b e) -> p h a b e", h=WH, a=WIN, b=WIN)
                    dve.wait_ge(loaded[u], i * 16 + 16)
                    dve.wait_ge(out_ready, i * 2 + u + 2)
                    for hd in range(WH):
                        ins = nc.vector.tensor_tensor(heads[:, hd], outer(row[:, :, 0, hd, :], WIN, 2), outer(row[:, :, 1, hd, :], WIN, 1), ALU.mult)
                    step(ins)
                    step(nc.vector.tensor_reduce(scores[:, :], prod[:, :].rearrange("p (s e) -> p s e", e=WD), X, ALU.add))
                    step(nc.vector.scalar_tensor_tensor(biased[:, :], scores[:, :], WD ** -0.5, bias[:, :], ALU.mult, ALU.add))
                    per = lambda a: a.rearrange("p (r k) -> p r k", k=WIN)
                    step(nc.vector.tensor_reduce(most[:, :], per(biased[:, :]), X, ALU.max))
                    nc.vector.tensor_tensor(per(scores[:, :]), per(biased[:, :]), inner(most[:, :], WIN), ALU.subtract).then_inc(centred, 1)
                    dve.wait_ge(exp_ready, i * 2 + u + 1)
                    step(nc.vector.tensor_reduce(total[:, :], per(probs[:, :]), X, ALU.add))
                    step(nc.vector.reciprocal(inv[:, :], total[:, :]))
                    step(nc.vector.tensor_tensor(per(biased[:, :]), per(probs[:, :]), inner(inv[:, :], WIN), ALU.mult))
                    pr = biased[:, :].rearrange("p (h q k) -> p h q k", h=WH, q=WIN)
                    for hd in range(WH):
                        v = row[:, :, 2, hd, :].rearrange("p k d -> p d k")
                        ins = nc.vector.tensor_tensor(heads[:, hd], outer(pr[:, hd], WD, 2), outer(v, WIN, 1), ALU.mult)
                    step(ins)
                    dve.wait_ge(stored[u], i * 16 + 1)
                    nc.vector.tensor_reduce(out[:, u, :].rearrange("p (q h d) -> p h q d", h=WH, d=WD), heads, X, ALU.add).then_inc(out_ready, 1)
                step.end(tiles // 2)

        @block.scalar
        def _(act):
            with act.Fori(0, tiles // 2) as i:
                for u in range(2):
                    n = i * 2 + u
                    act.wait_ge(centred, n + 1)
                    nc.scalar.activation(probs[:, :], scores[:, :], ACT.Exp).then_inc(exp_ready, 1)
                    act.wait_ge(out_ready, n + 3)
                    act.dma_start(out_rows[bass.ds(n * 128, 128), :], out[:, u, :]).then_inc(stored[u], 16)
            act.wait_ge(stored[0], 16 * (tiles // 2) + 1)
            act.wait_ge(stored[1], 16 * (tiles // 2) + 1)


def window_projection(nc, m, c, out_dram):
    with Layer(nc) as ctx:
        w = ctx.enter_context(nc.sbuf_tensor("wino_w_sb", [D + 1, D], F32))
        weights = ctx.enter_context(nc.semaphore("wino_weights"))
        loaded = ctx.enter_context(nc.semaphore("wino_loaded"))
        ready = ctx.enter_context(nc.semaphore("wino_ready"))
        added = ctx.enter_context(nc.semaphore("wino_added"))
        t = Turned(nc, m, ctx, "wino")
        block = ctx.block()

        @block.sync
        def _(sp):
            sp.dma_start(w[:, :], c["win_proj"]).then_inc(weights, 16)
            x3 = m.xn[:, 0:F].rearrange("t (b d) -> t b d", d=D)
            sp.dma_start(x3[SHIFT:T], out_dram[:, 0:T - SHIFT, :].rearrange("b t d -> t b d")).then_inc(loaded, 16)
            sp.dma_start(x3[0:SHIFT], out_dram[:, TP - SHIFT:TP, :].rearrange("b t d -> t b d")).then_inc(loaded, 16)

        @block.gpsimd
        def _(pool):
            t.credits(pool)
            pool.wait_ge(loaded, 32)
            with pool.Fori(0, NG // 2) as i:
                for u in range(2):
                    t.copy_in(pool, i * 2 + u, u)

        @block.tensor
        def _(pe):
            pe.wait_ge(weights, 16)
            pe.wait_ge(t.ones_set, 1)
            with pe.Fori(0, NG // 2) as i:
                for u in range(2):
                    n = i * 2 + u
                    t.turn(pe, n, u)
                    pe.wait_ge(added, n + 1)
                    for q in range(G):
                        at = 512 * (1 + u) + q * D
                        ins = nc.tensor.matmul(m.ps[0:T, at:at + D], t.columns(u, q), w[:, :], start=True, stop=True)
                    ins.then_inc(ready, 1)
                    pe.wait_ge(ready, n + 1)
                    pe.sem_inc(t.x_used, 1)

        @block.scalar
        def _(act):
            with act.Fori(0, NG // 2) as i:
                for u in range(2):
                    t.take_out(act, i * 2 + u, u)

        @block.vector
        def _(dve):
            dve.sem_inc(added, 2)
            with dve.Fori(0, NG // 2) as i:
                for u in range(2):
                    n = i * 2 + u
                    dve.wait_ge(ready, n + 1)
                    group = m.h[:, bass.ds(n * (G * D), G * D)]
                    nc.vector.tensor_tensor(group, m.ps[0:T, 512 * (1 + u):512 * (1 + u) + G * D], group, ALU.add).then_inc(added, 1)


E1 = 32
H1 = D // 4
FAR = 1.0e30


def top1_experts(nc, m, c):
    CH = E1 * H1 // 128
    with Layer(nc) as ctx:
        wr = ctx.enter_context(nc.sbuf_tensor("top1_wr_sb", [D + 1, E1], F32))
        w1 = ctx.enter_context(nc.sbuf_tensor("top1_w1_sb", [D + 1, E1 * H1], F32))
        w2 = ctx.enter_context(nc.sbuf_tensor("top1_w2_sb", [128, CH * D], F32))
        b2 = ctx.enter_context(nc.sbuf_tensor("top1_b2_sb", [E1, D], F32))
        spread = ctx.enter_context(nc.sbuf_tensor("top1_spread_sb", [E1, E1 * H1], F32))
        count = ctx.enter_context(nc.sbuf_tensor("top1_count_sb", [T, E1], F32))
        logits = ctx.enter_context(nc.sbuf_tensor("top1_logits", [T, G, E1], F32))
        top = ctx.enter_context(nc.sbuf_tensor("top1_top", [T, G, 8], F32))
        at8 = ctx.enter_context(nc.sbuf_tensor("top1_at", [T, G, 8], U32))
        atf = ctx.enter_context(nc.sbuf_tensor("top1_atf", [T, G], F32))
        chosen = ctx.enter_context(nc.sbuf_tensor("top1_chosen", [T, G, E1], F32))
        chosenT = ctx.enter_context(nc.sbuf_tensor("top1_chosenT", [E1, GT], F32))
        farT = ctx.enter_context(nc.sbuf_tensor("top1_farT", [E1, GT], F32))
        hidden = ctx.enter_context(nc.sbuf_tensor("top1_hidden", [128, CH, GT], F32))
        weights = ctx.enter_context(nc.semaphore("top1_weights"))
        rated = ctx.enter_context(nc.semaphore("top1_rated"))
        chosen_ready = ctx.enter_context(nc.semaphore("top1_chosen_ready"))
        chosen_turned = ctx.enter_context(nc.semaphore("top1_chosen_turned"))
        far_ready = ctx.enter_context(nc.semaphore("top1_far_ready"))
        hidden_ready = ctx.enter_context(nc.semaphore("top1_hidden_ready"))
        relu_ready = ctx.enter_context(nc.semaphore("top1_relu_ready"))
        out_ready = ctx.enter_context(nc.semaphore("top1_out_ready"))
        added = ctx.enter_context(nc.semaphore("top1_added"))
        dve_gap = ctx.enter_context(nc.semaphore("top1_dve_gap"))
        steps = ctx.enter_context(nc.semaphore("top1_steps"))
        t = Turned(nc, m, ctx, "top1")
        block = ctx.block()
        ps = m.ps

        @block.sync
        def _(sp):
            for to, name in ((wr, "top1_wr"), (w1, "top1_w1"), (w2, "top1_w2"), (b2, "top1_b2"), (spread, "top1_spread")):
                sp.dma_start(to[:, :], c[name]).then_inc(weights, 16)
            sp.dma_start(count[:, :], c["count"][:, 0:E1].broadcast_to([T, E1])).then_inc(weights, 16)

        @block.gpsimd
        def _(pool):
            t.credits(pool)
            with pool.Fori(0, NG // 2) as i:
                for u in range(2):
                    t.copy_in(pool, i * 2 + u, u)

        @block.tensor
        def _(pe):
            pe.wait_ge(weights, 96)
            pe.wait_ge(t.ones_set, 1)
            with pe.Fori(0, NG // 2) as i:
                for u in range(2):
                    n = i * 2 + u
                    t.turn(pe, n, u)
                    pe.wait_ge(far_ready, n + 1)
                    for q in range(G):
                        ins = nc.tensor.matmul(ps[0:T, 512 + q * E1:512 + (q + 1) * E1], t.columns(u, q), wr[:, :], start=True, stop=True)
                    ins.then_inc(rated, 1)
                    pe.wait_ge(relu_ready, n + 1)
                    pe.wait_ge(chosen_ready, n + 1)
                    for q in range(G):
                        ins = nc.tensor.transpose(ps[0:E1, 1024 + q * T:1024 + (q + 1) * T], chosen[:, q, :], m.ident[0:T, 0:T])
                    ins.then_inc(chosen_turned, 1)
                    pe.wait_ge(far_ready, n + 2)
                    for k in range(CH):
                        out = ps[:, 512 * (3 + k):512 * (3 + k) + GT]
                        nc.tensor.matmul(out, w1[:, k * 128:(k + 1) * 128], t.xT[:, u, :], start=True, stop=False)
                        ins = nc.tensor.matmul(out, spread[:, k * 128:(k + 1) * 128], farT[:, :], start=False, stop=True)
                    ins.then_inc(hidden_ready, 1)
                    pe.wait_ge(relu_ready, n + 2)
                    pe.sem_inc(t.x_used, 1)
                    pe.wait_ge(added, n + 1)
                    for q in range(G):
                        out = ps[0:T, 3584 + q * D:3584 + (q + 1) * D]
                        for k in range(CH):
                            nc.tensor.matmul(out, hidden[:, k, q * T:(q + 1) * T], w2[:, k * D:(k + 1) * D], start=(k == 0), stop=False)
                        ins = nc.tensor.matmul(out, chosenT[:, q * T:(q + 1) * T], b2[:, :], start=False, stop=True)
                    ins.then_inc(out_ready, 1)

        @block.scalar
        def _(act):
            act.sem_inc(relu_ready, 1)
            with act.Fori(0, NG // 2) as i:
                for u in range(2):
                    n = i * 2 + u
                    t.take_out(act, n, u)
                    act.wait_ge(hidden_ready, n + 1)
                    act.wait_ge(out_ready, n + 1)
                    for k in range(CH):
                        ins = nc.scalar.activation(hidden[:, k, :], ps[:, 512 * (3 + k):512 * (3 + k) + GT], ACT.Relu)
                    ins.then_inc(relu_ready, 1)

        @block.vector
        def _(dve):
            step = Chain(dve, steps, dve_gap)
            dve.sem_inc(far_ready, 1)
            dve.sem_inc(added, 1)
            dve.sem_inc(out_ready, 1)
            dve.wait_ge(weights, 96)
            N = 5
            with dve.Fori(0, NG // 2) as i:
                step.begin(i, 2 * N)
                for u in range(2):
                    n = i * 2 + u
                    dve.wait_ge(rated, n + 1)
                    step(nc.vector.tensor_copy(logits[:, :, :], ps[0:T, 512:512 + G * E1].rearrange("t (q e) -> t q e", e=E1)), gap=True)
                    for q in range(G):
                        ins = nc.vector.max(top[:, q, :], logits[:, q, :])
                    step(ins, gap=True)
                    for q in range(G):
                        ins = nc.vector.max_index(at8[:, q, :], top[:, q, :], logits[:, q, :])
                    step(ins)
                    step(nc.vector.tensor_copy(atf[:, :], at8[:, :, 0]))
                    nc.vector.tensor_tensor(chosen[:, :, :], outer(count[:, :], G), inner(atf[:, :], E1), ALU.is_equal).then_inc(chosen_ready, 1)
                    dve.wait_ge(chosen_turned, n + 1)
                    dve.wait_ge(out_ready, n + 1)
                    step(nc.vector.tensor_copy(chosenT[:, :], ps[0:E1, 1024:1024 + GT]))
                    nc.vector.tensor_scalar(farT[:, :], chosenT[:, :], FAR, -FAR, ALU.mult, ALU.add).then_inc(far_ready, 1)
                    dve.wait_ge(out_ready, n + 2)
                    group = m.h[:, bass.ds(n * (G * D), G * D)]
                    nc.vector.scalar_tensor_tensor(group, ps[0:T, 3584:3584 + G * D], 0.0, group, ALU.max, ALU.add).then_inc(added, 1)
                step.end(NG // 2)


DG = 32
NGRP = D // DG
KC = T // 4


def pair_attention(nc, m, c):
    NP = G // 2
    NCH = T // KC
    with Layer(nc) as ctx:
        w = ctx.enter_context(nc.sbuf_tensor("pair_w_sb", [D, 3 * D], F32))
        mlp = ctx.enter_context(nc.sbuf_tensor("pair_mlp_sb", [128, 2 * NGRP], F32))
        b = ctx.enter_context(nc.sbuf_tensor("pair_b_sb", [T, 1], F32))
        qT = ctx.enter_context(nc.sbuf_tensor("pair_q", [128, NP, T], F32))
        kT = ctx.enter_context(nc.sbuf_tensor("pair_k", [128, NP, T], F32))
        v = ctx.enter_context(nc.sbuf_tensor("pair_v", [T, G, D], F32))
        diff = ctx.enter_context(nc.sbuf_tensor("pair_diff", [128, 2, KC * T], F32))
        scores = ctx.enter_context(nc.sbuf_tensor("pair_scores", [T, 2 * NGRP, T], F32))
        centre = ctx.enter_context(nc.sbuf_tensor("pair_centred_sb", [T, 2 * NGRP, T], F32))
        exps = ctx.enter_context(nc.sbuf_tensor("pair_exp", [T, 2 * NGRP, T], F32))
        probs = ctx.enter_context(nc.sbuf_tensor("pair_probs", [T, 2 * NGRP, T], F32))
        probsT = ctx.enter_context(nc.sbuf_tensor("pair_probsT", [T, 2 * NGRP * T], F32))
        small = ctx.enter_context(nc.sbuf_tensor("pair_small", [T, 3, 2 * NGRP], F32))
        weights = ctx.enter_context(nc.semaphore("pair_weights"))
        qk_ready = ctx.enter_context(nc.semaphore("pair_qk_ready"))
        qk_copied = ctx.enter_context(nc.semaphore("pair_qk_copied"))
        v_ready = ctx.enter_context(nc.semaphore("pair_v_ready"))
        v_copied = ctx.enter_context(nc.semaphore("pair_v_copied"))
        diff_ready = ctx.enter_context(nc.semaphore("pair_diff_ready"))
        relu_ready = ctx.enter_context(nc.semaphore("pair_relu_ready"))
        chunk_used = ctx.enter_context(nc.semaphore("pair_chunk_used"))
        scores_read = ctx.enter_context(nc.semaphore("pair_scores_read"))
        centre_ready = ctx.enter_context(nc.semaphore("pair_centre_ready"))
        exp_ready = ctx.enter_context(nc.semaphore("pair_exp_ready"))
        probs_ready = ctx.enter_context(nc.semaphore("pair_probs_ready"))
        probs_turned = ctx.enter_context(nc.semaphore("pair_probs_turned"))
        probsT_ready = ctx.enter_context(nc.semaphore("pair_probsT_ready"))
        out_ready = ctx.enter_context(nc.semaphore("pair_out_ready"))
        added = ctx.enter_context(nc.semaphore("pair_added"))
        steps = ctx.enter_context(nc.semaphore("pair_steps"))
        t = Turned(nc, m, ctx, "pair")
        block = ctx.block()
        ps = m.ps
        Q_BANK, K_BANK, V_BANK, S_BANK, T_BANK, O_BANK = 512, 1024, 1536, 2048, 3072, 3584

        @block.sync
        def _(sp):
            sp.dma_start(w[:, :], c["pair_w"]).then_inc(weights, 16)
            sp.dma_start(mlp[:, :], c["pair_mlp"]).then_inc(weights, 16)
            sp.dma_start(b[:, :], c["pair_b"].broadcast_to([T, 1])).then_inc(weights, 16)

        @block.gpsimd
        def _(pool):
            t.credits(pool)
            with pool.Fori(0, NG // 2) as i:
                for u in range(2):
                    t.copy_in(pool, i * 2 + u, u)

        @block.tensor
        def _(pe):
            pe.sem_inc(chunk_used, 2)
            pe.wait_ge(weights, 48)
            pe.wait_ge(t.ones_set, 1)
            with pe.Fori(0, NG // 2) as i:
                for u in range(2):
                    n = i * 2 + u
                    t.turn(pe, n, u)
                    pe.wait_ge(qk_copied, n + 1)
                    pe.wait_ge(v_copied, n + 1)
                    pe.sem_inc(t.gap, 1)
                    for q in range(G):
                        row, col = (q % 2) * D, (q // 2) * T
                        x = t.xT[0:D, u, q * T:(q + 1) * T]
                        nc.tensor.matmul(ps[row:row + D, Q_BANK + col:Q_BANK + col + T], w[:, 0:D], x, start=True, stop=True)
                        ins = nc.tensor.matmul(ps[row:row + D, K_BANK + col:K_BANK + col + T], w[:, D:2 * D], x, start=True, stop=True)
                    ins.then_inc(qk_ready, 1)
                    for q in range(G):
                        ins = nc.tensor.matmul(ps[0:T, V_BANK + q * D:V_BANK + (q + 1) * D], t.xT[0:D, u, q * T:(q + 1) * T], w[:, 2 * D:3 * D], start=True, stop=True)
                    ins.then_inc(v_ready, 1)
                    pe.wait_ge(v_ready, n + 1)
                    pe.sem_inc(t.x_used, 1)
                    for r in range(NP):
                        pe.wait_ge(scores_read, n * NP + r + 1)
                        for k in range(NCH):
                            at = (r * NCH + k) % 2
                            pe.wait_ge(relu_ready, n * (NP * NCH) + r * NCH + k + 1)
                            for j in range(KC):
                                col = S_BANK + 512 * r + (k * KC + j) * 2 * NGRP
                                ins = nc.tensor.matmul(ps[0:T, col:col + 2 * NGRP], diff[:, at, j * T:(j + 1) * T], mlp[:, :], start=True, stop=True)
                            ins.then_inc(chunk_used, 1)
                    for r in range(NP):
                        pe.wait_ge(probs_ready, n * NP + r + 1)
                        for a in range(2 * NGRP):
                            ins = nc.tensor.transpose(ps[0:T, T_BANK + a * T:T_BANK + (a + 1) * T], probs[:, a, :], m.ident[0:T, 0:T])
                        ins.then_inc(probs_turned, 1)
                        pe.wait_ge(probsT_ready, n * NP + r + 1)
                        pe.wait_ge(added, n * NP + r + 1)
                        for a in range(2 * NGRP):
                            s, g = a // NGRP, a % NGRP
                            ins = nc.tensor.matmul(ps[0:T, O_BANK + a * DG:O_BANK + (a + 1) * DG], probsT[:, a * T:(a + 1) * T], v[:, 2 * r + s, g * DG:(g + 1) * DG], start=True, stop=True)
                        ins.then_inc(out_ready, 1)

        @block.scalar
        def _(act):
            act.sem_inc(v_copied, 1)
            with act.Fori(0, NG // 2) as i:
                for u in range(2):
                    n = i * 2 + u
                    t.take_out(act, n, u)
                    act.wait_ge(v_ready, n + 1)
                    act.wait_ge(out_ready, n * NP + 1)
                    nc.scalar.activation(v[:, :, :], ps[0:T, V_BANK:V_BANK + G * D].rearrange("t (q d) -> t q d", d=D), ACT.Copy).then_inc(v_copied, 1)
                    for k in range(NP * NCH):
                        act.wait_ge(diff_ready, n * (NP * NCH) + k + 1)
                        nc.scalar.activation(diff[:, k % 2, :], diff[:, k % 2, :], ACT.Relu).then_inc(relu_ready, 1)
                    for r in range(NP):
                        act.wait_ge(centre_ready, n * NP + r + 1)
                        nc.scalar.activation(exps[:, :, :], centre[:, :, :], ACT.Exp).then_inc(exp_ready, 1)
                        act.wait_ge(probs_turned, n * NP + r + 2)
                        act.wait_ge(out_ready, n * NP + r + 1)
                        nc.scalar.activation(probsT[:, :], ps[0:T, T_BANK:T_BANK + 2 * NGRP * T], ACT.Copy).then_inc(probsT_ready, 1)

        @block.vector
        def _(dve):
            step = Chain(dve, steps)
            dve.sem_inc(qk_copied, 1)
            dve.sem_inc(scores_read, NP)
            dve.sem_inc(out_ready, 1)
            dve.sem_inc(probs_turned, 1)
            dve.sem_inc(added, 1)
            dve.wait_ge(weights, 48)
            N = 2 + 4 * NP
            with dve.Fori(0, NG // 2) as i:
                step.begin(i, 2 * N)
                for u in range(2):
                    n = i * 2 + u
                    dve.wait_ge(qk_ready, n + 1)
                    step(nc.vector.tensor_copy(qT[:, :, :], ps[:, Q_BANK:Q_BANK + NP * T].rearrange("p (r t) -> p r t", t=T)))
                    ins = nc.vector.tensor_copy(kT[:, :, :], ps[:, K_BANK:K_BANK + NP * T].rearrange("p (r t) -> p r t", t=T))
                    ins.then_inc(qk_copied, 1)
                    dve.wait_ge(qk_copied, n + 2)
                    for r in range(NP):
                        for k in range(NCH):
                            at = (r * NCH + k) % 2
                            dve.wait_ge(chunk_used, n * (NP * NCH) + r * NCH + k + 1)
                            nc.vector.tensor_tensor(diff[:, at, :].rearrange("p (k q) -> p k q", q=T), outer(qT[:, r, :], KC), inner(kT[:, r, k * KC:(k + 1) * KC], T), ALU.subtract).then_inc(diff_ready, 1)
                    for r in range(NP):
                        dve.wait_ge(chunk_used, n * (NP * NCH) + (r + 1) * NCH + 2)
                        ins = nc.vector.tensor_scalar(scores[:, :, :], ps[0:T, S_BANK + 512 * r:S_BANK + 512 * r + 2 * NGRP * T].rearrange("t (k a) -> t a k", a=2 * NGRP), b[:, 0:1], 0.0, ALU.add, ALU.max)
                        ins.then_inc(scores_read, 1)
                        dve.wait_ge(scores_read, n * NP + r + 1 + NP)
                        step(nc.vector.tensor_reduce(small[:, 0, :], scores[:, :, :], X, ALU.max))
                        nc.vector.tensor_tensor(centre[:, :, :], scores[:, :, :], inner(small[:, 0, :], T), ALU.subtract).then_inc(centre_ready, 1)
                        dve.wait_ge(exp_ready, n * NP + r + 1)
                        step(nc.vector.tensor_reduce(small[:, 1, :], exps[:, :, :], X, ALU.add))
                        step(nc.vector.reciprocal(small[:, 2, :], small[:, 1, :]))
                        dve.wait_ge(probs_turned, n * NP + r + 1)
                        nc.vector.tensor_tensor(probs[:, :, :], exps[:, :, :], inner(small[:, 2, :], T), ALU.mult).then_inc(probs_ready, 1)
                        dve.wait_ge(out_ready, n * NP + r + 2)
                        group = m.h[:, bass.ds((n * NP + r) * (2 * D), 2 * D)].rearrange("p (s d g) -> p s g d", s=2, g=NGRP)
                        ins = nc.vector.tensor_tensor(group, ps[0:T, O_BANK:O_BANK + 2 * D].rearrange("p (s g d) -> p s g d", s=2, g=NGRP), group, ALU.add)
                        ins.then_inc(added, 1)
                        step(nc.vector.memset(small[:, 0, :], 0.0))
                    step(nc.vector.memset(small[:, 1, :], 0.0))
                step.end(NG // 2)


E2 = 8


def gated_ffn(nc, m, c):
    with Layer(nc) as ctx:
        w1 = ctx.enter_context(nc.sbuf_tensor("gate_w1_sb", [D, HID], F32))
        b1 = ctx.enter_context(nc.sbuf_tensor("gate_b1_sb", [128, 2], F32))
        wg = ctx.enter_context(nc.sbuf_tensor("gate_wg_sb", [128, 2 * E2], F32))
        bg = ctx.enter_context(nc.sbuf_tensor("gate_bg_sb", [1, E2], F32))
        wd = ctx.enter_context(nc.sbuf_tensor("gate_wd_sb", [128, 2 * E2 * D], F32))
        bd = ctx.enter_context(nc.sbuf_tensor("gate_bd_sb", [1, E2 * D], F32))
        count = ctx.enter_context(nc.sbuf_tensor("gate_count_sb", [T, E2], F32))
        g = ctx.enter_context(nc.sbuf_tensor("gate_g", [128, 2, GT], F32))
        centre = ctx.enter_context(nc.sbuf_tensor("gate_centre", [T, G, E2], F32))
        exps = ctx.enter_context(nc.sbuf_tensor("gate_exp", [T, G, E2], F32))
        probs = ctx.enter_context(nc.sbuf_tensor("gate_probs", [T, G, E2], F32))
        top = ctx.enter_context(nc.sbuf_tensor("gate_top", [T, G, 8], F32))
        at8 = ctx.enter_context(nc.sbuf_tensor("gate_at", [T, G, 8], U32))
        atf = ctx.enter_context(nc.sbuf_tensor("gate_atf", [T, G], F32))
        small = ctx.enter_context(nc.sbuf_tensor("gate_small", [T, 3, G], F32))
        chosen = ctx.enter_context(nc.sbuf_tensor("gate_chosen", [T, G, E2], F32))
        prod = ctx.enter_context(nc.sbuf_tensor("gate_prod", [T, 2, E2 * D], F32))
        y = ctx.enter_context(nc.sbuf_tensor("gate_y", [T, G * D], F32))
        weights = ctx.enter_context(nc.semaphore("gate_weights"))
        hidden_ready = ctx.enter_context(nc.semaphore("gate_hidden_ready"))
        act_ready = ctx.enter_context(nc.semaphore("gate_act_ready"))
        rated = ctx.enter_context(nc.semaphore("gate_rated"))
        centre_ready = ctx.enter_context(nc.semaphore("gate_centre_ready"))
        exp_ready = ctx.enter_context(nc.semaphore("gate_exp_ready"))
        y_ready = ctx.enter_context(nc.semaphore("gate_y_ready"))
        y_read = ctx.enter_context(nc.semaphore("gate_y_read"))
        dve_gap = ctx.enter_context(nc.semaphore("gate_dve_gap"))
        steps = ctx.enter_context(nc.semaphore("gate_steps"))
        t = Turned(nc, m, ctx, "gate")
        block = ctx.block()
        ps = m.ps

        @block.sync
        def _(sp):
            for to, name in ((w1, "gate_w1"), (b1, "gate_b1"), (wg, "gate_wg"), (bg, "gate_bg"), (wd, "gate_wd"), (bd, "gate_bd")):
                sp.dma_start(to[:, :], c[name]).then_inc(weights, 16)
            sp.dma_start(count[:, :], c["count"][:, 0:E2].broadcast_to([T, E2])).then_inc(weights, 16)

        @block.gpsimd
        def _(pool):
            t.credits(pool)
            with pool.Fori(0, NG // 2) as i:
                for u in range(2):
                    t.copy_in(pool, i * 2 + u, u)

        @block.tensor
        def _(pe):
            pe.wait_ge(weights, 112)
            pe.wait_ge(t.ones_set, 1)
            with pe.Fori(0, NG // 2) as i:
                for u in range(2):
                    n = i * 2 + u
                    t.turn(pe, n, u)
                    pe.wait_ge(act_ready, n + 1)
                    for k in range(2):
                        ins = nc.tensor.matmul(ps[:, 512 * (1 + k):512 * (1 + k) + GT], w1[:, k * 128:(k + 1) * 128], t.xT[0:D, u, :], start=True, stop=True)
                    ins.then_inc(hidden_ready, 1)
                    pe.wait_ge(act_ready, n + 2)
                    pe.sem_inc(t.x_used, 1)
                    pe.wait_ge(centre_ready, n + 1)
                    for q in range(G):
                        out = ps[0:T, 1536 + q * E2:1536 + (q + 1) * E2]
                        for k in range(2):
                            nc.tensor.matmul(out, g[:, k, q * T:(q + 1) * T], wg[:, k * E2:(k + 1) * E2], start=(k == 0), stop=False)
                        ins = nc.tensor.matmul(out, m.ones[0:1, 0:T], bg[0:1, :], start=False, stop=True)
                    ins.then_inc(rated, 1)
                    for q in range(G):
                        pe.wait_ge(y_read, n * G + q + 1)
                        out = ps[0:T, 2048 + 512 * q:2048 + 512 * (q + 1)]
                        for k in range(2):
                            nc.tensor.matmul(out, g[:, k, q * T:(q + 1) * T], wd[:, k * E2 * D:(k + 1) * E2 * D], start=(k == 0), stop=False)
                        nc.tensor.matmul(out, m.ones[0:1, 0:T], bd[0:1, :], start=False, stop=True).then_inc(y_ready, 1)

        @block.scalar
        def _(act):
            act.sem_inc(act_ready, 1)
            act.wait_ge(weights, 112)
            with act.Fori(0, NG // 2) as i:
                for u in range(2):
                    n = i * 2 + u
                    t.take_out(act, n, u)
                    act.wait_ge(hidden_ready, n + 1)
                    act.wait_ge(y_ready, n * G + 1)
                    for k in range(2):
                        ins = nc.scalar.activation(g[:, k, :], ps[:, 512 * (1 + k):512 * (1 + k) + GT], ACT.Gelu, bias=b1[:, k:k + 1])
                    ins.then_inc(act_ready, 1)
                    act.wait_ge(centre_ready, n + 2)
                    nc.scalar.activation(exps[:, :, :], centre[:, :, :], ACT.Exp).then_inc(exp_ready, 1)

        @block.vector
        def _(dve):
            step = Chain(dve, steps, dve_gap)
            dve.sem_inc(centre_ready, 1)
            dve.sem_inc(y_ready, 1)
            dve.sem_inc(y_read, G)
            dve.wait_ge(weights, 112)
            N = 9 + G
            with dve.Fori(0, NG // 2) as i:
                step.begin(i, 2 * N)
                for u in range(2):
                    n = i * 2 + u
                    dve.wait_ge(rated, n + 1)
                    gates = ps[0:T, 1536:1536 + G * E2].rearrange("t (q e) -> t q e", e=E2)
                    step(nc.vector.tensor_reduce(small[:, 0, :], gates, X, ALU.max))
                    nc.vector.tensor_tensor(centre[:, :, :], gates, inner(small[:, 0, :], E2), ALU.subtract).then_inc(centre_ready, 1)
                    dve.wait_ge(exp_ready, n + 1)
                    step(nc.vector.tensor_reduce(small[:, 1, :], exps[:, :, :], X, ALU.add))
                    step(nc.vector.reciprocal(small[:, 2, :], small[:, 1, :]))
                    step(nc.vector.tensor_tensor(probs[:, :, :], exps[:, :, :], inner(small[:, 2, :], E2), ALU.mult), gap=True)
                    for q in range(G):
                        ins = nc.vector.max(top[:, q, :], probs[:, q, :])
                    step(ins, gap=True)
                    for q in range(G):
                        ins = nc.vector.max_index(at8[:, q, :], top[:, q, :], probs[:, q, :])
                    step(ins)
                    step(nc.vector.tensor_copy(atf[:, :], at8[:, :, 0]))
                    step(nc.vector.tensor_tensor(chosen[:, :, :], outer(count[:, :], G), inner(atf[:, :], E2), ALU.is_equal))
                    step(nc.vector.tensor_tensor(chosen[:, :, :], chosen[:, :, :], probs[:, :, :], ALU.mult))
                    for q in range(G):
                        dve.wait_ge(y_ready, n * G + q + 2)
                        ins = nc.vector.tensor_tensor(prod[:, q % 2, :].rearrange("t (e d) -> t e d", d=D), ps[0:T, 2048 + 512 * q:2048 + 512 * (q + 1)].rearrange("t (e d) -> t e d", d=D), inner(chosen[:, q, :], D), ALU.mult)
                        ins.then_inc(y_read, 1)
                        dve.wait_ge(y_read, n * G + q + 1 + G)
                        step(nc.vector.tensor_reduce(y[:, q * D:(q + 1) * D], prod[:, q % 2, :].rearrange("t (e d) -> t d e", d=D), X, ALU.add))
                    group = m.h[:, bass.ds(n * (G * D), G * D)]
                    nc.vector.tensor_tensor(group, group, y[:, :], ALU.add)
                step.end(NG // 2)


def top2_experts(nc, m, c):
    with Layer(nc) as ctx:
        wg = ctx.enter_context(nc.sbuf_tensor("moe_wg_sb", [D + 1, E2], F32))
        w1 = ctx.enter_context(nc.sbuf_tensor("moe_w1_sb", [D, E2 * HID], F32))
        b1 = ctx.enter_context(nc.sbuf_tensor("moe_b1_sb", [128, 2 * E2], F32))
        w2 = ctx.enter_context(nc.sbuf_tensor("moe_w2_sb", [128, 2 * E2 * D], F32))
        b2 = ctx.enter_context(nc.sbuf_tensor("moe_b2_sb", [1, E2 * D], F32))
        count = ctx.enter_context(nc.sbuf_tensor("moe_count_sb", [T, E2], F32))
        g = ctx.enter_context(nc.sbuf_tensor("moe_g", [128, 2, 2, GT], F32))
        gates = ctx.enter_context(nc.sbuf_tensor("moe_gates", [T, G, E2], F32))
        centre = ctx.enter_context(nc.sbuf_tensor("moe_centre", [T, G, E2], F32))
        exps = ctx.enter_context(nc.sbuf_tensor("moe_exp", [T, G, E2], F32))
        top = ctx.enter_context(nc.sbuf_tensor("moe_top", [T, G, 8], F32))
        at8 = ctx.enter_context(nc.sbuf_tensor("moe_at", [T, G, 8], U32))
        atf = ctx.enter_context(nc.sbuf_tensor("moe_atf", [T, G, 2], F32))
        first = ctx.enter_context(nc.sbuf_tensor("moe_first", [T, G, E2], F32))
        second = ctx.enter_context(nc.sbuf_tensor("moe_second", [T, G, E2], F32))
        small = ctx.enter_context(nc.sbuf_tensor("moe_small", [T, 2, G], F32))
        share = ctx.enter_context(nc.sbuf_tensor("moe_share", [T, G, E2], F32))
        prod = ctx.enter_context(nc.sbuf_tensor("moe_prod", [T, G * D], F32))
        acc = ctx.enter_context(nc.sbuf_tensor("moe_acc", [T, G * D], F32))
        weights = ctx.enter_context(nc.semaphore("moe_weights"))
        rated = ctx.enter_context(nc.semaphore("moe_rated"))
        gates_read = ctx.enter_context(nc.semaphore("moe_gates_read"))
        centre_ready = ctx.enter_context(nc.semaphore("moe_centre_ready"))
        exp_ready = ctx.enter_context(nc.semaphore("moe_exp_ready"))
        hidden_ready = ctx.enter_context(nc.semaphore("moe_hidden_ready"))
        act_ready = ctx.enter_context(nc.semaphore("moe_act_ready"))
        y_ready = ctx.enter_context(nc.semaphore("moe_y_ready"))
        y_read = ctx.enter_context(nc.semaphore("moe_y_read"))
        dve_gap = ctx.enter_context(nc.semaphore("moe_dve_gap"))
        steps = ctx.enter_context(nc.semaphore("moe_steps"))
        t = Turned(nc, m, ctx, "moe")
        block = ctx.block()
        ps = m.ps

        @block.sync
        def _(sp):
            for to, name in ((wg, "moe_wg"), (w1, "moe_w1"), (b1, "moe_b1"), (w2, "moe_w2"), (b2, "moe_b2")):
                sp.dma_start(to[:, :], c[name]).then_inc(weights, 16)
            sp.dma_start(count[:, :], c["count"][:, 0:E2].broadcast_to([T, E2])).then_inc(weights, 16)

        @block.gpsimd
        def _(pool):
            t.credits(pool)
            with pool.Fori(0, NG // 2) as i:
                for u in range(2):
                    t.copy_in(pool, i * 2 + u, u)

        @block.tensor
        def _(pe):
            def hidden(n, u, e):
                pe.wait_ge(act_ready, n * E2 + e + 1)
                for k in range(2):
                    at = 1024 + (e % 2) * 1024 + 512 * k
                    ins = nc.tensor.matmul(ps[:, at:at + GT], w1[:, e * HID + k * 128:e * HID + (k + 1) * 128], t.xT[0:D, u, :], start=True, stop=True)
                ins.then_inc(hidden_ready, 1)

            def output(n, u, e):
                pe.wait_ge(act_ready, n * E2 + e + 3)
                pe.wait_ge(y_read, n * E2 + e + 1)
                for q in range(G):
                    at = 3072 + 512 * (e % 2) + q * D
                    for k in range(2):
                        nc.tensor.matmul(ps[0:T, at:at + D], g[:, e % 2, k, q * T:(q + 1) * T], w2[:, (2 * e + k) * D:(2 * e + k + 1) * D], start=(k == 0), stop=False)
                    ins = nc.tensor.matmul(ps[0:T, at:at + D], m.ones[0:1, 0:T], b2[0:1, e * D:(e + 1) * D], start=False, stop=True)
                ins.then_inc(y_ready, 1)

            pe.wait_ge(weights, 96)
            pe.wait_ge(t.ones_set, 1)
            with pe.Fori(0, NG // 2) as i:
                for u in range(2):
                    n = i * 2 + u
                    t.turn(pe, n, u)
                    pe.wait_ge(gates_read, n + 1)
                    for q in range(G):
                        ins = nc.tensor.matmul(ps[0:T, 512 + q * E2:512 + (q + 1) * E2], t.columns(u, q), wg[:, :], start=True, stop=True)
                    ins.then_inc(rated, 1)
                    hidden(n, u, 0)
                    for e in range(E2):
                        if e + 1 < E2:
                            hidden(n, u, e + 1)
                        output(n, u, e)
                    pe.sem_inc(t.x_used, 1)

        @block.scalar
        def _(act):
            act.sem_inc(act_ready, 2)
            act.wait_ge(weights, 96)
            with act.Fori(0, NG // 2) as i:
                for u in range(2):
                    n = i * 2 + u
                    t.take_out(act, n, u)
                    act.wait_ge(centre_ready, n + 1)
                    nc.scalar.activation(exps[:, :, :], centre[:, :, :], ACT.Exp).then_inc(exp_ready, 1)
                    for e in range(E2):
                        act.wait_ge(hidden_ready, n * E2 + e + 1)
                        act.wait_ge(y_ready, n * E2 + e + 1)
                        for k in range(2):
                            at = 1024 + (e % 2) * 1024 + 512 * k
                            ins = nc.scalar.activation(g[:, e % 2, k, :], ps[:, at:at + GT], ACT.Gelu, bias=b1[:, 2 * e + k:2 * e + k + 1])
                        ins.then_inc(act_ready, 1)

        @block.vector
        def _(dve):
            step = Chain(dve, steps, dve_gap)
            dve.sem_inc(gates_read, 1)
            dve.sem_inc(y_ready, 2)
            dve.sem_inc(y_read, 2)
            dve.wait_ge(weights, 96)
            N = 10 + E2
            with dve.Fori(0, NG // 2) as i:
                step.begin(i, 2 * N)
                for u in range(2):
                    n = i * 2 + u
                    dve.wait_ge(rated, n + 1)
                    nc.vector.tensor_copy(gates[:, :, :], ps[0:T, 512:512 + G * E2].rearrange("t (q e) -> t q e", e=E2)).then_inc(gates_read, 1)
                    dve.wait_ge(gates_read, n + 2)
                    dve.sem_inc(dve_gap, 1)
                    for q in range(G):
                        ins = nc.vector.max(top[:, q, :], gates[:, q, :])
                    step(ins, gap=True)
                    nc.vector.tensor_tensor(centre[:, :, :], gates[:, :, :], inner(top[:, :, 0], E2), ALU.subtract).then_inc(centre_ready, 1)
                    for q in range(G):
                        ins = nc.vector.max_index(at8[:, q, :], top[:, q, :], gates[:, q, :])
                    step(ins)
                    step(nc.vector.tensor_copy(atf[:, :, :], at8[:, :, 0:2]))
                    nc.vector.tensor_tensor(first[:, :, :], outer(count[:, :], G), inner(atf[:, :, 0], E2), ALU.is_equal)
                    step(nc.vector.tensor_tensor(second[:, :, :], outer(count[:, :], G), inner(atf[:, :, 1], E2), ALU.is_equal))
                    step(nc.vector.tensor_tensor(first[:, :, :], first[:, :, :], second[:, :, :], ALU.add))
                    dve.wait_ge(exp_ready, n + 1)
                    step(nc.vector.tensor_tensor(first[:, :, :], first[:, :, :], exps[:, :, :], ALU.mult))
                    step(nc.vector.tensor_reduce(small[:, 0, :], first[:, :, :], X, ALU.add))
                    step(nc.vector.reciprocal(small[:, 1, :], small[:, 0, :]))
                    step(nc.vector.tensor_tensor(share[:, :, :], first[:, :, :], inner(small[:, 1, :], E2), ALU.mult))
                    for e in range(E2):
                        dve.wait_ge(y_ready, n * E2 + e + 3)
                        v = ps[0:T, 3072 + 512 * (e % 2):3072 + 512 * (e % 2) + G * D].rearrange("t (q d) -> t q d", d=D)
                        to = acc if e == 0 else prod
                        ins = nc.vector.tensor_tensor(to[:, :].rearrange("t (q d) -> t q d", d=D), v, inner(share[:, :, e], D), ALU.mult)
                        ins.then_inc(y_read, 1)
                        dve.wait_ge(y_read, n * E2 + e + 3)
                        if e:
                            step(nc.vector.tensor_tensor(acc[:, :], acc[:, :], prod[:, :], ALU.add))
                    group = m.h[:, bass.ds(n * (G * D), G * D)]
                    step(nc.vector.tensor_tensor(group, group, acc[:, :], ALU.add))
                    step(nc.vector.memset(prod[:, 0:1], 0.0))
                step.end(NG // 2)


BR = 4
KM = 15
KS = 16
REL = KM + 2
NS = BR * T
SB = 7
NB = 56
NBR = -(-NS // SB)
SP_ = NB * SB
RB_ = SB * REL
CB = SB * KM
SUP = 4
SW = SUP * CB
PH = 16
RH = 64
SILU = float(np.pi / np.sqrt(3.0))
MASKED = -1.0e30
CUT = [(0, 31), (31, 62), (62, 92)]
OC = 7


def palette_attention(nc, m, c):
    with Layer(nc) as ctx:
        w = ctx.enter_context(nc.sbuf_tensor("pal_w_sb", [D, (BR + 1) * D], F32))
        turn = ctx.enter_context(nc.sbuf_tensor("pal_turn_sb", [T, 2 * D], F32))
        causal = ctx.enter_context(nc.sbuf_tensor("pal_causal_sb", [T, T], F32))
        shift = ctx.enter_context(nc.sbuf_tensor("pal_shift_sb", [T, KS], F32))
        age = ctx.enter_context(nc.sbuf_tensor("pal_age_sb", [T, NS], F32))
        key = ctx.enter_context(nc.sbuf_tensor("pal_key_sb", [T, 1], F32))
        pick = ctx.enter_context(nc.sbuf_tensor("pal_pick_sb", [BR * KS, KM], F32))
        rowsf = ctx.enter_context(nc.sbuf_tensor("pal_rows_sb", [BR * KS, BR * T], F32))
        rows = ctx.enter_context(nc.sbuf_tensor("pal_rows16", [BR * KS, BR * T], BF16))
        own = ctx.enter_context(nc.sbuf_tensor("pal_own_sb", [RB_, SW], F32))
        w1 = ctx.enter_context(nc.sbuf_tensor("pal_w1_sb", [RB_, RH], F32))
        b1 = ctx.enter_context(nc.sbuf_tensor("pal_b1_sb", [128, 1], F32))
        b1s = ctx.enter_context(nc.sbuf_tensor("pal_b1s", [128, 1], F32))
        w2T = ctx.enter_context(nc.sbuf_tensor("pal_w2T_sb", [RH, RH], F32))
        b2 = ctx.enter_context(nc.sbuf_tensor("pal_b2_sb", [RH, CB], F32))
        wcm = ctx.enter_context(nc.sbuf_tensor("pal_wcm_sb", [RH, 3], F32))
        bcm = ctx.enter_context(nc.sbuf_tensor("pal_bcm_sb", [CB, 3], F32))
        heads = ctx.enter_context(nc.sbuf_tensor("pal_heads", [128, 6], F32))
        hbias = ctx.enter_context(nc.sbuf_tensor("pal_hbias", [CB, 3], F32))
        soft = ctx.enter_context(nc.sbuf_tensor("pal_soft_sb", [NB, CB], F32))
        grid = ctx.enter_context(nc.sbuf_tensor("pal_grid_sb", [CB, PH], F32))
        site = ctx.enter_context(nc.sbuf_tensor("pal_site_sb", [CB, SB], F32))
        palette = ctx.enter_context(nc.sbuf_tensor("pal_palette_sb", [128, 2 * D], F32))
        wo = ctx.enter_context(nc.sbuf_tensor("pal_wo_sb", [D, BR * D], F32))
        x = ctx.enter_context(nc.sbuf_tensor("pal_x", [T, D], F32))
        xT = ctx.enter_context(nc.sbuf_tensor("pal_xT", [D, T], F32))
        ta = ctx.enter_context(nc.sbuf_tensor("pal_ta", [T, BR + 1, D], F32))
        tb = ctx.enter_context(nc.sbuf_tensor("pal_tb", [T, BR + 1, D], F32))
        ip = ctx.enter_context(nc.sbuf_tensor("pal_ip", [T, 2, (BR + 1) * D], F32))
        n2 = ctx.enter_context(nc.sbuf_tensor("pal_n2", [T, 4, BR + 1], F32))
        ipT = ctx.enter_context(nc.sbuf_tensor("pal_ipT", [D, 2, (BR + 1) * T], F32))
        logits = ctx.enter_context(nc.sbuf_tensor("pal_logits", [T, BR, T], F32))
        gram = ctx.enter_context(nc.sbuf_tensor("pal_gram", [T, T], F32))
        top = ctx.enter_context(nc.sbuf_tensor("pal_top", [T, BR, KS], F32))
        at = ctx.enter_context(nc.sbuf_tensor("pal_at", [T, BR, KS], U32))
        atf = ctx.enter_context(nc.sbuf_tensor("pal_atf", [T, BR, KS], F32))
        spread = ctx.enter_context(nc.sbuf_tensor("pal_spread", [BR * KS, T * KM], BF16))
        onehot = ctx.enter_context(nc.sbuf_tensor("pal_onehot", [T, SP_ * KM], F32))
        rext = ctx.enter_context(nc.sbuf_tensor("pal_rext", [T, SP_, REL], F32))
        rel = ctx.enter_context(nc.sbuf_tensor("pal_rel", [RB_, 2, SW], F32))
        hid = ctx.enter_context(nc.sbuf_tensor("pal_act", [128, 2, SW], F32))
        z = ctx.enter_context(nc.sbuf_tensor("pal_z", [CB, 2, NB], F32))
        g = ctx.enter_context(nc.sbuf_tensor("pal_g", [CB, 2, NB], F32))
        mix = ctx.enter_context(nc.sbuf_tensor("pal_mix", [CB, NB], F32))
        mixT = ctx.enter_context(nc.sbuf_tensor("pal_mixT", [NB, 4, CB], F32))
        msum = ctx.enter_context(nc.sbuf_tensor("pal_msum", [NB, 3, SB], F32))
        hat = ctx.enter_context(nc.sbuf_tensor("pal_hat", [CB, 2, NB * PH], F32))
        places = ctx.enter_context(nc.sbuf_tensor("pal_places", [CB, 2, OC * PH * PH], F32))
        a = ctx.enter_context(nc.sbuf_tensor("pal_a", [128, 2, NS], F32))
        vT = ctx.enter_context(nc.sbuf_tensor("pal_vT", [D, NS], F32))
        def sem(name):
            return ctx.enter_context(nc.semaphore("pal_" + name))

        weights, set_up, zeroed = sem("weights"), sem("set_up"), sem("zeroed")
        x_staged, x_turned, xT_ready = sem("x_staged"), sem("x_turned"), sem("xT_ready")
        ip_made, ip_squared, n_ready, ip_ready = sem("ip_made"), sem("ip_squared"), sem("n_ready"), sem("ip_ready")
        ip_turned, ipT_ready, products = sem("ip_turned"), sem("ipT_ready"), sem("products")
        products_read, at_ready, at_turned, spread_ready = sem("products_read"), sem("at_ready"), sem("at_turned"), sem("spread_ready")
        keys_spread, onehot_ready, gathered, rext_ready = sem("keys_spread"), sem("onehot_ready"), sem("gathered"), sem("rext_ready")
        related, rel_ready, hidden_ready, act_ready = sem("related"), sem("rel_ready"), sem("hidden_ready"), sem("act_ready")
        placed, z_ready, mix_ready, mix_turned = sem("placed"), sem("z_ready"), sem("mix_ready"), sem("mix_turned")
        mix_centred, mix_exp, shares_ready, shares_turned = sem("mix_centred"), sem("mix_exp"), sem("shares_ready"), sem("shares_turned")
        away, hat_ready, places_ready, places_used = sem("away"), sem("hat_ready"), sem("places_ready"), sem("places_used")
        a_ready, a_copied, v_ready, vT_ready, y_ready, added = sem("a_ready"), sem("a_copied"), sem("v_ready"), sem("vT_ready"), sem("y_ready"), sem("added")
        g_ready, steps, dve_gap, pe_gap = sem("g_ready"), sem("steps"), sem("dve_gap"), sem("pe_gap")
        block = ctx.block()
        ps = m.ps
        BANK = [512 * k for k in range(8)]
        NCUT = BR * len(CUT)
        NSUP = NB // SUP
        NOC = -(-NBR // OC)
        loads = [(w, "pal_w"), (turn, "pal_turn"), (causal, "pal_causal"), (shift, "pal_shift"), (age, "pal_age"),
                 (key, "pal_key"), (pick, "pal_pick"), (rowsf, "pal_rows"), (own, "pal_own"), (w1, "pal_w1"),
                 (b1, "pal_b1"), (w2T, "pal_w2T"), (b2, "pal_b2"), (wcm, "pal_wcm"), (bcm, "pal_bcm"),
                 (soft, "pal_soft"), (grid, "pal_grid"), (site, "pal_site"), (palette, "pal_palette"), (wo, "pal_wo")]
        LOADED = 16 * len(loads)

        def sites(r, cut):
            lo, hi = r * T + cut[0], r * T + cut[1]
            return lo, hi, lo * KM, hi * KM

        @block.sync
        def _(sp):
            for to, name in loads:
                sp.dma_start(to[:, :], c[name]).then_inc(weights, 16)

        @block.tensor
        def _(pe):
            pe.wait_ge(weights, LOADED)
            nc.tensor.matmul(ps[0:RH, BANK[0]:BANK[0] + 3], w2T[:, :], wcm[:, :], start=True, stop=True)
            nc.tensor.matmul(ps[RH:128, BANK[0]:BANK[0] + 3], w2T[:, :], wcm[:, :], start=True, stop=True)
            nc.tensor.matmul(ps[0:CB, BANK[1]:BANK[1] + 3], b2[:, :], wcm[:, :], start=True, stop=True).then_inc(set_up, 1)
            pe.wait_ge(zeroed, 1)
            with pe.Fori(0, B) as n:
                pe.wait_ge(x_staged, n + 1)
                pe.sem_inc(pe_gap, 1)
                nc.tensor.transpose(ps[0:D, BANK[0]:BANK[0] + T], x[:, :], m.ident[0:T, 0:T]).then_inc(x_turned, 1)
                pe.wait_ge(xT_ready, n + 1)
                nc.tensor.matmul(ps[0:T, BANK[1]:BANK[1] + (BR + 1) * D], xT[:, :], w[:, :], start=True, stop=True).then_inc(ip_made, 1)
                pe.wait_ge(ip_ready, n + 1)
                pe.sem_inc(pe_gap, 1)
                for k in range(2):
                    for r in range(BR + 1):
                        ins = nc.tensor.transpose(ps[0:D, BANK[k] + r * T:BANK[k] + (r + 1) * T], ip[:, k, r * D:(r + 1) * D], m.ident[0:T, 0:T])
                ins.then_inc(ip_turned, 1)
                pe.wait_ge(ipT_ready, n + 1)
                for r in range(BR):
                    nc.tensor.matmul(ps[0:T, BANK[0] + r * T:BANK[0] + (r + 1) * T], ipT[:, 0, r * T:(r + 1) * T], ipT[:, 0, BR * T:], start=True, stop=True)
                nc.tensor.matmul(ps[0:T, BANK[1]:BANK[1] + (BR + 1) * T], ipT[:, 1, BR * T:], ipT[:, 1, :], start=True, stop=True).then_inc(products, 1)
                pe.wait_ge(at_ready, n + 1)
                pe.sem_inc(pe_gap, 1)
                nc.tensor.transpose(ps[0:BR * KS, BANK[0]:BANK[0] + T], atf[:, :, :].rearrange("t r k -> t (r k)"), m.ident[0:T, 0:T]).then_inc(at_turned, 1)
                pe.wait_ge(spread_ready, n + 1)

                def spread_keys(j):
                    lo, hi = CUT[j % 3]
                    if j >= 2:
                        pe.wait_ge(onehot_ready, n * NCUT + j - 1)
                    nc.tensor.matmul(ps[0:T, BANK[2 + j % 2]:BANK[2 + j % 2] + (hi - lo) * KM], rows[:, (j // 3) * T:(j // 3 + 1) * T], spread[:, lo * KM:hi * KM], start=True, stop=True).then_inc(keys_spread, 1)

                def gather(j):
                    _, _, a0, b0 = sites(j // 3, CUT[j % 3])
                    pe.wait_ge(onehot_ready, n * NCUT + j + 1)
                    if j >= 2:
                        pe.wait_ge(rext_ready, n * NCUT + j - 1)
                    nc.tensor.matmul(ps[0:T, BANK[4 + j % 2]:BANK[4 + j % 2] + b0 - a0], gram[:, :], onehot[:, a0:b0], start=True, stop=True).then_inc(gathered, 1)

                spread_keys(0)
                for j in range(NCUT):
                    if j + 1 < NCUT:
                        spread_keys(j + 1)
                    gather(j)
                pe.wait_ge(rext_ready, (n + 1) * NCUT)

                def relate(s):
                    if s >= 2:
                        pe.wait_ge(rel_ready, n * NSUP + s - 1)
                    for k in range(SUP):
                        b = s * SUP + k
                        ins = nc.tensor.matmul(ps[0:RB_, BANK[6 + s % 2] + k * CB:BANK[6 + s % 2] + (k + 1) * CB], rext[:, b * SB:(b + 1) * SB, :].rearrange("t s f -> t (s f)"), onehot[:, b * CB:(b + 1) * CB], start=True, stop=True)
                    ins.then_inc(related, 1)

                def hidden(s):
                    pe.wait_ge(rel_ready, n * NSUP + s + 1)
                    pair, half = s // 2, s % 2
                    if s >= 4 and half == 0:
                        pe.wait_ge(act_ready, n * (NSUP // 2) + pair - 1)
                    pe.sem_inc(pe_gap, 1)
                    nc.tensor.matmul(ps[half * RH:(half + 1) * RH, BANK[4 + pair % 2]:BANK[4 + pair % 2] + SW], w1[:, :], rel[:, s % 2, :], start=True, stop=True).then_inc(hidden_ready, 1)

                def place(pair):
                    pe.wait_ge(act_ready, n * (NSUP // 2) + pair + 1)
                    for k in range(SUP):
                        at_ = BANK[3] + (pair * SUP + k) * 6
                        ins = nc.tensor.matmul(ps[0:CB, at_:at_ + 6], hid[:, pair % 2, k * CB:(k + 1) * CB], heads[:, :], start=True, stop=True)
                    ins.then_inc(placed, 1)

                relate(0)
                for s in range(NSUP):
                    if s + 1 < NSUP:
                        relate(s + 1)
                    hidden(s)
                    if s % 2 == 1 and s >= 3:
                        place(s // 2 - 1)
                place(NSUP // 2 - 1)
                pe.wait_ge(mix_ready, n + 1)
                pe.sem_inc(pe_gap, 1)
                nc.tensor.transpose(ps[0:NB, BANK[0]:BANK[0] + CB], mix[:, :], m.ident[0:CB, 0:CB]).then_inc(mix_turned, 1)
                pe.wait_ge(shares_ready, n + 1)
                pe.sem_inc(pe_gap, 1)
                nc.tensor.transpose(ps[0:CB, BANK[1]:BANK[1] + NB], mixT[:, 3, :], m.ident[0:NB, 0:NB]).then_inc(shares_turned, 1)
                for k in range(NOC):
                    pe.wait_ge(places_ready, n * NOC + k + 1)
                    nb = min(OC, NBR - k * OC)
                    for j in range(nb):
                        b = k * OC + j
                        for half in range(2):
                            ins = nc.tensor.matmul(ps[:, BANK[4 + half] + b * SB:BANK[4 + half] + (b + 1) * SB], places[:, k % 2, j * PH * PH + half * 128:j * PH * PH + (half + 1) * 128], site[:, :], start=True, stop=True)
                    ins.then_inc(places_used, 1)
                pe.wait_ge(a_copied, n + 1)
                for half in range(2):
                    ins = nc.tensor.matmul(ps[0:D, BANK[6]:BANK[6] + NS], palette[:, half * D:(half + 1) * D], a[:, half, :], start=(half == 0), stop=(half == 1))
                ins.then_inc(v_ready, 1)
                pe.wait_ge(vT_ready, n + 1)
                for r in range(BR):
                    ins = nc.tensor.matmul(ps[0:T, BANK[7]:BANK[7] + D], vT[:, r * T:(r + 1) * T], wo[:, r * D:(r + 1) * D], start=(r == 0), stop=(r == BR - 1))
                ins.then_inc(y_ready, 1)
                pe.wait_ge(added, n + 1)

        @block.scalar
        def _(act):
            act.wait_ge(weights, LOADED)
            nc.scalar.activation(b1s[:, :], b1[:, :], ACT.Copy, scale=SILU).then_inc(set_up, 1)
            act.wait_ge(set_up, 3)
            with act.Fori(0, B) as n:
                nc.scalar.activation(x[:, :], m.xn[:, bass.ds(n * D, D)], ACT.Copy).then_inc(x_staged, 1)
                act.wait_ge(x_turned, n + 1)
                nc.scalar.activation(xT[:, :], ps[0:D, BANK[0]:BANK[0] + T], ACT.Copy).then_inc(xT_ready, 1)
                act.wait_ge(ip_squared, n + 1)
                nc.scalar.activation(n2[:, 1, :], n2[:, 0, :], ACT.Sqrt).then_inc(n_ready, 1)
                act.wait_ge(ip_turned, n + 1)
                for k in range(2):
                    ins = nc.scalar.activation(ipT[:, k, :], ps[0:D, BANK[k]:BANK[k] + (BR + 1) * T], ACT.Copy)
                ins.then_inc(ipT_ready, 1)
                for j in range(NCUT):
                    lo, hi, a0, b0 = sites(j // 3, CUT[j % 3])
                    act.wait_ge(gathered, n * NCUT + j + 1)
                    nc.scalar.activation(rext[:, lo:hi, 0:KM], ps[0:T, BANK[4 + j % 2]:BANK[4 + j % 2] + b0 - a0].rearrange("t (s k) -> t s k", k=KM), ACT.Copy).then_inc(rext_ready, 1)
                for pair in range(NSUP // 2):
                    act.wait_ge(hidden_ready, n * NSUP + 2 * pair + 2)
                    if pair >= 2:
                        act.wait_ge(placed, n * (NSUP // 2) + pair - 1)
                    nc.scalar.activation(hid[:, pair % 2, :], ps[:, BANK[4 + pair % 2]:BANK[4 + pair % 2] + SW], ACT.Silu, bias=b1s[:, 0:1], scale=SILU).then_inc(act_ready, 1)
                act.wait_ge(placed, (n + 1) * (NSUP // 2))
                out = ps[0:CB, BANK[3]:BANK[3] + NB * 3].rearrange("p (q k h c) -> p c q h k", k=SUP, h=2, c=3)
                for k in range(2):
                    ins = nc.scalar.activation(z[:, k, :].rearrange("p (q h k) -> p q h k", h=2, k=SUP), out[:, k], ACT.Tanh, bias=hbias[:, k:k + 1])
                nc.scalar.activation(mix[:, :].rearrange("p (q h k) -> p q h k", h=2, k=SUP), out[:, 2], ACT.Identity, bias=hbias[:, 2:3]).then_inc(mix_ready, 1)
                act.wait_ge(mix_ready, n + 1)
                act.sem_inc(z_ready, 1)
                act.wait_ge(mix_centred, n + 1)
                nc.scalar.activation(mixT[:, 2, :], mixT[:, 1, :], ACT.Exp).then_inc(mix_exp, 1)
                act.wait_ge(away, n + 1)
                nc.scalar.activation(hat[:, :, :], hat[:, :, :], ACT.Abs).then_inc(hat_ready, 1)
                act.wait_ge(hat_ready, 2 * n + 1)
                nc.scalar.activation(hat[:, :, :], hat[:, :, :], ACT.Relu, bias=1.0, scale=-1.0).then_inc(hat_ready, 1)
                act.wait_ge(places_used, (n + 1) * NOC)
                for half in range(2):
                    ins = nc.scalar.activation(a[:, half, :], ps[:, BANK[4 + half]:BANK[4 + half] + NS], ACT.Copy)
                ins.then_inc(a_copied, 1)
                act.wait_ge(v_ready, n + 1)
                nc.scalar.activation(vT[:, :], ps[0:D, BANK[6]:BANK[6] + NS], ACT.Copy).then_inc(vT_ready, 1)

        @block.vector
        def _(dve):
            step = Chain(dve, steps, dve_gap)
            dve.wait_ge(weights, LOADED)
            dve.wait_ge(set_up, 2)
            nc.vector.memset(onehot[:, :], 0.0)
            nc.vector.memset(rext[:, :, :], 0.0)
            nc.vector.memset(heads[:, :], 0.0)
            step(nc.vector.tensor_copy(rows[:, :], rowsf[:, :]))
            nc.vector.tensor_copy(rext[:, 0:NS, KM + 1], age[:, :])
            for half in range(2):
                nc.vector.tensor_scalar(heads[half * RH:(half + 1) * RH, 3 * half:3 * half + 3], ps[half * RH:(half + 1) * RH, BANK[0]:BANK[0] + 3], 1.0 / SILU, None, ALU.mult)
            nc.vector.tensor_tensor(hbias[:, :], ps[0:CB, BANK[1]:BANK[1] + 3], bcm[:, :], ALU.add).then_inc(set_up, 1)
            dve.wait_ge(set_up, 3)
            step(nc.vector.memset(n2[:, 3, :], 0.0))
            dve.sem_inc(zeroed, 1)
            H = D // 2
            N = 20
            with dve.Fori(0, B) as n:
                step.begin(n, N)
                dve.wait_ge(ip_made, n + 1)
                src = ps[0:T, BANK[1]:BANK[1] + (BR + 1) * D].rearrange("t (r d) -> t r d", d=D)
                rotated = ip[:, 0, :].rearrange("t (r d) -> t r d", d=D)
                unit = ip[:, 1, :].rearrange("t (r d) -> t r d", d=D)
                cos2, sin = turn[:, 0:D], turn[:, D:D + H]
                nc.vector.tensor_tensor(ta[:, :, :], src, outer(cos2, BR + 1), ALU.mult)
                nc.vector.tensor_tensor(tb[:, :, 0:H], src[:, :, H:D], outer(sin, BR + 1), ALU.mult)
                step(nc.vector.tensor_tensor(tb[:, :, H:D], src[:, :, 0:H], outer(sin, BR + 1), ALU.mult))
                nc.vector.tensor_tensor(rotated[:, :, 0:H], ta[:, :, 0:H], tb[:, :, 0:H], ALU.subtract)
                step(nc.vector.tensor_tensor(rotated[:, :, H:D], ta[:, :, H:D], tb[:, :, H:D], ALU.add))
                step(nc.vector.tensor_tensor(ta[:, :, :], rotated, rotated, ALU.mult))
                nc.vector.tensor_reduce(n2[:, 0, :], ta[:, :, :], X, ALU.add).then_inc(ip_squared, 1)
                dve.wait_ge(n_ready, n + 1)
                step(nc.vector.tensor_scalar(n2[:, 2, :], n2[:, 1, :], 1e-12, None, ALU.max))
                step(nc.vector.reciprocal(n2[:, 3, :], n2[:, 2, :]))
                nc.vector.tensor_tensor(unit, rotated, inner(n2[:, 3, :], D), ALU.mult).then_inc(ip_ready, 1)
                dve.wait_ge(products, n + 1)
                step(nc.vector.scalar_tensor_tensor(logits[:, :, :], ps[0:T, BANK[0]:BANK[0] + BR * T].rearrange("t (r s) -> t r s", s=T), D ** -0.5, outer(causal[:, :], BR), ALU.mult, ALU.add), gap=True)
                nc.vector.tensor_scalar(rext[:, 0:NS, KM], ps[0:T, BANK[1]:BANK[1] + NS], 1.0, -1.0, ALU.min, ALU.max)
                step(nc.vector.tensor_scalar(gram[:, :], ps[0:T, BANK[1] + NS:BANK[1] + NS + T], 1.0, -1.0, ALU.min, ALU.max), gap=True)
                for r in range(BR):
                    ins = nc.vector.max(top[:, r, 0:8], logits[:, r, :])
                step(ins, gap=True)
                for r in range(BR):
                    ins = nc.vector.max_index(at[:, r, 0:8], top[:, r, 0:8], logits[:, r, :])
                step(ins, gap=True)
                for r in range(BR):
                    ins = nc.vector.match_replace(logits[:, r, :], top[:, r, 0:8], logits[:, r, :], GONE)
                step(ins, gap=True)
                for r in range(BR):
                    ins = nc.vector.max(top[:, r, 8:16], logits[:, r, :])
                step(ins, gap=True)
                for r in range(BR):
                    ins = nc.vector.max_index(at[:, r, 8:16], top[:, r, 8:16], logits[:, r, :])
                step(ins)
                step(nc.vector.tensor_copy(atf[:, :, :], at[:, :, :]))
                nc.vector.tensor_tensor(atf[:, :, :], atf[:, :, :], outer(shift[:, :], BR), ALU.add).then_inc(at_ready, 1)
                dve.wait_ge(at_turned, n + 1)
                nc.vector.tensor_tensor(spread[:, :].rearrange("r (t k) -> r t k", k=KM), inner(ps[0:BR * KS, BANK[0]:BANK[0] + T], KM), outer(pick[:, :], T), ALU.mult).then_inc(spread_ready, 1)
                for j in range(NCUT):
                    _, _, a0, b0 = sites(j // 3, CUT[j % 3])
                    dve.wait_ge(keys_spread, n * NCUT + j + 1)
                    nc.vector.tensor_scalar(onehot[:, a0:b0], ps[0:T, BANK[2 + j % 2]:BANK[2 + j % 2] + b0 - a0], key[:, 0:1], None, ALU.is_equal).then_inc(onehot_ready, 1)
                for s in range(NSUP):
                    dve.wait_ge(related, n * NSUP + s + 1)
                    if s >= 2:
                        dve.wait_ge(hidden_ready, n * NSUP + s - 1)
                    nc.vector.tensor_tensor(rel[:, s % 2, :], ps[0:RB_, BANK[6 + s % 2]:BANK[6 + s % 2] + SW], own[:, :], ALU.mult).then_inc(rel_ready, 1)
                dve.wait_ge(z_ready, n + 1)
                step(nc.vector.tensor_scalar(g[:, :, :], z[:, :, :], 1.0, 0.5 * (PH - 1), ALU.add, ALU.mult))
                step(nc.vector.tensor_scalar(g[:, :, :], g[:, :, :], 0.0, PH - 1.0, ALU.max, ALU.min))
                nc.vector.tensor_tensor(hat[:, :, :].rearrange("p w (b v) -> p (w b) v", v=PH), inner(g[:, :, :].rearrange("p w b -> p (w b)"), PH), outer(grid[:, :], 2 * NB), ALU.subtract).then_inc(away, 1)
                dve.wait_ge(mix_turned, n + 1)
                per = lambda v: v.rearrange("b (s k) -> b s k", k=KM)
                step(nc.vector.tensor_tensor(mixT[:, 0, :], ps[0:NB, BANK[0]:BANK[0] + CB], soft[:, :], ALU.add))
                step(nc.vector.tensor_reduce(msum[:, 0, :], per(mixT[:, 0, :]), X, ALU.max))
                nc.vector.tensor_tensor(per(mixT[:, 1, :]), per(mixT[:, 0, :]), inner(msum[:, 0, :], KM), ALU.subtract).then_inc(mix_centred, 1)
                dve.wait_ge(mix_exp, n + 1)
                step(nc.vector.tensor_reduce(msum[:, 1, :], per(mixT[:, 2, :]), X, ALU.add))
                step(nc.vector.reciprocal(msum[:, 2, :], msum[:, 1, :]))
                nc.vector.tensor_tensor(per(mixT[:, 3, :]), per(mixT[:, 2, :]), inner(msum[:, 2, :], KM), ALU.mult).then_inc(shares_ready, 1)
                dve.wait_ge(shares_turned, n + 1)
                dve.wait_ge(hat_ready, 2 * n + 2)
                hats = hat[:, :, :].rearrange("p w (b v) -> p w b v", v=PH)
                step(nc.vector.tensor_tensor(hats[:, 1], hats[:, 1], inner(ps[0:CB, BANK[1]:BANK[1] + NB], PH), ALU.mult))
                for k in range(NOC):
                    nb = min(OC, NBR - k * OC)
                    if k >= 2:
                        dve.wait_ge(places_used, n * NOC + k - 1)
                    to = places[:, k % 2, 0:nb * PH * PH].rearrange("p (b y x) -> p b y x", y=PH, x=PH)
                    nc.vector.tensor_tensor(to, inner(hats[:, 1, k * OC:k * OC + nb], PH), outer(hats[:, 0, k * OC:k * OC + nb], PH, 2), ALU.mult).then_inc(places_ready, 1)
                dve.wait_ge(y_ready, n + 1)
                group = m.h[:, bass.ds(n * D, D)]
                nc.vector.scalar_tensor_tensor(group, ps[0:T, BANK[7]:BANK[7] + D], 1.0 / BR, group, ALU.mult, ALU.add).then_inc(added, 1)
                dve.wait_ge(added, n + 1)
                step.end(B)


class Memory:
    pass


def program(nc, c, out):
    with ExitStack() as ctx:
        h = ctx.enter_context(nc.sbuf_tensor("h", [T, F], F32))
        xn = ctx.enter_context(nc.sbuf_tensor("xn", [T, F + D], F32))
        ident = ctx.enter_context(nc.sbuf_tensor("ident", [128, 128], F32))
        ones = ctx.enter_context(nc.sbuf_tensor("ones", [1, 512], F32))
        ps = ctx.enter_context(nc.psum_tensor("ps", [128, 4096], F32))
        m = Memory()
        m.h, m.ident, m.ones, m.ps, m.xn = h, ident, ones, ps, xn
        tokens(nc, m, c)
        layer_norm(nc, m, m.h[:, :], m.h[:, :], "tok_ln", c["tok_gamma"], c["tok_beta"])
        shifted = xn[:, D:D + F]
        layer_norm(nc, m, h[:, :], shifted, "fw_ln")
        add_in(nc, h[:, :], shifted, "fw_skip")
        layer_norm(nc, m, shifted, shifted, "fw_ln2", c["fw_gain"], c["fw_shift"])
        fast_weights(nc, m, c)
        layer_norm(nc, m, h[:, :], xn[:, 0:F], "mod_ln")
        depth_ffn(nc, m, c)
        layer_norm(nc, m, h[:, :], xn[:, 0:F], "win_ln")
        window_attention(nc, m, c)
        layer_norm(nc, m, h[:, :], xn[:, 0:F], "top1_ln")
        top1_experts(nc, m, c)
        layer_norm(nc, m, h[:, :], xn[:, 0:F], "pair_ln")
        pair_attention(nc, m, c)
        layer_norm(nc, m, h[:, :], xn[:, 0:F], "gate_ln")
        gated_ffn(nc, m, c)
        layer_norm(nc, m, h[:, :], xn[:, 0:F], "pal_ln")
        palette_attention(nc, m, c)
        layer_norm(nc, m, h[:, :], xn[:, 0:F], "moe_ln")
        top2_experts(nc, m, c)
        with nc.semaphore("out_stored") as out_stored, nc.Block() as block:
            @block.sync
            def _(sp):
                sp.dma_start(out.rearrange("b t d -> t b d"), h[:, :].rearrange("t (b d) -> t b d", d=D)).then_inc(out_stored, 16)
                sp.wait_ge(out_stored, 16)


def add_in(nc, acc, more, tag):
    with nc.Block() as block:
        @block.vector
        def _(dve):
            nc.vector.tensor_tensor(acc, acc, more, ALU.add)


def laid_out(inp):
    f = {k: np.asarray(v) for k, v in inp.items()}
    a = {}
    a["ident"] = np.eye(128, dtype=np.float32)
    a["ones"] = np.ones((1, 512), np.float32)
    x = f["x"].reshape(B, -1)[:, :ROWS * PATCH_COLS].reshape(B, ROWS, PATCH_COLS)
    a["tok_rows"] = x.transpose(2, 0, 1).reshape(PATCH_COLS, B * ROWS)
    a["tok_w"] = f["L0_tok_W"].reshape(D, 2, 128).transpose(2, 1, 0).reshape(128, 2 * D)
    a["tok_b"] = f["L0_tok_b"].reshape(1, D)
    a["tok_gamma"] = f["L0_tok_gamma"].reshape(1, D)
    a["tok_beta"] = f["L0_tok_beta"].reshape(1, D)
    w = f["L0_attn_slow_W"].reshape(HEADS, 5 * DH + 2, D)
    cut = [w[:, k * DH:(k + 1) * DH].reshape(HEADS * DH, D) for k in range(5)]
    q, k, v, rk, rv = cut
    a["fw_w"] = np.concatenate([q, k, rk, v, rv, w[:, 5 * DH], w[:, 5 * DH + 1]]).T
    a["fw_w_out"] = f["L0_attn_out_W"].reshape(D, 2, 128).transpose(2, 1, 0).reshape(128, 2 * D)
    a["fw_gain"] = f["L0_attn_ln_g"].reshape(1, D)
    a["fw_shift"] = f["L0_attn_ln_b"].reshape(1, D)
    a["mod_w1"] = f["L0_ffn_w1"]
    a["mod_b1"] = f["L0_ffn_b1"].reshape(2, 128).T
    a["mod_w2"] = f["L0_ffn_w2"].reshape(2, 128, D).transpose(1, 0, 2).reshape(128, 2 * D)
    a["mod_b2"] = f["L0_ffn_b2"].reshape(1, D)
    a["mod_wr"] = f["L0_ffn_wr"].reshape(1, D)
    a["mod_br"] = f["L0_ffn_br"].reshape(1, 1)
    a["win_w"] = np.concatenate([f["L1_attn_qkv_w"], f["L1_attn_qkv_b"][None]])
    a["win_proj"] = np.concatenate([f["L1_attn_proj_w"], f["L1_attn_proj_b"][None]])
    at = np.arange(WIN)
    a["win_bias"] = f["L1_attn_rel_bias"][at[None, :] - at[:, None] + WIN - 1].transpose(2, 0, 1).reshape(1, -1)
    a["count"] = np.arange(128, dtype=np.float32)[None]
    a["top1_wr"] = np.concatenate([f["L1_ffn_router_w"].T, f["L1_ffn_router_b"][None]])
    a["top1_w1"] = np.concatenate([f["L1_ffn_W1"].transpose(1, 0, 2).reshape(D, E1 * H1), f["L1_ffn_b1"].reshape(1, -1)])
    a["top1_w2"] = f["L1_ffn_W2"].reshape(-1, 128, D).transpose(1, 0, 2).reshape(128, -1)
    a["top1_b2"] = f["L1_ffn_b2"]
    a["top1_spread"] = np.repeat(np.eye(E1, dtype=np.float32), H1, axis=1)
    v = f["L2_attn_Wv"].T.reshape(D, DG, NGRP).transpose(0, 2, 1).reshape(D, D)
    a["pair_w"] = np.concatenate([f["L2_attn_Wq"].T, f["L2_attn_Wk"].T, v], axis=1)
    mlp = np.zeros((2, NGRP, DG, 2, NGRP), np.float32)
    for s in range(2):
        for g in range(NGRP):
            mlp[s, g, :, s, g] = f["L2_attn_w_mlp"]
    a["pair_mlp"] = mlp.reshape(128, 2 * NGRP)
    a["pair_b"] = f["L2_attn_b_mlp"].reshape(1, 1)
    a["gate_w1"] = f["L2_ffn_W1"]
    a["gate_b1"] = f["L2_ffn_b1"].reshape(2, 128).T
    a["gate_wg"] = f["L2_ffn_Wg"].reshape(2, 128, E2).transpose(1, 0, 2).reshape(128, -1)
    a["gate_bg"] = f["L2_ffn_bg"].reshape(1, E2)
    a["gate_wd"] = f["L2_ffn_Wd"].reshape(E2, 2, 128, D).transpose(2, 1, 0, 3).reshape(128, -1)
    a["gate_bd"] = f["L2_ffn_bd"].reshape(1, -1)
    halves = lambda w, r: w.reshape(D, r, D // 2, 2).transpose(0, 1, 3, 2).reshape(D, r * D)
    a["pal_w"] = np.concatenate([halves(f["L3_attn_Wi"], BR), halves(f["L3_attn_Wp"], 1)], axis=1)
    angle = np.outer(np.arange(T, dtype=np.float32), 1.0 / 10000.0 ** (np.arange(0, D, 2, dtype=np.float32) / D))
    cos, sin = np.cos(angle), np.sin(angle)
    a["pal_turn"] = np.concatenate([cos, cos, sin, sin], axis=1).astype(np.float32)
    t, k = np.arange(T), np.arange(KS)
    a["pal_causal"] = np.where(t[None, :] > t[:, None], MASKED, 0.0).astype(np.float32)
    a["pal_shift"] = np.where(k[None, :] > t[:, None], 128.0, 0.0).astype(np.float32)
    q = np.arange(NS) % T
    a["pal_age"] = (np.maximum(q[None, :] - t[:, None], 0).astype(np.float32) / np.float32(T)).astype(np.float32)
    a["pal_key"] = t.astype(np.float32)[:, None]
    place = np.arange(BR * KS)
    a["pal_pick"] = (place[:, None] % KS == np.arange(KM)[None]).astype(np.float32)
    a["pal_rows"] = (place[:, None] // KS == np.arange(NS)[None] // T).astype(np.float32)
    a["pal_own"] = (np.arange(RB_)[:, None] // REL == np.arange(SW)[None] % CB // KM).astype(np.float32)
    a["pal_w1"] = np.tile(f["L3_attn_W1"], (SB, 1))
    a["pal_b1"] = np.tile(f["L3_attn_b1"], 2).reshape(2 * RH, 1)
    a["pal_w2T"] = f["L3_attn_W2"].T
    a["pal_b2"] = np.repeat(f["L3_attn_b2"][:, None], CB, axis=1)
    a["pal_wcm"] = np.concatenate([f["L3_attn_Wc"], f["L3_attn_Wm"]], axis=1)
    a["pal_bcm"] = np.repeat(np.concatenate([f["L3_attn_bc"], f["L3_attn_bm"]])[None], CB, axis=0)
    col = np.arange(CB)
    s = np.arange(NB)[:, None] * SB + col[None] // KM
    a["pal_soft"] = np.where((col[None] % KM > s % T) & (s < NS), MASKED, 0.0).astype(np.float32)
    a["pal_grid"] = np.repeat(np.arange(PH, dtype=np.float32)[None], CB, axis=0)
    a["pal_site"] = (col[:, None] // KM == np.arange(SB)[None]).astype(np.float32)
    a["pal_palette"] = f["L3_attn_palette"].reshape(D, 2, 128).transpose(2, 1, 0).reshape(128, 2 * D)
    a["pal_wo"] = f["L3_attn_Wo"].transpose(1, 0, 2).reshape(D, BR * D)
    a["moe_wg"] = np.concatenate([f["L3_ffn_Wg"], f["L3_ffn_bg"][None]])
    a["moe_w1"] = f["L3_ffn_W1"].transpose(1, 0, 2).reshape(D, -1)
    a["moe_b1"] = f["L3_ffn_b1"].reshape(2 * E2, 128).T
    a["moe_w2"] = f["L3_ffn_W2"].reshape(2 * E2, 128, D).transpose(1, 0, 2).reshape(128, -1)
    a["moe_b2"] = f["L3_ffn_b2"].reshape(1, -1)
    return {k: np.ascontiguousarray(v) for k, v in a.items()}




def kernel(**inputs):
    import concourse.bacc as bacc
    from concourse.bass_utils import run_bass_kernel_spmd

    nc = bacc.Bacc("TRN2", target_bir_lowering=False, num_devices=1)
    arrays = laid_out(inputs)
    c = {k: nc.dram_tensor(k + "_in", v.shape, mybir.dt.from_np(v.dtype), kind="ExternalInput").ap() for k, v in arrays.items()}
    out = nc.dram_tensor("out", (B, T, D), F32, kind="ExternalOutput").ap()
    program(nc, c, out)
    r = run_bass_kernel_spmd(nc, [{k + "_in": v for k, v in arrays.items()}], core_ids=[0])
    return r.results[0]["out"]
```

```python
from contextlib import ExitStack

import numpy as np
import concourse.bass as bass
from concourse import mybir
from concourse.alu_op_type import AluOpType as ALU

F32 = mybir.dt.float32
BF16 = mybir.dt.bfloat16
U32 = mybir.dt.uint32
ACT = mybir.ActivationFunctionType
X = mybir.AxisListType.X
XY = mybir.AxisListType.XY

B = 64
T = 92
D = 64
F = B * D
PATCH_COLS = 128
ROWS = T + 1
G = 4
NG = B // G
GT = G * T
EPS = 1e-5


class Layer(ExitStack):

    def __init__(self, nc):
        super().__init__()
        self.nc, self.semaphores = nc, []

    def enter_context(self, cm):
        got = super().enter_context(cm)
        if isinstance(got, bass.SemaphoreHandle):
            self.semaphores.append(got)
        return got

    def block(self):
        self.callback(self.clear)
        return super().enter_context(self.nc.Block())

    def clear(self):
        numbers = sorted(s.num for s in self.semaphores)
        while numbers:
            n = 1
            while n < len(numbers) and numbers[n] == numbers[0] + n:
                n += 1
            self.nc.gpsimd.sem_clear(range(numbers[0], numbers[0] + n))
            numbers = numbers[n:]


class Chain:

    def __init__(self, eng, sem, gap=None):
        self.eng, self.sem, self.gap = eng, sem, gap
        self.before, self.n, self.i, self.per = 0, 0, 0, 0

    def begin(self, i, per, first=0):
        self.before += self.n
        self.i, self.per, self.n, self.first = i, per, 0, first

    def end(self, times):
        assert self.n == self.per, f"{self.sem.name}: {self.n} steps in a body, {self.per} said"
        self.before += self.per * times
        self.i, self.per, self.n = 0, 0, 0

    def __call__(self, ins, gap=False):
        ins.then_inc(self.sem, 1)
        self.n += 1
        at = self.before + self.n
        if self.per:
            at = (self.i - self.first) * self.per + at if self.first else self.i * self.per + at
        self.eng.wait_ge(self.sem, at)
        if gap:
            self.eng.sem_inc(self.gap, 1)


def inner(ap, n):
    return ap.unsqueeze(len(ap.shape)).broadcast_to(list(ap.shape) + [n])


def outer(ap, n, axis=1):
    shape = list(ap.shape)
    shape.insert(axis, n)
    return ap.unsqueeze(axis).broadcast_to(shape)


def tokens(nc, m, c):
    with Layer(nc) as ctx:
        rows = ctx.enter_context(nc.sbuf_tensor("tok_rows", [128, 2, G * ROWS], F32))
        w = ctx.enter_context(nc.sbuf_tensor("tok_w_sb", [128, 2 * D], F32))
        b = ctx.enter_context(nc.sbuf_tensor("tok_b_sb", [1, D], F32))
        weights = ctx.enter_context(nc.semaphore("tok_weights"))
        rows0 = ctx.enter_context(nc.semaphore("tok_rows0"))
        rows1 = ctx.enter_context(nc.semaphore("tok_rows1"))
        rows_free = ctx.enter_context(nc.semaphore("tok_rows_free"))
        done = ctx.enter_context(nc.semaphore("tok_done"))
        psum_free = ctx.enter_context(nc.semaphore("tok_psum_free"))
        block = ctx.block()
        rows_loaded = [rows0, rows1]

        @block.sync
        def _(sp):
            sp.dma_start(w[:, :], c["tok_w"]).then_inc(weights, 16)
            sp.dma_start(b[:, :], c["tok_b"]).then_inc(weights, 16)
            sp.dma_start(m.ident[:, :], c["ident"]).then_inc(weights, 16)
            sp.dma_start(m.ones[:, :], c["ones"]).then_inc(weights, 16)
            with sp.Fori(0, NG // 2) as i:
                for u in range(2):
                    sp.wait_ge(rows_free, i * 2 + u + 1)
                    sp.dma_start(rows[:, u, :], c["tok_rows"][:, bass.ds((i * 2 + u) * (G * ROWS), G * ROWS)]).then_inc(rows_loaded[u], 16)

        @block.tensor
        def _(pe):
            pe.sem_inc(rows_free, 2)
            pe.wait_ge(weights, 64)
            with pe.Fori(0, NG // 2) as i:
                for u in range(2):
                    pe.wait_ge(rows_loaded[u], i * 16 + 16)
                    pe.wait_ge(psum_free, i * 2 + u + 1)
                    for q in range(G):
                        out = m.ps[0:T, u * 512 + q * D:u * 512 + (q + 1) * D]
                        at = q * ROWS
                        nc.tensor.matmul(out, rows[:, u, at:at + T], w[:, 0:D], start=True, stop=False)
                        nc.tensor.matmul(out, rows[:, u, at + 1:at + 1 + T], w[:, D:2 * D], start=False, stop=False)
                        last = nc.tensor.matmul(out, m.ones[0:1, 0:T], b[0:1, :], start=False, stop=True)
                    last.then_inc(done, 1)
                    pe.wait_ge(done, i * 2 + u + 1)
                    pe.sem_inc(rows_free, 1)

        @block.scalar
        def _(act):
            act.sem_inc(psum_free, 2)
            with act.Fori(0, NG // 2) as i:
                for u in range(2):
                    act.wait_ge(done, i * 2 + u + 1)
                    nc.scalar.activation(m.h[:, bass.ds((i * 2 + u) * (G * D), G * D)], m.ps[0:T, u * 512:u * 512 + G * D], ACT.Copy).then_inc(psum_free, 1)


def layer_norm(nc, m, src, dst, tag, gain=None, shift=None):
    with Layer(nc) as ctx:
        sq = ctx.enter_context(nc.sbuf_tensor(f"{tag}_sq", [T, F], F32))
        total = ctx.enter_context(nc.sbuf_tensor(f"{tag}_sum", [T, B], F32))
        mean = ctx.enter_context(nc.sbuf_tensor(f"{tag}_mean", [T, B], F32))
        var = ctx.enter_context(nc.sbuf_tensor(f"{tag}_var", [T, B], F32))
        std = ctx.enter_context(nc.sbuf_tensor(f"{tag}_std", [T, B], F32))
        rstd = ctx.enter_context(nc.sbuf_tensor(f"{tag}_rstd", [T, B], F32))
        affine = ctx.enter_context(nc.sbuf_tensor(f"{tag}_gain", [T, 2, D], F32))
        affine_loaded = ctx.enter_context(nc.semaphore(f"{tag}_affine_loaded"))
        centred = ctx.enter_context(nc.semaphore(f"{tag}_centred"))
        squared = ctx.enter_context(nc.semaphore(f"{tag}_squared"))
        var_ready = ctx.enter_context(nc.semaphore(f"{tag}_var_ready"))
        std_ready = ctx.enter_context(nc.semaphore(f"{tag}_std_ready"))
        steps = ctx.enter_context(nc.semaphore(f"{tag}_steps"))
        block = ctx.block()
        v3 = lambda ap: ap.rearrange("p (b d) -> p b d", d=D)

        @block.sync
        def _(sp):
            if gain is not None:
                sp.dma_start(affine[:, 0, :], gain.broadcast_to([T, D])).then_inc(affine_loaded, 16)
                sp.dma_start(affine[:, 1, :], shift.broadcast_to([T, D])).then_inc(affine_loaded, 16)

        @block.vector
        def _(dve):
            step = Chain(dve, steps)
            step(nc.vector.tensor_reduce(total[:, :], v3(src), X, ALU.add))
            step(nc.vector.tensor_scalar(mean[:, :], total[:, :], 1.0 / D, None, ALU.mult))
            nc.vector.tensor_tensor(v3(dst), v3(src), inner(mean[:, :], D), ALU.subtract).then_inc(centred, 1)
            dve.wait_ge(squared, 1)
            step(nc.vector.tensor_reduce(total[:, :], v3(sq[:, :]), X, ALU.add))
            nc.vector.tensor_scalar(var[:, :], total[:, :], 1.0 / D, EPS, ALU.mult, ALU.add).then_inc(var_ready, 1)
            dve.wait_ge(std_ready, 1)
            step(nc.vector.reciprocal(rstd[:, :], std[:, :]))
            step(nc.vector.tensor_tensor(v3(dst), v3(dst), inner(rstd[:, :], D), ALU.mult))
            if gain is not None:
                dve.wait_ge(affine_loaded, 32)
                step(nc.vector.tensor_tensor(v3(dst), v3(dst), outer(affine[:, 0, :], B), ALU.mult))
                step(nc.vector.tensor_tensor(v3(dst), v3(dst), outer(affine[:, 1, :], B), ALU.add))

        @block.scalar
        def _(act):
            act.wait_ge(centred, 1)
            nc.scalar.activation(sq[:, :], dst, ACT.Square).then_inc(squared, 1)
            act.wait_ge(var_ready, 1)
            nc.scalar.activation(std[:, :], var[:, :], ACT.Sqrt).then_inc(std_ready, 1)


HEADS = 8
DH = 32
UNIT = 2 * DH * DH
PAIRS = T * HEADS
SLOTS = 6
PR = -(-PAIRS // SLOTS)
GIVEN = 5 * DH + 2
KEY, VALUE, QUERY, BETA = 0, 2 * DH, 4 * DH, 5 * DH
OWN = 3
EARLY = 1
POOL_GROUPS = [(OWN, 2), (OWN + 2, 1)]


def fast_weights(nc, m, c):
    CUTS = [(0, 512), (512, 1024), (1024, 1296)]
    QK, RK, VV, RV, BB = 0, 512, 768, 1024, 1280
    IN_BANK, H_BANK, QOUT = 0, 512, 1024
    KOUT = {first: 512 * (3 + k) for k, (first, _) in enumerate(POOL_GROUPS)}
    given_dram = nc.dram_tensor("fw_given_scratch", (PAIRS, GIVEN), F32).ap()
    h_dram = nc.dram_tensor("fw_h_scratch", (PAIRS, DH), F32).ap()
    FULL = PAIRS // SLOTS
    with Layer(nc) as ctx:
        state = ctx.enter_context(nc.sbuf_tensor("fw_state", [PR, SLOTS * UNIT], F32))
        growth = ctx.enter_context(nc.sbuf_tensor("fw_growth", [PR, UNIT], F32))
        pool_growth = ctx.enter_context(nc.sbuf_tensor("fw_pool_growth", [PR, 2 * UNIT], F32))
        own_sums = ctx.enter_context(nc.sbuf_tensor("fw_own_sums", [PR, OWN * 2 * DH], F32))
        pool_q = ctx.enter_context(nc.sbuf_tensor("fw_pool_q", [PR, 2 * UNIT], F32))
        pool_k = ctx.enter_context(nc.sbuf_tensor("fw_pool_k", [PR, 2 * UNIT], F32))
        w = ctx.enter_context(nc.sbuf_tensor("fw_w", [D, 1296], F32))
        w_out = ctx.enter_context(nc.sbuf_tensor("fw_w_out", [128, 2 * D], F32))
        raw = ctx.enter_context(nc.sbuf_tensor("fw_raw", [T, 1296], F32))
        o = ctx.enter_context(nc.sbuf_tensor("fw_o", [T, 2, D], F32))
        oT = ctx.enter_context(nc.sbuf_tensor("fw_oT", [D, T], F32))
        neg = ctx.enter_context(nc.sbuf_tensor("fw_neg", [T, 512], F32))
        small = ctx.enter_context(nc.sbuf_tensor("fw_small", [T, 8, 16], F32))
        be = ctx.enter_context(nc.sbuf_tensor("fw_be", [T, 2, 16], F32))
        made = ctx.enter_context(nc.sbuf_tensor("fw_made", [T, HEADS * GIVEN], F32))
        given = ctx.enter_context(nc.sbuf_tensor("fw_given", [PR, 2, SLOTS * GIVEN], F32))
        Q = ctx.enter_context(nc.sbuf_tensor("fw_Q", [PR, SLOTS * 2 * DH], F32))
        dv = ctx.enter_context(nc.sbuf_tensor("fw_dv", [PR, SLOTS * 2 * DH], F32))
        hs = ctx.enter_context(nc.sbuf_tensor("fw_h", [PR, SLOTS * DH], F32))
        hx = ctx.enter_context(nc.sbuf_tensor("fw_hx", [PR, SLOTS * DH], F32))
        he = ctx.enter_context(nc.sbuf_tensor("fw_he", [PR, SLOTS * DH], F32))
        soft = ctx.enter_context(nc.sbuf_tensor("fw_soft", [PR, 3, SLOTS], F32))
        h_tokens = ctx.enter_context(nc.sbuf_tensor("fw_h_tokens", [T, HEADS * DH], F32))
        hT = ctx.enter_context(nc.sbuf_tensor("fw_hT", [128, 2 * T], F32))
        weights = ctx.enter_context(nc.semaphore("fw_weights"))
        given_out = ctx.enter_context(nc.semaphore("fw_given_out"))
        given_in = ctx.enter_context(nc.semaphore("fw_given_in"))
        h_out = ctx.enter_context(nc.semaphore("fw_h_out"))
        h_in = ctx.enter_context(nc.semaphore("fw_h_in"))
        dve_done = ctx.enter_context(nc.semaphore("fw_dve_done"))
        zeroed = ctx.enter_context(nc.semaphore("fw_zeroed"))
        o_staged = ctx.enter_context(nc.semaphore("fw_o_staged"))
        o_turned = ctx.enter_context(nc.semaphore("fw_o_turned"))
        oT_ready = ctx.enter_context(nc.semaphore("fw_oT_ready"))
        qkv_ready = ctx.enter_context(nc.semaphore("fw_qkv_ready"))
        qkv_read = ctx.enter_context(nc.semaphore("fw_qkv_read"))
        neg_ready = ctx.enter_context(nc.semaphore("fw_neg_ready"))
        exp_ready = ctx.enter_context(nc.semaphore("fw_exp_ready"))
        rk_ready = ctx.enter_context(nc.semaphore("fw_rk_ready"))
        rke_ready = ctx.enter_context(nc.semaphore("fw_rke_ready"))
        be_ready = ctx.enter_context(nc.semaphore("fw_be_ready"))
        v_ready = ctx.enter_context(nc.semaphore("fw_v_ready"))
        k_ready = ctx.enter_context(nc.semaphore("fw_k_ready"))
        q_ready = ctx.enter_context(nc.semaphore("fw_q_ready"))
        dv_ready = ctx.enter_context(nc.semaphore("fw_dv_ready"))
        hx_ready = ctx.enter_context(nc.semaphore("fw_hx_ready"))
        he_ready = ctx.enter_context(nc.semaphore("fw_he_ready"))
        h_ready = ctx.enter_context(nc.semaphore("fw_h_ready"))
        h_turned = ctx.enter_context(nc.semaphore("fw_h_turned"))
        hT_ready = ctx.enter_context(nc.semaphore("fw_hT_ready"))
        proj_done = ctx.enter_context(nc.semaphore("fw_proj_done"))
        stored = ctx.enter_context(nc.semaphore("fw_stored"))
        pool_prod_q = ctx.enter_context(nc.semaphore("fw_pool_prod_q"))
        pool_prod_k = ctx.enter_context(nc.semaphore("fw_pool_prod_k"))
        pool_updated = ctx.enter_context(nc.semaphore("fw_pool_updated"))
        pool_q_summed = ctx.enter_context(nc.semaphore("fw_pool_q_summed"))
        pool_k_summed = ctx.enter_context(nc.semaphore("fw_pool_k_summed"))
        pe_gap = ctx.enter_context(nc.semaphore("fw_pe_gap"))
        sp_gap = ctx.enter_context(nc.semaphore("fw_sp_gap"))
        dve_steps = ctx.enter_context(nc.semaphore("fw_dve_steps"))
        pool_steps = ctx.enter_context(nc.semaphore("fw_pool_steps"))
        block = ctx.block()
        def slots2(ap, first, n, w=DH):
            return ap[:, first * 2 * w:(first + n) * 2 * w].rearrange("p (u j) -> p u j", j=w)

        def given_of(p):
            return given[:, p, :].rearrange("p (k f) -> p k f", f=GIVEN)

        def keys(p, k):
            return given_of(p)[:, k, KEY:VALUE].rearrange("p (w j) -> p w j", j=DH)

        made_heads = made[:, :].rearrange("p (h f) -> p h f", f=GIVEN)

        def grid(ap, first, n):
            return ap[:, first * UNIT:(first + n) * UNIT].rearrange("p (u i j) -> p u i j", i=DH, j=DH)

        def per_head(ap):
            return ap.rearrange("p (h j) -> p h j", j=DH)

        ps = m.ps
        NPG = len(POOL_GROUPS)

        @block.sync
        def _(sp):
            sp.dma_start(w[:, :], c["fw_w"]).then_inc(weights, 16)
            sp.dma_start(w_out[:, :], c["fw_w_out"]).then_inc(weights, 16)

            def spread_given(s, p):
                sp.wait_ge(k_ready, s + 1)
                sp.sem_inc(sp_gap, 1)
                sp.wait_ge(v_ready, s + 1)
                sp.sem_inc(sp_gap, 1)
                if not (type(s) is int and s == 0):
                    sp.wait_ge(given_in, 32 * s)
                sp.dma_start(given_dram.rearrange("(t h) f -> t (h f)", h=HEADS), made[:, :]).then_inc(given_out, 16)
                sp.wait_ge(given_out, 16 * (s + 1))
                sp.sem_inc(sp_gap, 1)
                sp.wait_ge(dve_done, s + 1)
                sp.sem_inc(sp_gap, 1)
                if not (type(s) is int and s == 0):
                    sp.wait_ge(pool_updated, (s - 1) * NPG + 1)
                sp.dma_start(given[0:FULL, p, :], given_dram[0:FULL * SLOTS, :].rearrange("(q k) f -> q (k f)", k=SLOTS)).then_inc(given_in, 16)
                sp.dma_start(given[FULL:PR, p, 0:(PAIRS - FULL * SLOTS) * GIVEN], given_dram[FULL * SLOTS:PAIRS, :].rearrange("(q k) f -> q (k f)", q=1)).then_inc(given_in, 16)

            def gather_h(s):
                sp.wait_ge(h_ready, s + 1)
                sp.sem_inc(sp_gap, 1)
                if not (type(s) is int and s == 0):
                    sp.wait_ge(h_in, 16 * s)
                sp.dma_start(h_dram[0:FULL * SLOTS, :].rearrange("(q k) j -> q (k j)", k=SLOTS), hs[0:FULL, :]).then_inc(h_out, 16)
                sp.dma_start(h_dram[FULL * SLOTS:PAIRS, :].rearrange("(q k) j -> q (k j)", q=1), hs[FULL:PR, 0:(PAIRS - FULL * SLOTS) * DH]).then_inc(h_out, 16)
                sp.wait_ge(h_out, 32 * (s + 2))
                sp.sem_inc(sp_gap, 1)
                sp.wait_ge(h_turned, s + 1)
                sp.dma_start(h_tokens[:, :], h_dram.rearrange("(t h) j -> t (h j)", h=HEADS)).then_inc(h_in, 16)

            sp.wait_ge(zeroed, 2)
            spread_given(0, 0)
            gather_h(0)
            spread_given(1, 1)
            with sp.Fori(0, B // 2 - 1) as i:
                for u in range(2):
                    gather_h(i * 2 + u + 1)
                    spread_given(i * 2 + u + 2, u)
            gather_h(B - 1)
            gather_h(B)

        @block.vector
        def _(dve):
            step = Chain(dve, dve_steps)

            def features_exponents(s):
                dve.wait_ge(qkv_read, 3 * s + 6)
                if not (type(s) is int and s == 0):
                    dve.wait_ge(given_out, 16 * s)
                nc.vector.tensor_scalar(neg[:, :], raw[:, QK:QK + 512], 0.0, None, ALU.min).then_inc(neg_ready, 1)
                step(nc.vector.tensor_reduce(small[:, 0, 0:8], per_head(raw[:, RK:RK + 256]), X, ALU.max))
                nc.vector.tensor_tensor(per_head(raw[:, RK:RK + 256]), per_head(raw[:, RK:RK + 256]), inner(small[:, 0, 0:8], DH), ALU.subtract).then_inc(rk_ready, 1)

            def features(s):
                dve.wait_ge(exp_ready, s + 1)
                step(nc.vector.scalar_tensor_tensor(raw[:, QK:QK + 512], raw[:, QK:QK + 512], 0.0, neg[:, :], ALU.max, ALU.add))
                step(nc.vector.tensor_reduce(small[:, 1, :], per_head(raw[:, QK:QK + 512]), X, ALU.add))
                step(nc.vector.reciprocal(small[:, 2, :], small[:, 1, :]))
                dve.wait_ge(rke_ready, s + 1)
                step(nc.vector.tensor_reduce(small[:, 3, 0:8], per_head(raw[:, RK:RK + 256]), X, ALU.add))
                step(nc.vector.reciprocal(small[:, 4, 0:8], small[:, 3, 0:8]))
                dve.wait_ge(be_ready, s + 1)
                step(nc.vector.tensor_scalar(be[:, 1, :], be[:, 0, :], 1.0, None, ALU.add))
                nc.vector.reciprocal(made_heads[:, :, BETA:BETA + 2], be[:, 1, :].rearrange("p (h w) -> p h w", w=2))
                nc.vector.tensor_tensor(made_heads[:, :, QUERY:BETA], per_head(raw[:, QK:QK + 256]), inner(small[:, 2, 0:8], DH), ALU.mult)
                nc.vector.tensor_tensor(made_heads[:, :, KEY:KEY + DH], per_head(raw[:, QK + 256:QK + 512]), inner(small[:, 2, 8:16], DH), ALU.mult)
                ins = nc.vector.tensor_tensor(made_heads[:, :, KEY + DH:VALUE], per_head(raw[:, RK:RK + 256]), inner(small[:, 4, 0:8], DH), ALU.mult)
                ins.then_inc(k_ready, 1)
                dve.wait_ge(k_ready, s + 1)

            def delta(first, n, p, sums):
                g = given_of(p)[:, first:first + n, :]
                to = dv[:, first * 2 * DH:(first + n) * 2 * DH].rearrange("p (k f) -> p k f", f=2 * DH)
                step(nc.vector.tensor_tensor(to, g[:, :, VALUE:QUERY], sums.rearrange("p (k f) -> p k f", f=2 * DH), ALU.subtract))
                halves = to.rearrange("p k (w j) -> p k w j", j=DH)
                return nc.vector.tensor_tensor(halves, halves, inner(g[:, :, BETA:GIVEN], DH), ALU.mult)

            def summed(first, n):
                return ps[0:PR, KOUT[first]:KOUT[first] + n * 64]

            def pool_delta(s, g, p):
                first, n = POOL_GROUPS[g]
                dve.wait_ge(pool_k_summed, s * NPG + g + 1)
                delta(first, n, p, summed(first, n)).then_inc(dv_ready, 1)

            def grow(k, p):
                step(nc.vector.tensor_tensor(grid(growth, 0, 1), inner(slots2(dv, k, 1), DH), outer(keys(p, k), DH, 2), ALU.mult))
                step(nc.vector.tensor_tensor(grid(state, k, 1), grid(state, k, 1), grid(growth, 0, 1), ALU.add))

            def own_slots(s, first, n, p, last):
                for k in range(first, first + n):
                    grow(k, p)
                    step(nc.vector.tensor_tensor(grid(growth, 0, 1), grid(state, k, 1), outer(slots2(Q, k, 1), DH, 2), ALU.mult))
                    step(nc.vector.tensor_reduce(hs[:, k * DH:(k + 1) * DH], growth[:, :].rearrange("p (w i j) -> p i w j", i=DH, j=DH), XY, ALU.add))
                    if not last:
                        if k == 0:
                            dve.wait_ge(given_in, 32 * (s + 2))
                        step(nc.vector.tensor_tensor(grid(growth, 0, 1), grid(state, k, 1), outer(keys(1 - p, k), DH, 2), ALU.mult))
                        step(nc.vector.tensor_reduce(own_sums[:, k * 64:(k + 1) * 64], growth[:, :].rearrange("p (r j) -> p r j", j=DH), X, ALU.add))

            def outputs(s):
                dve.wait_ge(pool_q_summed, (s + 1) * NPG)
                dve.wait_ge(h_out, 32 * (s + 1))
                both = ps[0:PR, QOUT + OWN * 64:QOUT + SLOTS * 64].rearrange("p (h w j) -> p h j w", w=2, j=DH)
                ins = nc.vector.tensor_reduce(per_head(hs[:, OWN * DH:]), both, X, ALU.add)
                ins.then_inc(h_ready, 1)
                dve.wait_ge(h_ready, s + 1)

            def soft_exponents(s):
                outputs(s)
                step(nc.vector.tensor_reduce(soft[:, 0, :], per_head(hs[:, :]), X, ALU.max))
                nc.vector.tensor_tensor(per_head(hx[:, :]), per_head(hs[:, :]), inner(soft[:, 0, :], DH), ALU.subtract).then_inc(hx_ready, 1)

            def soft_query(s, p):
                dve.wait_ge(he_ready, s + 1)
                step(nc.vector.tensor_reduce(soft[:, 1, :], per_head(he[:, :]), X, ALU.add))
                step(nc.vector.reciprocal(soft[:, 2, :], soft[:, 1, :]))
                halves = Q[:, :].rearrange("p (k w j) -> p k w j", w=2, j=DH)
                nc.vector.tensor_copy(halves[:, :, 0, :], given_of(p)[:, :, QUERY:BETA])
                nc.vector.tensor_tensor(halves[:, :, 1, :], per_head(he[:, :]), inner(soft[:, 2, :], DH), ALU.mult).then_inc(q_ready, 1)
                dve.wait_ge(q_ready, s + 1)

            def whole_step(s, p, last=False):
                dve.wait_ge(given_in, 32 * (s + 1))
                soft_exponents(s)
                if not last:
                    features_exponents(s + 1)
                soft_query(s, p)
                if not last:
                    features(s + 1)
                step(delta(0, OWN, p, own_sums[:, :]))
                dve.wait_ge(h_out, 32 * (s + 2))
                own_slots(s, 0, EARLY, p, last)
                pool_delta(s, 1, p)
                own_slots(s, EARLY, 1, p, last)
                if not last:
                    pool_delta(s + 1, 0, 1 - p)
                own_slots(s, EARLY + 1, OWN - EARLY - 1, p, last)
                dve.sem_inc(dve_done, 1)

            nc.vector.memset(state[:, 0:POOL_GROUPS[0][0] * UNIT], 0.0)
            for at in KOUT.values():
                nc.vector.memset(ps[0:PR, at:at + 128], 0.0)
            nc.vector.memset(given[:, :, :], 0.0)
            nc.vector.memset(hs[:, :], 0.0)
            nc.vector.memset(own_sums[:, :], 0.0)
            step(nc.vector.memset(ps[0:PR, QOUT:QOUT + 512], 0.0))
            dve.sem_inc(zeroed, 1)
            dve.sem_inc(pool_updated, 1)
            dve.sem_inc(pool_q_summed, NPG)
            dve.sem_inc(pool_k_summed, NPG)
            dve.sem_inc(h_turned, 1)
            dve.sem_inc(h_out, 32)
            dve.sem_inc(dve_done, 2)
            features_exponents(0)
            features(0)
            dve.wait_ge(given_in, 32)
            pool_delta(0, 0, 0)
            N = 32
            with dve.Fori(0, B // 2 - 1) as i:
                step.begin(i, 2 * N)
                for u in range(2):
                    whole_step(i * 2 + u, u)
                step.end(B // 2 - 1)
            whole_step(B - 2, 0)
            whole_step(B - 1, 1, last=True)
            outputs(B)
            dve.wait_ge(stored, B + 2)
            step(nc.vector.tensor_tensor(m.h[:, :], m.h[:, :], m.xn[:, D:D + F], ALU.add))

        @block.gpsimd
        def _(pool):
            step = Chain(pool, pool_steps)

            def times_k(s, g, p):
                first, n = POOL_GROUPS[g]
                for k in range(n):
                    ins = nc.gpsimd.tensor_tensor(grid(pool_k, k, 1), grid(state, first + k, 1), outer(keys(p, first + k), DH, 2), ALU.mult)
                ins.then_inc(pool_prod_k, 1)

            def whole_step(s, p, last=False):
                for g in range(NPG):
                    first, n = POOL_GROUPS[g]
                    pool.wait_ge(dv_ready, s * NPG + g + 1)
                    for k in range(n):
                        ins = nc.gpsimd.tensor_tensor(grid(pool_growth, k, 1), inner(slots2(dv, first + k, 1), DH), outer(keys(p, first + k), DH, 2), ALU.mult)
                    step(ins)
                    ins = nc.gpsimd.tensor_tensor(grid(state, first, n), grid(state, first, n), grid(pool_growth, 0, n), ALU.add)
                    ins.then_inc(pool_updated, 1)
                    pool.wait_ge(pool_updated, s * NPG + g + 2)
                    pool.wait_ge(q_ready, s + 1)
                    pool.wait_ge(pool_q_summed, s * NPG + g + NPG)
                    nc.gpsimd.tensor_tensor(grid(pool_q, 0, n), grid(state, first, n), outer(slots2(Q, first, n), DH, 2), ALU.mult).then_inc(pool_prod_q, 1)
                    if not last:
                        pool.wait_ge(given_in, 32 * (s + 2))
                        pool.wait_ge(pool_k_summed, s * NPG + g + NPG)
                        times_k(s, g, 1 - p)

            nc.gpsimd.memset(state[:, POOL_GROUPS[0][0] * UNIT:], 0.0).then_inc(zeroed, 1)
            pool.wait_ge(zeroed, 2)
            N = 2
            with pool.Fori(0, B // 2 - 1) as i:
                step.begin(i, 2 * N)
                for u in range(2):
                    whole_step(i * 2 + u, u)
                step.end(B // 2 - 1)
            whole_step(B - 2, 0)
            whole_step(B - 1, 1, last=True)

        @block.tensor
        def _(pe):
            def turn_and_project(s):
                pe.wait_ge(o_staged, s + 1)
                pe.wait_ge(qkv_read, 3 * s + 3)
                pe.sem_inc(pe_gap, 1)
                nc.tensor.transpose(ps[0:D, IN_BANK:IN_BANK + T], o[:, 0, :], m.ident[0:T, 0:T]).then_inc(o_turned, 1)
                pe.wait_ge(oT_ready, s + 1)
                for k, (a, b) in enumerate(CUTS):
                    if k == 1 and not (type(s) is int and s == 0):
                        pe.wait_ge(stored, s)
                    if k == 2:
                        pe.wait_ge(qkv_read, 3 * s + 4)
                    at = (IN_BANK, H_BANK)[k % 2]
                    nc.tensor.matmul(ps[0:T, at:at + b - a], oT[:, :], w[:, a:b], start=True, stop=True).then_inc(qkv_ready, 1)

            def sum_rows(products, at, n):
                v = products[:, 0:n * UNIT].rearrange("p (r j) -> p r j", j=DH)
                for j in range(DH):
                    ins = nc.tensor.matmul(ps[0:PR, at:at + n * 2 * DH], m.ident[0:PR, 0:PR], v[:, :, j], start=(j == 0), stop=(j == DH - 1))
                return ins

            def project_h(s, bank_used=True):
                pe.wait_ge(h_in, 16 * (s + 1))
                pe.wait_ge(hT_ready, s + 1)
                pe.wait_ge(stored, s + 1)
                if bank_used:
                    pe.wait_ge(qkv_read, 3 * s + 8)
                for k in range(2):
                    ins = nc.tensor.transpose(ps[:, H_BANK + k * T:H_BANK + (k + 1) * T], h_tokens[:, k * 128:(k + 1) * 128], m.ident[0:T, 0:T])
                ins.then_inc(h_turned, 1)
                pe.wait_ge(hT_ready, s + 2)
                nc.tensor.matmul(ps[0:T, H_BANK + 256:H_BANK + 256 + D], hT[:, 0:T], w_out[:, 0:D], start=True, stop=False)
                nc.tensor.matmul(ps[0:T, H_BANK + 256:H_BANK + 256 + D], hT[:, T:2 * T], w_out[:, D:2 * D], start=False, stop=True).then_inc(proj_done, 1)

            def whole_step(s, p, last=False, more=True):
                project_h(s, bank_used=not last)
                for g, (first, n) in enumerate(POOL_GROUPS):
                    pe.wait_ge(pool_prod_q, s * NPG + g + 1)
                    sum_rows(pool_q, QOUT + first * 2 * DH, n).then_inc(pool_q_summed, 1)
                    if not last:
                        pe.wait_ge(pool_prod_k, s * NPG + g + 1)
                        sum_rows(pool_k, KOUT[first], n).then_inc(pool_k_summed, 1)
                    if g == 0 and more:
                        turn_and_project(s + 2)

            pe.wait_ge(weights, 32)
            pe.wait_ge(zeroed, 2)
            turn_and_project(0)
            turn_and_project(1)
            with pe.Fori(0, B // 2 - 1) as i:
                for u in range(2):
                    whole_step(i * 2 + u, u)
            whole_step(B - 2, 0, more=False)
            whole_step(B - 1, 1, last=True, more=False)
            project_h(B, bank_used=False)

        @block.scalar
        def _(act):
            def stage(s):
                act.wait_ge(o_turned, s + 1)
                nc.scalar.activation(o[:, 0, :], m.xn[:, bass.ds((s + 1) * D, D)], ACT.Copy).then_inc(o_staged, 1)
                act.wait_ge(o_turned, s + 2)
                nc.scalar.activation(oT[:, :], ps[0:D, IN_BANK:IN_BANK + T], ACT.Copy).then_inc(oT_ready, 1)
                if not (type(s) is int and s == 0):
                    act.wait_ge(k_ready, s)
                for k, (a, b) in enumerate(CUTS):
                    act.wait_ge(qkv_ready, 3 * s + k + 1)
                    at = (IN_BANK, H_BANK)[k % 2]
                    nc.scalar.activation(raw[:, a:b], ps[0:T, at:at + b - a], ACT.Copy).then_inc(qkv_read, 1)

            def features(s):
                act.wait_ge(neg_ready, s + 1)
                nc.scalar.activation(neg[:, :], neg[:, :], ACT.Exp).then_inc(exp_ready, 1)
                act.wait_ge(rk_ready, s + 1)
                nc.scalar.activation(raw[:, RK:RK + 256], raw[:, RK:RK + 256], ACT.Exp).then_inc(rke_ready, 1)
                nc.scalar.activation(be[:, 0, :].rearrange("p (h w) -> p w h", w=2), raw[:, BB:BB + 16].rearrange("p (w h) -> p w h", w=2), ACT.Exp, scale=-1.0).then_inc(be_ready, 1)
                nc.scalar.activation(made_heads[:, :, VALUE:VALUE + DH], per_head(raw[:, VV:VV + 256]), ACT.Copy)
                nc.scalar.activation(made_heads[:, :, VALUE + DH:QUERY], per_head(raw[:, RV:RV + 256]), ACT.Copy).then_inc(v_ready, 1)

            def soft(s):
                act.wait_ge(hx_ready, s + 1)
                nc.scalar.activation(he[:, :], hx[:, :], ACT.Exp).then_inc(he_ready, 1)

            def finish(s):
                act.wait_ge(h_turned, s + 2)
                act.wait_ge(proj_done, s + 1)
                nc.scalar.activation(hT[:, :], ps[:, H_BANK:H_BANK + 2 * T], ACT.Copy).then_inc(hT_ready, 1)
                act.wait_ge(proj_done, s + 2)
                nc.scalar.activation(m.xn[:, bass.ds(s * D, D)], ps[0:T, H_BANK + 256:H_BANK + 256 + D], ACT.Copy).then_inc(stored, 1)

            def whole_step(s, p, last=False, more=True):
                soft(s)
                if not last:
                    features(s + 1)
                finish(s)
                if more:
                    stage(s + 2)

            act.sem_inc(qkv_read, 3)
            act.sem_inc(o_turned, 1)
            act.sem_inc(hT_ready, 1)
            act.sem_inc(stored, 1)
            act.sem_inc(proj_done, 1)
            stage(0)
            features(0)
            stage(1)
            with act.Fori(0, B // 2 - 1) as i:
                for u in range(2):
                    whole_step(i * 2 + u, u)
            whole_step(B - 2, 0, more=False)
            whole_step(B - 1, 1, last=True, more=False)
            finish(B)


class Turned:

    def __init__(self, nc, m, ctx, tag):
        self.nc, self.m = nc, m
        self.staged = ctx.enter_context(nc.sbuf_tensor(f"{tag}_staged", [T, 2, G * D], F32))
        self.xT = ctx.enter_context(nc.sbuf_tensor(f"{tag}_xT", [D + 1, 2, GT], F32))
        self.x_staged = ctx.enter_context(nc.semaphore(f"{tag}_x_staged"))
        self.x_turned = ctx.enter_context(nc.semaphore(f"{tag}_x_turned"))
        self.x_ready = ctx.enter_context(nc.semaphore(f"{tag}_x_ready"))
        self.x_used = ctx.enter_context(nc.semaphore(f"{tag}_x_used"))
        self.gap = ctx.enter_context(nc.semaphore(f"{tag}_gap"))
        self.ones_set = ctx.enter_context(nc.semaphore(f"{tag}_ones_set"))

    def credits(self, pool):
        self.nc.gpsimd.memset(self.xT[D:D + 1, :, :], 1.0).then_inc(self.ones_set, 1)
        pool.wait_ge(self.ones_set, 1)
        pool.sem_inc(self.x_turned, 2)
        pool.sem_inc(self.x_ready, 1)
        pool.sem_inc(self.x_used, 2)

    def copy_in(self, pool, n, u):
        pool.wait_ge(self.x_turned, n + 1)
        self.nc.gpsimd.tensor_copy(self.staged[:, u, :], self.m.xn[:, bass.ds(n * (G * D), G * D)]).then_inc(self.x_staged, 1)

    def turn(self, pe, n, u):
        pe.wait_ge(self.x_staged, n + 1)
        pe.wait_ge(self.x_ready, n + 1)
        pe.sem_inc(self.gap, 1)
        for q in range(G):
            ins = self.nc.tensor.transpose(self.m.ps[0:D, q * T:(q + 1) * T], self.staged[:, u, q * D:(q + 1) * D], self.m.ident[0:T, 0:T])
        ins.then_inc(self.x_turned, 1)
        pe.wait_ge(self.x_ready, n + 2)

    def take_out(self, act, n, u):
        act.wait_ge(self.x_turned, n + 3)
        act.wait_ge(self.x_used, n + 1)
        self.nc.scalar.activation(self.xT[0:D, u, :], self.m.ps[0:D, 0:GT], ACT.Copy).then_inc(self.x_ready, 1)

    def columns(self, u, q):
        return self.xT[:, u, q * T:(q + 1) * T]


GONE = -3.0e38
HID = 4 * D
KEPT = max(1, T // 2) - 1


def depth_ffn(nc, m, c):
    with Layer(nc) as ctx:
        w1 = ctx.enter_context(nc.sbuf_tensor("mod_w1_sb", [D, HID], F32))
        b1 = ctx.enter_context(nc.sbuf_tensor("mod_b1_sb", [128, 2], F32))
        w2 = ctx.enter_context(nc.sbuf_tensor("mod_w2_sb", [128, 2 * D], F32))
        b2 = ctx.enter_context(nc.sbuf_tensor("mod_b2_sb", [1, D], F32))
        wr = ctx.enter_context(nc.sbuf_tensor("mod_wr_sb", [T, D], F32))
        br = ctx.enter_context(nc.sbuf_tensor("mod_br_sb", [T, 1], F32))
        y = ctx.enter_context(nc.sbuf_tensor("mod_y", [T, F], F32))
        rating = ctx.enter_context(nc.sbuf_tensor("mod_rating", [T, B], F32))
        rated = ctx.enter_context(nc.sbuf_tensor("mod_rated", [T, B], F32))
        ratingT = ctx.enter_context(nc.sbuf_tensor("mod_ratingT", [B, T], F32))
        left = ctx.enter_context(nc.sbuf_tensor("mod_left", [B, T], F32))
        top = ctx.enter_context(nc.sbuf_tensor("mod_top", [B, 8], F32))
        keptT = ctx.enter_context(nc.sbuf_tensor("mod_keptT", [B, T], F32))
        kept = ctx.enter_context(nc.sbuf_tensor("mod_kept", [T, B], F32))
        g = ctx.enter_context(nc.sbuf_tensor("mod_g", [128, 2, 2, GT], F32))
        weights = ctx.enter_context(nc.semaphore("mod_weights"))
        rating_ready = ctx.enter_context(nc.semaphore("mod_rating_ready"))
        rating_turned = ctx.enter_context(nc.semaphore("mod_rating_turned"))
        kept_ready = ctx.enter_context(nc.semaphore("mod_kept_ready"))
        kept_turned = ctx.enter_context(nc.semaphore("mod_kept_turned"))
        hidden_ready = ctx.enter_context(nc.semaphore("mod_hidden_ready"))
        act_ready = ctx.enter_context(nc.semaphore("mod_act_ready"))
        y_ready = ctx.enter_context(nc.semaphore("mod_y_ready"))
        y_read = ctx.enter_context(nc.semaphore("mod_y_read"))
        steps = ctx.enter_context(nc.semaphore("mod_steps"))
        t = Turned(nc, m, ctx, "mod")
        block = ctx.block()
        ps = m.ps

        @block.sync
        def _(sp):
            sp.dma_start(w1[:, :], c["mod_w1"]).then_inc(weights, 16)
            sp.dma_start(b1[:, :], c["mod_b1"]).then_inc(weights, 16)
            sp.dma_start(w2[:, :], c["mod_w2"]).then_inc(weights, 16)
            sp.dma_start(b2[:, :], c["mod_b2"]).then_inc(weights, 16)
            sp.dma_start(wr[:, :], c["mod_wr"].broadcast_to([T, D])).then_inc(weights, 16)
            sp.dma_start(br[:, :], c["mod_br"].broadcast_to([T, 1])).then_inc(weights, 16)

        @block.gpsimd
        def _(pool):
            t.credits(pool)
            with pool.Fori(0, NG // 2) as i:
                for u in range(2):
                    t.copy_in(pool, i * 2 + u, u)

        @block.vector
        def _(dve):
            step = Chain(dve, steps)
            dve.sem_inc(y_read, 2)
            dve.wait_ge(weights, 96)
            y3 = y[:, :].rearrange("p (b d) -> p b d", d=D)
            step(nc.vector.tensor_tensor(y3, m.xn[:, 0:F].rearrange("p (b d) -> p b d", d=D), outer(wr[:, :], B), ALU.mult))
            step(nc.vector.tensor_reduce(rating[:, :], y3, X, ALU.add))
            nc.vector.tensor_scalar(rated[:, :], rating[:, :], br[:, 0:1], None, ALU.add).then_inc(rating_ready, 1)
            dve.wait_ge(rating_turned, 1)
            step(nc.vector.tensor_copy(ratingT[:, :], ps[0:B, 3584:3584 + T]))
            step(nc.vector.tensor_copy(left[:, :], ratingT[:, :]))
            for k in range(0, KEPT, 8):
                step(nc.vector.max(top[:, :], left[:, :]))
                if KEPT - k < 8:
                    step(nc.vector.memset(top[:, KEPT - k:8], GONE))
                step(nc.vector.match_replace(left[:, :], top[:, :], left[:, :], GONE))
            nc.vector.scalar_tensor_tensor(keptT[:, :], left[:, :], GONE, ratingT[:, :], ALU.is_equal, ALU.mult).then_inc(kept_ready, 1)
            dve.wait_ge(kept_turned, 1)
            step(nc.vector.tensor_copy(kept[:, :], ps[0:T, 3584:3584 + B]))
            with dve.Fori(0, NG // 2) as i:
                for u in range(2):
                    n = i * 2 + u
                    dve.wait_ge(y_ready, n + 3)
                    nc.vector.tensor_tensor(y[:, bass.ds(n * (G * D), G * D)].rearrange("p (b d) -> p b d", d=D),
                                            ps[0:T, 1536 + u * 512:1536 + u * 512 + G * D].rearrange("p (b d) -> p b d", d=D),
                                            inner(kept[:, bass.ds(n * G, G)], D), ALU.mult).then_inc(y_read, 1)
            dve.wait_ge(y_read, NG + 2)
            step(nc.vector.tensor_tensor(m.h[:, :], m.h[:, :], m.xn[:, 0:F], ALU.add))
            step(nc.vector.tensor_tensor(m.h[:, :], m.h[:, :], y[:, :], ALU.add))

        @block.tensor
        def _(pe):
            pe.sem_inc(y_ready, 2)
            pe.wait_ge(rating_ready, 1)
            nc.tensor.transpose(ps[0:B, 3584:3584 + T], rated[:, :], m.ident[0:T, 0:T]).then_inc(rating_turned, 1)
            pe.wait_ge(kept_ready, 1)
            nc.tensor.transpose(ps[0:T, 3584:3584 + B], keptT[:, :], m.ident[0:B, 0:B]).then_inc(kept_turned, 1)
            pe.wait_ge(weights, 96)
            pe.wait_ge(t.ones_set, 1)
            with pe.Fori(0, NG // 2) as i:
                for u in range(2):
                    n = i * 2 + u
                    t.turn(pe, n, u)
                    pe.wait_ge(act_ready, n + 1)
                    for k in range(2):
                        ins = nc.tensor.matmul(ps[:, 512 * (1 + k):512 * (1 + k) + GT], w1[:, k * 128:(k + 1) * 128], t.xT[0:D, u, :], start=True, stop=True)
                    ins.then_inc(hidden_ready, 1)
                    pe.wait_ge(act_ready, n + 2)
                    pe.sem_inc(t.x_used, 1)
                    pe.wait_ge(y_read, n + 1)
                    for q in range(G):
                        out = ps[0:T, 1536 + u * 512 + q * D:1536 + u * 512 + (q + 1) * D]
                        for k in range(2):
                            nc.tensor.matmul(out, g[:, u, k, q * T:(q + 1) * T], w2[:, k * D:(k + 1) * D], start=(k == 0), stop=False)
                        ins = nc.tensor.matmul(out, m.ones[0:1, 0:T], b2[0:1, :], start=False, stop=True)
                    ins.then_inc(y_ready, 1)

        @block.scalar
        def _(act):
            act.sem_inc(act_ready, 1)
            act.wait_ge(weights, 96)
            act.wait_ge(kept_turned, 1)
            with act.Fori(0, NG // 2) as i:
                for u in range(2):
                    n = i * 2 + u
                    t.take_out(act, n, u)
                    act.wait_ge(hidden_ready, n + 1)
                    act.wait_ge(y_ready, n + 1)
                    for k in range(2):
                        ins = nc.scalar.activation(g[:, u, k, :], ps[:, 512 * (1 + k):512 * (1 + k) + GT], ACT.Gelu_apprx_tanh, bias=b1[:, k:k + 1])
                    ins.then_inc(act_ready, 1)


WIN = 8
SHIFT = 4
TP = -(-T // WIN) * WIN
NWIN = B * TP // WIN
WH = 8
WD = D // WH


def window_attention(nc, m, c):
    qkv_dram = nc.dram_tensor("win_qkv_scratch", (B, TP, 3 * D), F32).ap()
    out_dram = nc.dram_tensor("win_out_scratch", (B, TP, D), F32).ap()
    window_products(nc, m, c, qkv_dram)
    window_heads(nc, m, c, qkv_dram, out_dram)
    window_projection(nc, m, c, out_dram)


def window_products(nc, m, c, qkv_dram):
    with Layer(nc) as ctx:
        w = ctx.enter_context(nc.sbuf_tensor("winp_w_sb", [D + 1, 3 * D], F32))
        out = ctx.enter_context(nc.sbuf_tensor("winp_out", [T, 2, G * 3 * D], F32))
        weights = ctx.enter_context(nc.semaphore("winp_weights"))
        padded = ctx.enter_context(nc.semaphore("winp_padded"))
        ready = ctx.enter_context(nc.semaphore("winp_ready"))
        copied = ctx.enter_context(nc.semaphore("winp_copied"))
        stored0 = ctx.enter_context(nc.semaphore("winp_stored0"))
        stored1 = ctx.enter_context(nc.semaphore("winp_stored1"))
        t = Turned(nc, m, ctx, "winp")
        block = ctx.block()
        stored = [stored0, stored1]

        @block.sync
        def _(sp):
            sp.dma_start(w[:, :], c["win_w"]).then_inc(weights, 16)
            sp.dma_start(qkv_dram[:, T - SHIFT:TP - SHIFT, :], c["win_w"][D:D + 1, :].unsqueeze(1).broadcast_to([B, TP - T, 3 * D])).then_inc(padded, 16)
            with sp.Fori(0, NG // 2) as i:
                for u in range(2):
                    n = i * 2 + u
                    sp.wait_ge(copied, n + 3)
                    to = qkv_dram[bass.ds(n * G, G), :, :]
                    src = out[:, u, :].rearrange("t (b e) -> t b e", e=3 * D)
                    sp.dma_start(to[:, 0:T - SHIFT, :].rearrange("b t e -> t b e"), src[SHIFT:T]).then_inc(stored[u], 16)
                    sp.dma_start(to[:, TP - SHIFT:TP, :].rearrange("b t e -> t b e"), src[0:SHIFT]).then_inc(stored[u], 16)
            sp.wait_ge(stored[0], 16 * NG + 1)
            sp.wait_ge(stored[1], 16 * NG + 1)
            sp.wait_ge(padded, 16)

        @block.gpsimd
        def _(pool):
            t.credits(pool)
            with pool.Fori(0, NG // 2) as i:
                for u in range(2):
                    t.copy_in(pool, i * 2 + u, u)

        @block.tensor
        def _(pe):
            pe.wait_ge(weights, 16)
            pe.wait_ge(t.ones_set, 1)
            with pe.Fori(0, NG // 2) as i:
                for u in range(2):
                    n = i * 2 + u
                    t.turn(pe, n, u)
                    pe.wait_ge(copied, n + 1)
                    for q in range(G):
                        at = 512 * (1 + 2 * u + q // 2) + (q % 2) * 3 * D
                        ins = nc.tensor.matmul(m.ps[0:T, at:at + 3 * D], t.columns(u, q), w[:, :], start=True, stop=True)
                    ins.then_inc(ready, 1)
                    pe.wait_ge(ready, n + 1)
                    pe.sem_inc(t.x_used, 1)

        @block.scalar
        def _(act):
            with act.Fori(0, NG // 2) as i:
                for u in range(2):
                    t.take_out(act, i * 2 + u, u)

        @block.vector
        def _(dve):
            dve.sem_inc(copied, 2)
            dve.sem_inc(stored0, 1)
            dve.sem_inc(stored1, 1)
            with dve.Fori(0, NG // 2) as i:
                for u in range(2):
                    n = i * 2 + u
                    dve.wait_ge(ready, n + 1)
                    dve.wait_ge(stored[u], i * 32 + 1)
                    src = m.ps[0:T, 512 * (1 + 2 * u):512 * (3 + 2 * u)].rearrange("t (k e) -> t k e", k=2)[:, :, 0:6 * D]
                    nc.vector.tensor_copy(out[:, u, :].rearrange("t (k e) -> t k e", k=2), src).then_inc(copied, 1)


def window_heads(nc, m, c, qkv_dram, out_dram):
    tiles = NWIN // 128
    SC = WH * WIN * WIN
    qkv_rows = qkv_dram.rearrange("b (w t) e -> (b w) (t e)", t=WIN)
    out_rows = out_dram.rearrange("b (w t) e -> (b w) (t e)", t=WIN)
    with Layer(nc) as ctx:
        rows = ctx.enter_context(nc.sbuf_tensor("winh_in", [128, 2, WIN * 3 * D], F32))
        bias = ctx.enter_context(nc.sbuf_tensor("winh_bias", [128, SC], F32))
        prod = ctx.enter_context(nc.sbuf_tensor("winh_prod", [128, SC * WD], F32))
        scores = ctx.enter_context(nc.sbuf_tensor("winh_scores", [128, SC], F32))
        biased = ctx.enter_context(nc.sbuf_tensor("winh_biased", [128, SC], F32))
        probs = ctx.enter_context(nc.sbuf_tensor("winh_probs", [128, SC], F32))
        most = ctx.enter_context(nc.sbuf_tensor("winh_max", [128, WH * WIN], F32))
        total = ctx.enter_context(nc.sbuf_tensor("winh_sum", [128, WH * WIN], F32))
        inv = ctx.enter_context(nc.sbuf_tensor("winh_inv", [128, WH * WIN], F32))
        out = ctx.enter_context(nc.sbuf_tensor("winh_out", [128, 2, WIN * D], F32))
        bias_loaded = ctx.enter_context(nc.semaphore("winh_bias_loaded"))
        loaded0 = ctx.enter_context(nc.semaphore("winh_loaded0"))
        loaded1 = ctx.enter_context(nc.semaphore("winh_loaded1"))
        stored0 = ctx.enter_context(nc.semaphore("winh_stored0"))
        stored1 = ctx.enter_context(nc.semaphore("winh_stored1"))
        centred = ctx.enter_context(nc.semaphore("winh_centred"))
        exp_ready = ctx.enter_context(nc.semaphore("winh_exp_ready"))
        out_ready = ctx.enter_context(nc.semaphore("winh_out_ready"))
        steps = ctx.enter_context(nc.semaphore("winh_steps"))
        block = ctx.block()
        loaded, stored = [loaded0, loaded1], [stored0, stored1]

        @block.sync
        def _(sp):
            sp.dma_start(bias[:, :], c["win_bias"].broadcast_to([128, SC])).then_inc(bias_loaded, 16)
            with sp.Fori(0, tiles // 2) as i:
                for u in range(2):
                    sp.wait_ge(out_ready, i * 2 + u + 1)
                    sp.dma_start(rows[:, u, :], qkv_rows[bass.ds((i * 2 + u) * 128, 128), :]).then_inc(loaded[u], 16)

        @block.vector
        def _(dve):
            step = Chain(dve, steps)
            dve.sem_inc(out_ready, 2)
            dve.sem_inc(stored0, 1)
            dve.sem_inc(stored1, 1)
            dve.wait_ge(bias_loaded, 16)
            N = 8
            with dve.Fori(0, tiles // 2) as i:
                step.begin(i, 2 * N)
                for u in range(2):
                    row = rows[:, u, :].rearrange("p (t s h d) -> p t s h d", t=WIN, s=3, h=WH)
                    heads = prod[:, :].rearrange("p (h a b e) -> p h a b e", h=WH, a=WIN, b=WIN)
                    dve.wait_ge(loaded[u], i * 16 + 16)
                    dve.wait_ge(out_ready, i * 2 + u + 2)
                    for hd in range(WH):
                        ins = nc.vector.tensor_tensor(heads[:, hd], outer(row[:, :, 0, hd, :], WIN, 2), outer(row[:, :, 1, hd, :], WIN, 1), ALU.mult)
                    step(ins)
                    step(nc.vector.tensor_reduce(scores[:, :], prod[:, :].rearrange("p (s e) -> p s e", e=WD), X, ALU.add))
                    step(nc.vector.scalar_tensor_tensor(biased[:, :], scores[:, :], WD ** -0.5, bias[:, :], ALU.mult, ALU.add))
                    per = lambda a: a.rearrange("p (r k) -> p r k", k=WIN)
                    step(nc.vector.tensor_reduce(most[:, :], per(biased[:, :]), X, ALU.max))
                    nc.vector.tensor_tensor(per(scores[:, :]), per(biased[:, :]), inner(most[:, :], WIN), ALU.subtract).then_inc(centred, 1)
                    dve.wait_ge(exp_ready, i * 2 + u + 1)
                    step(nc.vector.tensor_reduce(total[:, :], per(probs[:, :]), X, ALU.add))
                    step(nc.vector.reciprocal(inv[:, :], total[:, :]))
                    step(nc.vector.tensor_tensor(per(biased[:, :]), per(probs[:, :]), inner(inv[:, :], WIN), ALU.mult))
                    pr = biased[:, :].rearrange("p (h q k) -> p h q k", h=WH, q=WIN)
                    for hd in range(WH):
                        v = row[:, :, 2, hd, :].rearrange("p k d -> p d k")
                        ins = nc.vector.tensor_tensor(heads[:, hd], outer(pr[:, hd], WD, 2), outer(v, WIN, 1), ALU.mult)
                    step(ins)
                    dve.wait_ge(stored[u], i * 16 + 1)
                    nc.vector.tensor_reduce(out[:, u, :].rearrange("p (q h d) -> p h q d", h=WH, d=WD), heads, X, ALU.add).then_inc(out_ready, 1)
                step.end(tiles // 2)

        @block.scalar
        def _(act):
            with act.Fori(0, tiles // 2) as i:
                for u in range(2):
                    n = i * 2 + u
                    act.wait_ge(centred, n + 1)
                    nc.scalar.activation(probs[:, :], scores[:, :], ACT.Exp).then_inc(exp_ready, 1)
                    act.wait_ge(out_ready, n + 3)
                    act.dma_start(out_rows[bass.ds(n * 128, 128), :], out[:, u, :]).then_inc(stored[u], 16)
            act.wait_ge(stored[0], 16 * (tiles // 2) + 1)
            act.wait_ge(stored[1], 16 * (tiles // 2) + 1)


def window_projection(nc, m, c, out_dram):
    with Layer(nc) as ctx:
        w = ctx.enter_context(nc.sbuf_tensor("wino_w_sb", [D + 1, D], F32))
        weights = ctx.enter_context(nc.semaphore("wino_weights"))
        loaded = ctx.enter_context(nc.semaphore("wino_loaded"))
        ready = ctx.enter_context(nc.semaphore("wino_ready"))
        added = ctx.enter_context(nc.semaphore("wino_added"))
        t = Turned(nc, m, ctx, "wino")
        block = ctx.block()

        @block.sync
        def _(sp):
            sp.dma_start(w[:, :], c["win_proj"]).then_inc(weights, 16)
            x3 = m.xn[:, 0:F].rearrange("t (b d) -> t b d", d=D)
            sp.dma_start(x3[SHIFT:T], out_dram[:, 0:T - SHIFT, :].rearrange("b t d -> t b d")).then_inc(loaded, 16)
            sp.dma_start(x3[0:SHIFT], out_dram[:, TP - SHIFT:TP, :].rearrange("b t d -> t b d")).then_inc(loaded, 16)

        @block.gpsimd
        def _(pool):
            t.credits(pool)
            pool.wait_ge(loaded, 32)
            with pool.Fori(0, NG // 2) as i:
                for u in range(2):
                    t.copy_in(pool, i * 2 + u, u)

        @block.tensor
        def _(pe):
            pe.wait_ge(weights, 16)
            pe.wait_ge(t.ones_set, 1)
            with pe.Fori(0, NG // 2) as i:
                for u in range(2):
                    n = i * 2 + u
                    t.turn(pe, n, u)
                    pe.wait_ge(added, n + 1)
                    for q in range(G):
                        at = 512 * (1 + u) + q * D
                        ins = nc.tensor.matmul(m.ps[0:T, at:at + D], t.columns(u, q), w[:, :], start=True, stop=True)
                    ins.then_inc(ready, 1)
                    pe.wait_ge(ready, n + 1)
                    pe.sem_inc(t.x_used, 1)

        @block.scalar
        def _(act):
            with act.Fori(0, NG // 2) as i:
                for u in range(2):
                    t.take_out(act, i * 2 + u, u)

        @block.vector
        def _(dve):
            dve.sem_inc(added, 2)
            with dve.Fori(0, NG // 2) as i:
                for u in range(2):
                    n = i * 2 + u
                    dve.wait_ge(ready, n + 1)
                    group = m.h[:, bass.ds(n * (G * D), G * D)]
                    nc.vector.tensor_tensor(group, m.ps[0:T, 512 * (1 + u):512 * (1 + u) + G * D], group, ALU.add).then_inc(added, 1)


E1 = 32
H1 = D // 4
FAR = 1.0e30


def top1_experts(nc, m, c):
    CH = E1 * H1 // 128
    with Layer(nc) as ctx:
        wr = ctx.enter_context(nc.sbuf_tensor("top1_wr_sb", [D + 1, E1], F32))
        w1 = ctx.enter_context(nc.sbuf_tensor("top1_w1_sb", [D + 1, E1 * H1], F32))
        w2 = ctx.enter_context(nc.sbuf_tensor("top1_w2_sb", [128, CH * D], F32))
        b2 = ctx.enter_context(nc.sbuf_tensor("top1_b2_sb", [E1, D], F32))
        spread = ctx.enter_context(nc.sbuf_tensor("top1_spread_sb", [E1, E1 * H1], F32))
        count = ctx.enter_context(nc.sbuf_tensor("top1_count_sb", [T, E1], F32))
        logits = ctx.enter_context(nc.sbuf_tensor("top1_logits", [T, G, E1], F32))
        top = ctx.enter_context(nc.sbuf_tensor("top1_top", [T, G, 8], F32))
        at8 = ctx.enter_context(nc.sbuf_tensor("top1_at", [T, G, 8], U32))
        atf = ctx.enter_context(nc.sbuf_tensor("top1_atf", [T, G], F32))
        chosen = ctx.enter_context(nc.sbuf_tensor("top1_chosen", [T, G, E1], F32))
        chosenT = ctx.enter_context(nc.sbuf_tensor("top1_chosenT", [E1, GT], F32))
        farT = ctx.enter_context(nc.sbuf_tensor("top1_farT", [E1, GT], F32))
        hidden = ctx.enter_context(nc.sbuf_tensor("top1_hidden", [128, CH, GT], F32))
        weights = ctx.enter_context(nc.semaphore("top1_weights"))
        rated = ctx.enter_context(nc.semaphore("top1_rated"))
        chosen_ready = ctx.enter_context(nc.semaphore("top1_chosen_ready"))
        chosen_turned = ctx.enter_context(nc.semaphore("top1_chosen_turned"))
        far_ready = ctx.enter_context(nc.semaphore("top1_far_ready"))
        hidden_ready = ctx.enter_context(nc.semaphore("top1_hidden_ready"))
        relu_ready = ctx.enter_context(nc.semaphore("top1_relu_ready"))
        out_ready = ctx.enter_context(nc.semaphore("top1_out_ready"))
        added = ctx.enter_context(nc.semaphore("top1_added"))
        dve_gap = ctx.enter_context(nc.semaphore("top1_dve_gap"))
        steps = ctx.enter_context(nc.semaphore("top1_steps"))
        t = Turned(nc, m, ctx, "top1")
        block = ctx.block()
        ps = m.ps

        @block.sync
        def _(sp):
            for to, name in ((wr, "top1_wr"), (w1, "top1_w1"), (w2, "top1_w2"), (b2, "top1_b2"), (spread, "top1_spread")):
                sp.dma_start(to[:, :], c[name]).then_inc(weights, 16)
            sp.dma_start(count[:, :], c["count"][:, 0:E1].broadcast_to([T, E1])).then_inc(weights, 16)

        @block.gpsimd
        def _(pool):
            t.credits(pool)
            with pool.Fori(0, NG // 2) as i:
                for u in range(2):
                    t.copy_in(pool, i * 2 + u, u)

        @block.tensor
        def _(pe):
            pe.wait_ge(weights, 96)
            pe.wait_ge(t.ones_set, 1)
            with pe.Fori(0, NG // 2) as i:
                for u in range(2):
                    n = i * 2 + u
                    t.turn(pe, n, u)
                    pe.wait_ge(far_ready, n + 1)
                    for q in range(G):
                        ins = nc.tensor.matmul(ps[0:T, 512 + q * E1:512 + (q + 1) * E1], t.columns(u, q), wr[:, :], start=True, stop=True)
                    ins.then_inc(rated, 1)
                    pe.wait_ge(relu_ready, n + 1)
                    pe.wait_ge(chosen_ready, n + 1)
                    for q in range(G):
                        ins = nc.tensor.transpose(ps[0:E1, 1024 + q * T:1024 + (q + 1) * T], chosen[:, q, :], m.ident[0:T, 0:T])
                    ins.then_inc(chosen_turned, 1)
                    pe.wait_ge(far_ready, n + 2)
                    for k in range(CH):
                        out = ps[:, 512 * (3 + k):512 * (3 + k) + GT]
                        nc.tensor.matmul(out, w1[:, k * 128:(k + 1) * 128], t.xT[:, u, :], start=True, stop=False)
                        ins = nc.tensor.matmul(out, spread[:, k * 128:(k + 1) * 128], farT[:, :], start=False, stop=True)
                    ins.then_inc(hidden_ready, 1)
                    pe.wait_ge(relu_ready, n + 2)
                    pe.sem_inc(t.x_used, 1)
                    pe.wait_ge(added, n + 1)
                    for q in range(G):
                        out = ps[0:T, 3584 + q * D:3584 + (q + 1) * D]
                        for k in range(CH):
                            nc.tensor.matmul(out, hidden[:, k, q * T:(q + 1) * T], w2[:, k * D:(k + 1) * D], start=(k == 0), stop=False)
                        ins = nc.tensor.matmul(out, chosenT[:, q * T:(q + 1) * T], b2[:, :], start=False, stop=True)
                    ins.then_inc(out_ready, 1)

        @block.scalar
        def _(act):
            act.sem_inc(relu_ready, 1)
            with act.Fori(0, NG // 2) as i:
                for u in range(2):
                    n = i * 2 + u
                    t.take_out(act, n, u)
                    act.wait_ge(hidden_ready, n + 1)
                    act.wait_ge(out_ready, n + 1)
                    for k in range(CH):
                        ins = nc.scalar.activation(hidden[:, k, :], ps[:, 512 * (3 + k):512 * (3 + k) + GT], ACT.Relu)
                    ins.then_inc(relu_ready, 1)

        @block.vector
        def _(dve):
            step = Chain(dve, steps, dve_gap)
            dve.sem_inc(far_ready, 1)
            dve.sem_inc(added, 1)
            dve.sem_inc(out_ready, 1)
            dve.wait_ge(weights, 96)
            N = 5
            with dve.Fori(0, NG // 2) as i:
                step.begin(i, 2 * N)
                for u in range(2):
                    n = i * 2 + u
                    dve.wait_ge(rated, n + 1)
                    step(nc.vector.tensor_copy(logits[:, :, :], ps[0:T, 512:512 + G * E1].rearrange("t (q e) -> t q e", e=E1)), gap=True)
                    for q in range(G):
                        ins = nc.vector.max(top[:, q, :], logits[:, q, :])
                    step(ins, gap=True)
                    for q in range(G):
                        ins = nc.vector.max_index(at8[:, q, :], top[:, q, :], logits[:, q, :])
                    step(ins)
                    step(nc.vector.tensor_copy(atf[:, :], at8[:, :, 0]))
                    nc.vector.tensor_tensor(chosen[:, :, :], outer(count[:, :], G), inner(atf[:, :], E1), ALU.is_equal).then_inc(chosen_ready, 1)
                    dve.wait_ge(chosen_turned, n + 1)
                    dve.wait_ge(out_ready, n + 1)
                    step(nc.vector.tensor_copy(chosenT[:, :], ps[0:E1, 1024:1024 + GT]))
                    nc.vector.tensor_scalar(farT[:, :], chosenT[:, :], FAR, -FAR, ALU.mult, ALU.add).then_inc(far_ready, 1)
                    dve.wait_ge(out_ready, n + 2)
                    group = m.h[:, bass.ds(n * (G * D), G * D)]
                    nc.vector.scalar_tensor_tensor(group, ps[0:T, 3584:3584 + G * D], 0.0, group, ALU.max, ALU.add).then_inc(added, 1)
                step.end(NG // 2)


DG = 32
NGRP = D // DG
KC = T // 4


def pair_attention(nc, m, c):
    NP = G // 2
    NCH = T // KC
    with Layer(nc) as ctx:
        w = ctx.enter_context(nc.sbuf_tensor("pair_w_sb", [D, 3 * D], F32))
        mlp = ctx.enter_context(nc.sbuf_tensor("pair_mlp_sb", [128, 2 * NGRP], F32))
        b = ctx.enter_context(nc.sbuf_tensor("pair_b_sb", [T, 1], F32))
        qT = ctx.enter_context(nc.sbuf_tensor("pair_q", [128, NP, T], F32))
        kT = ctx.enter_context(nc.sbuf_tensor("pair_k", [128, NP, T], F32))
        v = ctx.enter_context(nc.sbuf_tensor("pair_v", [T, G, D], F32))
        diff = ctx.enter_context(nc.sbuf_tensor("pair_diff", [128, 2, KC * T], F32))
        scores = ctx.enter_context(nc.sbuf_tensor("pair_scores", [T, 2 * NGRP, T], F32))
        centre = ctx.enter_context(nc.sbuf_tensor("pair_centred_sb", [T, 2 * NGRP, T], F32))
        exps = ctx.enter_context(nc.sbuf_tensor("pair_exp", [T, 2 * NGRP, T], F32))
        probs = ctx.enter_context(nc.sbuf_tensor("pair_probs", [T, 2 * NGRP, T], F32))
        probsT = ctx.enter_context(nc.sbuf_tensor("pair_probsT", [T, 2 * NGRP * T], F32))
        small = ctx.enter_context(nc.sbuf_tensor("pair_small", [T, 3, 2 * NGRP], F32))
        weights = ctx.enter_context(nc.semaphore("pair_weights"))
        qk_ready = ctx.enter_context(nc.semaphore("pair_qk_ready"))
        qk_copied = ctx.enter_context(nc.semaphore("pair_qk_copied"))
        v_ready = ctx.enter_context(nc.semaphore("pair_v_ready"))
        v_copied = ctx.enter_context(nc.semaphore("pair_v_copied"))
        diff_ready = ctx.enter_context(nc.semaphore("pair_diff_ready"))
        relu_ready = ctx.enter_context(nc.semaphore("pair_relu_ready"))
        chunk_used = ctx.enter_context(nc.semaphore("pair_chunk_used"))
        scores_read = ctx.enter_context(nc.semaphore("pair_scores_read"))
        centre_ready = ctx.enter_context(nc.semaphore("pair_centre_ready"))
        exp_ready = ctx.enter_context(nc.semaphore("pair_exp_ready"))
        probs_ready = ctx.enter_context(nc.semaphore("pair_probs_ready"))
        probs_turned = ctx.enter_context(nc.semaphore("pair_probs_turned"))
        probsT_ready = ctx.enter_context(nc.semaphore("pair_probsT_ready"))
        out_ready = ctx.enter_context(nc.semaphore("pair_out_ready"))
        added = ctx.enter_context(nc.semaphore("pair_added"))
        steps = ctx.enter_context(nc.semaphore("pair_steps"))
        t = Turned(nc, m, ctx, "pair")
        block = ctx.block()
        ps = m.ps
        Q_BANK, K_BANK, V_BANK, S_BANK, T_BANK, O_BANK = 512, 1024, 1536, 2048, 3072, 3584

        @block.sync
        def _(sp):
            sp.dma_start(w[:, :], c["pair_w"]).then_inc(weights, 16)
            sp.dma_start(mlp[:, :], c["pair_mlp"]).then_inc(weights, 16)
            sp.dma_start(b[:, :], c["pair_b"].broadcast_to([T, 1])).then_inc(weights, 16)

        @block.gpsimd
        def _(pool):
            t.credits(pool)
            with pool.Fori(0, NG // 2) as i:
                for u in range(2):
                    t.copy_in(pool, i * 2 + u, u)

        @block.tensor
        def _(pe):
            pe.sem_inc(chunk_used, 2)
            pe.wait_ge(weights, 48)
            pe.wait_ge(t.ones_set, 1)
            with pe.Fori(0, NG // 2) as i:
                for u in range(2):
                    n = i * 2 + u
                    t.turn(pe, n, u)
                    pe.wait_ge(qk_copied, n + 1)
                    pe.wait_ge(v_copied, n + 1)
                    pe.sem_inc(t.gap, 1)
                    for q in range(G):
                        row, col = (q % 2) * D, (q // 2) * T
                        x = t.xT[0:D, u, q * T:(q + 1) * T]
                        nc.tensor.matmul(ps[row:row + D, Q_BANK + col:Q_BANK + col + T], w[:, 0:D], x, start=True, stop=True)
                        ins = nc.tensor.matmul(ps[row:row + D, K_BANK + col:K_BANK + col + T], w[:, D:2 * D], x, start=True, stop=True)
                    ins.then_inc(qk_ready, 1)
                    for q in range(G):
                        ins = nc.tensor.matmul(ps[0:T, V_BANK + q * D:V_BANK + (q + 1) * D], t.xT[0:D, u, q * T:(q + 1) * T], w[:, 2 * D:3 * D], start=True, stop=True)
                    ins.then_inc(v_ready, 1)
                    pe.wait_ge(v_ready, n + 1)
                    pe.sem_inc(t.x_used, 1)
                    for r in range(NP):
                        pe.wait_ge(scores_read, n * NP + r + 1)
                        for k in range(NCH):
                            at = (r * NCH + k) % 2
                            pe.wait_ge(relu_ready, n * (NP * NCH) + r * NCH + k + 1)
                            for j in range(KC):
                                col = S_BANK + 512 * r + (k * KC + j) * 2 * NGRP
                                ins = nc.tensor.matmul(ps[0:T, col:col + 2 * NGRP], diff[:, at, j * T:(j + 1) * T], mlp[:, :], start=True, stop=True)
                            ins.then_inc(chunk_used, 1)
                    for r in range(NP):
                        pe.wait_ge(probs_ready, n * NP + r + 1)
                        for a in range(2 * NGRP):
                            ins = nc.tensor.transpose(ps[0:T, T_BANK + a * T:T_BANK + (a + 1) * T], probs[:, a, :], m.ident[0:T, 0:T])
                        ins.then_inc(probs_turned, 1)
                        pe.wait_ge(probsT_ready, n * NP + r + 1)
                        pe.wait_ge(added, n * NP + r + 1)
                        for a in range(2 * NGRP):
                            s, g = a // NGRP, a % NGRP
                            ins = nc.tensor.matmul(ps[0:T, O_BANK + a * DG:O_BANK + (a + 1) * DG], probsT[:, a * T:(a + 1) * T], v[:, 2 * r + s, g * DG:(g + 1) * DG], start=True, stop=True)
                        ins.then_inc(out_ready, 1)

        @block.scalar
        def _(act):
            act.sem_inc(v_copied, 1)
            with act.Fori(0, NG // 2) as i:
                for u in range(2):
                    n = i * 2 + u
                    t.take_out(act, n, u)
                    act.wait_ge(v_ready, n + 1)
                    act.wait_ge(out_ready, n * NP + 1)
                    nc.scalar.activation(v[:, :, :], ps[0:T, V_BANK:V_BANK + G * D].rearrange("t (q d) -> t q d", d=D), ACT.Copy).then_inc(v_copied, 1)
                    for k in range(NP * NCH):
                        act.wait_ge(diff_ready, n * (NP * NCH) + k + 1)
                        nc.scalar.activation(diff[:, k % 2, :], diff[:, k % 2, :], ACT.Relu).then_inc(relu_ready, 1)
                    for r in range(NP):
                        act.wait_ge(centre_ready, n * NP + r + 1)
                        nc.scalar.activation(exps[:, :, :], centre[:, :, :], ACT.Exp).then_inc(exp_ready, 1)
                        act.wait_ge(probs_turned, n * NP + r + 2)
                        act.wait_ge(out_ready, n * NP + r + 1)
                        nc.scalar.activation(probsT[:, :], ps[0:T, T_BANK:T_BANK + 2 * NGRP * T], ACT.Copy).then_inc(probsT_ready, 1)

        @block.vector
        def _(dve):
            step = Chain(dve, steps)
            dve.sem_inc(qk_copied, 1)
            dve.sem_inc(scores_read, NP)
            dve.sem_inc(out_ready, 1)
            dve.sem_inc(probs_turned, 1)
            dve.sem_inc(added, 1)
            dve.wait_ge(weights, 48)
            N = 1 + 3 * NP
            with dve.Fori(0, NG // 2) as i:
                step.begin(i, 2 * N)
                for u in range(2):
                    n = i * 2 + u
                    dve.wait_ge(qk_ready, n + 1)
                    step(nc.vector.tensor_copy(qT[:, :, :], ps[:, Q_BANK:Q_BANK + NP * T].rearrange("p (r t) -> p r t", t=T)))
                    ins = nc.vector.tensor_copy(kT[:, :, :], ps[:, K_BANK:K_BANK + NP * T].rearrange("p (r t) -> p r t", t=T))
                    ins.then_inc(qk_copied, 1)
                    dve.wait_ge(qk_copied, n + 2)
                    for r in range(NP):
                        for k in range(NCH):
                            at = (r * NCH + k) % 2
                            dve.wait_ge(chunk_used, n * (NP * NCH) + r * NCH + k + 1)
                            nc.vector.tensor_tensor(diff[:, at, :].rearrange("p (k q) -> p k q", q=T), outer(qT[:, r, :], KC), inner(kT[:, r, k * KC:(k + 1) * KC], T), ALU.subtract).then_inc(diff_ready, 1)
                    for r in range(NP):
                        dve.wait_ge(chunk_used, n * (NP * NCH) + (r + 1) * NCH + 2)
                        ins = nc.vector.tensor_scalar(scores[:, :, :], ps[0:T, S_BANK + 512 * r:S_BANK + 512 * r + 2 * NGRP * T].rearrange("t (k a) -> t a k", a=2 * NGRP), b[:, 0:1], 0.0, ALU.add, ALU.max)
                        ins.then_inc(scores_read, 1)
                        dve.wait_ge(scores_read, n * NP + r + 1 + NP)
                        step(nc.vector.tensor_reduce(small[:, 0, :], scores[:, :, :], X, ALU.max))
                        nc.vector.tensor_tensor(centre[:, :, :], scores[:, :, :], inner(small[:, 0, :], T), ALU.subtract).then_inc(centre_ready, 1)
                        dve.wait_ge(exp_ready, n * NP + r + 1)
                        step(nc.vector.tensor_reduce(small[:, 1, :], exps[:, :, :], X, ALU.add))
                        step(nc.vector.reciprocal(small[:, 2, :], small[:, 1, :]))
                        dve.wait_ge(probs_turned, n * NP + r + 1)
                        nc.vector.tensor_tensor(probs[:, :, :], exps[:, :, :], inner(small[:, 2, :], T), ALU.mult).then_inc(probs_ready, 1)
                        dve.wait_ge(out_ready, n * NP + r + 2)
                        group = m.h[:, bass.ds((n * NP + r) * (2 * D), 2 * D)].rearrange("p (s d g) -> p s g d", s=2, g=NGRP)
                        ins = nc.vector.tensor_tensor(group, ps[0:T, O_BANK:O_BANK + 2 * D].rearrange("p (s g d) -> p s g d", s=2, g=NGRP), group, ALU.add)
                        ins.then_inc(added, 1)
                        dve.wait_ge(added, n * NP + r + 2)
                step.end(NG // 2)


E2 = 8


def gated_ffn(nc, m, c):
    with Layer(nc) as ctx:
        w1 = ctx.enter_context(nc.sbuf_tensor("gate_w1_sb", [D, HID], F32))
        b1 = ctx.enter_context(nc.sbuf_tensor("gate_b1_sb", [128, 2], F32))
        wg = ctx.enter_context(nc.sbuf_tensor("gate_wg_sb", [128, 2 * E2], F32))
        bg = ctx.enter_context(nc.sbuf_tensor("gate_bg_sb", [1, E2], F32))
        wd = ctx.enter_context(nc.sbuf_tensor("gate_wd_sb", [128, 2 * E2 * D], F32))
        bd = ctx.enter_context(nc.sbuf_tensor("gate_bd_sb", [1, E2 * D], F32))
        count = ctx.enter_context(nc.sbuf_tensor("gate_count_sb", [T, E2], F32))
        g = ctx.enter_context(nc.sbuf_tensor("gate_g", [128, 2, GT], F32))
        centre = ctx.enter_context(nc.sbuf_tensor("gate_centre", [T, G, E2], F32))
        exps = ctx.enter_context(nc.sbuf_tensor("gate_exp", [T, G, E2], F32))
        probs = ctx.enter_context(nc.sbuf_tensor("gate_probs", [T, G, E2], F32))
        top = ctx.enter_context(nc.sbuf_tensor("gate_top", [T, G, 8], F32))
        at8 = ctx.enter_context(nc.sbuf_tensor("gate_at", [T, G, 8], U32))
        atf = ctx.enter_context(nc.sbuf_tensor("gate_atf", [T, G], F32))
        small = ctx.enter_context(nc.sbuf_tensor("gate_small", [T, 3, G], F32))
        chosen = ctx.enter_context(nc.sbuf_tensor("gate_chosen", [T, G, E2], F32))
        prod = ctx.enter_context(nc.sbuf_tensor("gate_prod", [T, 2, E2 * D], F32))
        y = ctx.enter_context(nc.sbuf_tensor("gate_y", [T, G * D], F32))
        weights = ctx.enter_context(nc.semaphore("gate_weights"))
        hidden_ready = ctx.enter_context(nc.semaphore("gate_hidden_ready"))
        act_ready = ctx.enter_context(nc.semaphore("gate_act_ready"))
        rated = ctx.enter_context(nc.semaphore("gate_rated"))
        centre_ready = ctx.enter_context(nc.semaphore("gate_centre_ready"))
        exp_ready = ctx.enter_context(nc.semaphore("gate_exp_ready"))
        y_ready = ctx.enter_context(nc.semaphore("gate_y_ready"))
        y_read = ctx.enter_context(nc.semaphore("gate_y_read"))
        dve_gap = ctx.enter_context(nc.semaphore("gate_dve_gap"))
        steps = ctx.enter_context(nc.semaphore("gate_steps"))
        t = Turned(nc, m, ctx, "gate")
        block = ctx.block()
        ps = m.ps

        @block.sync
        def _(sp):
            for to, name in ((w1, "gate_w1"), (b1, "gate_b1"), (wg, "gate_wg"), (bg, "gate_bg"), (wd, "gate_wd"), (bd, "gate_bd")):
                sp.dma_start(to[:, :], c[name]).then_inc(weights, 16)
            sp.dma_start(count[:, :], c["count"][:, 0:E2].broadcast_to([T, E2])).then_inc(weights, 16)

        @block.gpsimd
        def _(pool):
            t.credits(pool)
            with pool.Fori(0, NG // 2) as i:
                for u in range(2):
                    t.copy_in(pool, i * 2 + u, u)

        @block.tensor
        def _(pe):
            pe.wait_ge(weights, 112)
            pe.wait_ge(t.ones_set, 1)
            with pe.Fori(0, NG // 2) as i:
                for u in range(2):
                    n = i * 2 + u
                    t.turn(pe, n, u)
                    pe.wait_ge(act_ready, n + 1)
                    for k in range(2):
                        ins = nc.tensor.matmul(ps[:, 512 * (1 + k):512 * (1 + k) + GT], w1[:, k * 128:(k + 1) * 128], t.xT[0:D, u, :], start=True, stop=True)
                    ins.then_inc(hidden_ready, 1)
                    pe.wait_ge(act_ready, n + 2)
                    pe.sem_inc(t.x_used, 1)
                    pe.wait_ge(centre_ready, n + 1)
                    for q in range(G):
                        out = ps[0:T, 1536 + q * E2:1536 + (q + 1) * E2]
                        for k in range(2):
                            nc.tensor.matmul(out, g[:, k, q * T:(q + 1) * T], wg[:, k * E2:(k + 1) * E2], start=(k == 0), stop=False)
                        ins = nc.tensor.matmul(out, m.ones[0:1, 0:T], bg[0:1, :], start=False, stop=True)
                    ins.then_inc(rated, 1)
                    for q in range(G):
                        pe.wait_ge(y_read, n * G + q + 1)
                        out = ps[0:T, 2048 + 512 * q:2048 + 512 * (q + 1)]
                        for k in range(2):
                            nc.tensor.matmul(out, g[:, k, q * T:(q + 1) * T], wd[:, k * E2 * D:(k + 1) * E2 * D], start=(k == 0), stop=False)
                        nc.tensor.matmul(out, m.ones[0:1, 0:T], bd[0:1, :], start=False, stop=True).then_inc(y_ready, 1)

        @block.scalar
        def _(act):
            act.sem_inc(act_ready, 1)
            act.wait_ge(weights, 112)
            with act.Fori(0, NG // 2) as i:
                for u in range(2):
                    n = i * 2 + u
                    t.take_out(act, n, u)
                    act.wait_ge(hidden_ready, n + 1)
                    act.wait_ge(y_ready, n * G + 1)
                    for k in range(2):
                        ins = nc.scalar.activation(g[:, k, :], ps[:, 512 * (1 + k):512 * (1 + k) + GT], ACT.Gelu, bias=b1[:, k:k + 1])
                    ins.then_inc(act_ready, 1)
                    act.wait_ge(centre_ready, n + 2)
                    nc.scalar.activation(exps[:, :, :], centre[:, :, :], ACT.Exp).then_inc(exp_ready, 1)

        @block.vector
        def _(dve):
            step = Chain(dve, steps, dve_gap)
            dve.sem_inc(centre_ready, 1)
            dve.sem_inc(y_ready, 1)
            dve.sem_inc(y_read, G)
            dve.wait_ge(weights, 112)
            N = 9 + G
            with dve.Fori(0, NG // 2) as i:
                step.begin(i, 2 * N)
                for u in range(2):
                    n = i * 2 + u
                    dve.wait_ge(rated, n + 1)
                    gates = ps[0:T, 1536:1536 + G * E2].rearrange("t (q e) -> t q e", e=E2)
                    step(nc.vector.tensor_reduce(small[:, 0, :], gates, X, ALU.max))
                    nc.vector.tensor_tensor(centre[:, :, :], gates, inner(small[:, 0, :], E2), ALU.subtract).then_inc(centre_ready, 1)
                    dve.wait_ge(exp_ready, n + 1)
                    step(nc.vector.tensor_reduce(small[:, 1, :], exps[:, :, :], X, ALU.add))
                    step(nc.vector.reciprocal(small[:, 2, :], small[:, 1, :]))
                    step(nc.vector.tensor_tensor(probs[:, :, :], exps[:, :, :], inner(small[:, 2, :], E2), ALU.mult), gap=True)
                    for q in range(G):
                        ins = nc.vector.max(top[:, q, :], probs[:, q, :])
                    step(ins, gap=True)
                    for q in range(G):
                        ins = nc.vector.max_index(at8[:, q, :], top[:, q, :], probs[:, q, :])
                    step(ins)
                    step(nc.vector.tensor_copy(atf[:, :], at8[:, :, 0]))
                    step(nc.vector.tensor_tensor(chosen[:, :, :], outer(count[:, :], G), inner(atf[:, :], E2), ALU.is_equal))
                    step(nc.vector.tensor_tensor(chosen[:, :, :], chosen[:, :, :], probs[:, :, :], ALU.mult))
                    for q in range(G):
                        dve.wait_ge(y_ready, n * G + q + 2)
                        ins = nc.vector.tensor_tensor(prod[:, q % 2, :].rearrange("t (e d) -> t e d", d=D), ps[0:T, 2048 + 512 * q:2048 + 512 * (q + 1)].rearrange("t (e d) -> t e d", d=D), inner(chosen[:, q, :], D), ALU.mult)
                        ins.then_inc(y_read, 1)
                        dve.wait_ge(y_read, n * G + q + 1 + G)
                        step(nc.vector.tensor_reduce(y[:, q * D:(q + 1) * D], prod[:, q % 2, :].rearrange("t (e d) -> t d e", d=D), X, ALU.add))
                    group = m.h[:, bass.ds(n * (G * D), G * D)]
                    nc.vector.tensor_tensor(group, group, y[:, :], ALU.add)
                step.end(NG // 2)


def top2_experts(nc, m, c):
    with Layer(nc) as ctx:
        wg = ctx.enter_context(nc.sbuf_tensor("moe_wg_sb", [D + 1, E2], F32))
        w1 = ctx.enter_context(nc.sbuf_tensor("moe_w1_sb", [D, E2 * HID], F32))
        b1 = ctx.enter_context(nc.sbuf_tensor("moe_b1_sb", [128, 2 * E2], F32))
        w2 = ctx.enter_context(nc.sbuf_tensor("moe_w2_sb", [128, 2 * E2 * D], F32))
        b2 = ctx.enter_context(nc.sbuf_tensor("moe_b2_sb", [1, E2 * D], F32))
        count = ctx.enter_context(nc.sbuf_tensor("moe_count_sb", [T, E2], F32))
        g = ctx.enter_context(nc.sbuf_tensor("moe_g", [128, 2, 2, GT], F32))
        gates = ctx.enter_context(nc.sbuf_tensor("moe_gates", [T, G, E2], F32))
        centre = ctx.enter_context(nc.sbuf_tensor("moe_centre", [T, G, E2], F32))
        exps = ctx.enter_context(nc.sbuf_tensor("moe_exp", [T, G, E2], F32))
        top = ctx.enter_context(nc.sbuf_tensor("moe_top", [T, G, 8], F32))
        at8 = ctx.enter_context(nc.sbuf_tensor("moe_at", [T, G, 8], U32))
        atf = ctx.enter_context(nc.sbuf_tensor("moe_atf", [T, G, 2], F32))
        first = ctx.enter_context(nc.sbuf_tensor("moe_first", [T, G, E2], F32))
        second = ctx.enter_context(nc.sbuf_tensor("moe_second", [T, G, E2], F32))
        small = ctx.enter_context(nc.sbuf_tensor("moe_small", [T, 2, G], F32))
        share = ctx.enter_context(nc.sbuf_tensor("moe_share", [T, G, E2], F32))
        prod = ctx.enter_context(nc.sbuf_tensor("moe_prod", [T, G * D], F32))
        acc = ctx.enter_context(nc.sbuf_tensor("moe_acc", [T, G * D], F32))
        weights = ctx.enter_context(nc.semaphore("moe_weights"))
        rated = ctx.enter_context(nc.semaphore("moe_rated"))
        gates_read = ctx.enter_context(nc.semaphore("moe_gates_read"))
        centre_ready = ctx.enter_context(nc.semaphore("moe_centre_ready"))
        exp_ready = ctx.enter_context(nc.semaphore("moe_exp_ready"))
        hidden_ready = ctx.enter_context(nc.semaphore("moe_hidden_ready"))
        act_ready = ctx.enter_context(nc.semaphore("moe_act_ready"))
        y_ready = ctx.enter_context(nc.semaphore("moe_y_ready"))
        y_read = ctx.enter_context(nc.semaphore("moe_y_read"))
        dve_gap = ctx.enter_context(nc.semaphore("moe_dve_gap"))
        steps = ctx.enter_context(nc.semaphore("moe_steps"))
        t = Turned(nc, m, ctx, "moe")
        block = ctx.block()
        ps = m.ps

        @block.sync
        def _(sp):
            for to, name in ((wg, "moe_wg"), (w1, "moe_w1"), (b1, "moe_b1"), (w2, "moe_w2"), (b2, "moe_b2")):
                sp.dma_start(to[:, :], c[name]).then_inc(weights, 16)
            sp.dma_start(count[:, :], c["count"][:, 0:E2].broadcast_to([T, E2])).then_inc(weights, 16)

        @block.gpsimd
        def _(pool):
            t.credits(pool)
            with pool.Fori(0, NG // 2) as i:
                for u in range(2):
                    t.copy_in(pool, i * 2 + u, u)

        @block.tensor
        def _(pe):
            def hidden(n, u, e):
                pe.wait_ge(act_ready, n * E2 + e + 1)
                for k in range(2):
                    at = 1024 + (e % 2) * 1024 + 512 * k
                    ins = nc.tensor.matmul(ps[:, at:at + GT], w1[:, e * HID + k * 128:e * HID + (k + 1) * 128], t.xT[0:D, u, :], start=True, stop=True)
                ins.then_inc(hidden_ready, 1)

            def output(n, u, e):
                pe.wait_ge(act_ready, n * E2 + e + 3)
                pe.wait_ge(y_read, n * E2 + e + 1)
                for q in range(G):
                    at = 3072 + 512 * (e % 2) + q * D
                    for k in range(2):
                        nc.tensor.matmul(ps[0:T, at:at + D], g[:, e % 2, k, q * T:(q + 1) * T], w2[:, (2 * e + k) * D:(2 * e + k + 1) * D], start=(k == 0), stop=False)
                    ins = nc.tensor.matmul(ps[0:T, at:at + D], m.ones[0:1, 0:T], b2[0:1, e * D:(e + 1) * D], start=False, stop=True)
                ins.then_inc(y_ready, 1)

            pe.wait_ge(weights, 96)
            pe.wait_ge(t.ones_set, 1)
            with pe.Fori(0, NG // 2) as i:
                for u in range(2):
                    n = i * 2 + u
                    t.turn(pe, n, u)
                    pe.wait_ge(gates_read, n + 1)
                    for q in range(G):
                        ins = nc.tensor.matmul(ps[0:T, 512 + q * E2:512 + (q + 1) * E2], t.columns(u, q), wg[:, :], start=True, stop=True)
                    ins.then_inc(rated, 1)
                    hidden(n, u, 0)
                    for e in range(E2):
                        if e + 1 < E2:
                            hidden(n, u, e + 1)
                        output(n, u, e)
                    pe.sem_inc(t.x_used, 1)

        @block.scalar
        def _(act):
            act.sem_inc(act_ready, 2)
            act.wait_ge(weights, 96)
            with act.Fori(0, NG // 2) as i:
                for u in range(2):
                    n = i * 2 + u
                    t.take_out(act, n, u)
                    act.wait_ge(centre_ready, n + 1)
                    nc.scalar.activation(exps[:, :, :], centre[:, :, :], ACT.Exp).then_inc(exp_ready, 1)
                    for e in range(E2):
                        act.wait_ge(hidden_ready, n * E2 + e + 1)
                        act.wait_ge(y_ready, n * E2 + e + 1)
                        for k in range(2):
                            at = 1024 + (e % 2) * 1024 + 512 * k
                            ins = nc.scalar.activation(g[:, e % 2, k, :], ps[:, at:at + GT], ACT.Gelu, bias=b1[:, 2 * e + k:2 * e + k + 1])
                        ins.then_inc(act_ready, 1)

        @block.vector
        def _(dve):
            step = Chain(dve, steps, dve_gap)
            dve.sem_inc(gates_read, 1)
            dve.sem_inc(y_ready, 2)
            dve.sem_inc(y_read, 2)
            dve.wait_ge(weights, 96)
            N = 10 + E2
            with dve.Fori(0, NG // 2) as i:
                step.begin(i, 2 * N)
                for u in range(2):
                    n = i * 2 + u
                    dve.wait_ge(rated, n + 1)
                    nc.vector.tensor_copy(gates[:, :, :], ps[0:T, 512:512 + G * E2].rearrange("t (q e) -> t q e", e=E2)).then_inc(gates_read, 1)
                    dve.wait_ge(gates_read, n + 2)
                    dve.sem_inc(dve_gap, 1)
                    for q in range(G):
                        ins = nc.vector.max(top[:, q, :], gates[:, q, :])
                    step(ins, gap=True)
                    nc.vector.tensor_tensor(centre[:, :, :], gates[:, :, :], inner(top[:, :, 0], E2), ALU.subtract).then_inc(centre_ready, 1)
                    for q in range(G):
                        ins = nc.vector.max_index(at8[:, q, :], top[:, q, :], gates[:, q, :])
                    step(ins)
                    step(nc.vector.tensor_copy(atf[:, :, :], at8[:, :, 0:2]))
                    nc.vector.tensor_tensor(first[:, :, :], outer(count[:, :], G), inner(atf[:, :, 0], E2), ALU.is_equal)
                    step(nc.vector.tensor_tensor(second[:, :, :], outer(count[:, :], G), inner(atf[:, :, 1], E2), ALU.is_equal))
                    step(nc.vector.tensor_tensor(first[:, :, :], first[:, :, :], second[:, :, :], ALU.add))
                    dve.wait_ge(exp_ready, n + 1)
                    step(nc.vector.tensor_tensor(first[:, :, :], first[:, :, :], exps[:, :, :], ALU.mult))
                    step(nc.vector.tensor_reduce(small[:, 0, :], first[:, :, :], X, ALU.add))
                    step(nc.vector.reciprocal(small[:, 1, :], small[:, 0, :]))
                    step(nc.vector.tensor_tensor(share[:, :, :], first[:, :, :], inner(small[:, 1, :], E2), ALU.mult))
                    for e in range(E2):
                        dve.wait_ge(y_ready, n * E2 + e + 3)
                        v = ps[0:T, 3072 + 512 * (e % 2):3072 + 512 * (e % 2) + G * D].rearrange("t (q d) -> t q d", d=D)
                        to = acc if e == 0 else prod
                        ins = nc.vector.tensor_tensor(to[:, :].rearrange("t (q d) -> t q d", d=D), v, inner(share[:, :, e], D), ALU.mult)
                        ins.then_inc(y_read, 1)
                        dve.wait_ge(y_read, n * E2 + e + 3)
                        if e:
                            step(nc.vector.tensor_tensor(acc[:, :], acc[:, :], prod[:, :], ALU.add))
                    group = m.h[:, bass.ds(n * (G * D), G * D)]
                    step(nc.vector.tensor_tensor(group, group, acc[:, :], ALU.add))
                    step(nc.vector.memset(prod[:, 0:1], 0.0))
                step.end(NG // 2)


BR = 4
KM = 15
KS = 16
REL = KM + 2
NS = BR * T
SB = 7
NB = 56
NBR = -(-NS // SB)
SP_ = NB * SB
RB_ = SB * REL
CB = SB * KM
SUP = 4
SW = SUP * CB
OUTS = 3 * NB // SUP
PH = 16
RH = 64
SILU = float(np.pi / np.sqrt(3.0))
MASKED = -1.0e30
CUT = [(0, 31), (31, 62), (62, 92)]
NQ = -(-NBR // SUP)
QW = SUP * SB * PH
HALF = NQ // 2


def palette_attention(nc, m, c):
    with Layer(nc) as ctx:
        w = ctx.enter_context(nc.sbuf_tensor("pal_w_sb", [D, (BR + 1) * D], F32))
        turn = ctx.enter_context(nc.sbuf_tensor("pal_turn_sb", [T, 2 * D], F32))
        causal = ctx.enter_context(nc.sbuf_tensor("pal_causal_sb", [T, T], F32))
        shift = ctx.enter_context(nc.sbuf_tensor("pal_shift_sb", [T, KS], F32))
        age = ctx.enter_context(nc.sbuf_tensor("pal_age_sb", [T, NS], F32))
        key = ctx.enter_context(nc.sbuf_tensor("pal_key_sb", [T, 1], F32))
        pick = ctx.enter_context(nc.sbuf_tensor("pal_pick_sb", [BR * KS, KM], F32))
        rowsf = ctx.enter_context(nc.sbuf_tensor("pal_rows_sb", [BR * KS, BR * T], F32))
        rows = ctx.enter_context(nc.sbuf_tensor("pal_rows16", [BR * KS, BR * T], BF16))
        own = ctx.enter_context(nc.sbuf_tensor("pal_own_sb", [RB_, SW], F32))
        w1 = ctx.enter_context(nc.sbuf_tensor("pal_w1_sb", [RB_, RH], F32))
        b1 = ctx.enter_context(nc.sbuf_tensor("pal_b1_sb", [128, 1], F32))
        b1s = ctx.enter_context(nc.sbuf_tensor("pal_b1s", [128, 1], F32))
        w2T = ctx.enter_context(nc.sbuf_tensor("pal_w2T_sb", [RH, RH], F32))
        b2 = ctx.enter_context(nc.sbuf_tensor("pal_b2_sb", [RH, CB], F32))
        wcm = ctx.enter_context(nc.sbuf_tensor("pal_wcm_sb", [RH, 3], F32))
        bcm = ctx.enter_context(nc.sbuf_tensor("pal_bcm_sb", [CB, 3], F32))
        heads = ctx.enter_context(nc.sbuf_tensor("pal_heads", [128, NB // SUP // 2, OUTS], F32))
        hbias = ctx.enter_context(nc.sbuf_tensor("pal_hbias", [CB, 3], F32))
        soft = ctx.enter_context(nc.sbuf_tensor("pal_soft_sb", [NB, CB], F32))
        grid = ctx.enter_context(nc.sbuf_tensor("pal_grid_sb", [CB, PH], F32))
        site = ctx.enter_context(nc.sbuf_tensor("pal_site_sb", [CB, SB], F32))
        palette = ctx.enter_context(nc.sbuf_tensor("pal_palette_sb", [PH, PH * D], F32))
        wo = ctx.enter_context(nc.sbuf_tensor("pal_wo_sb", [D, BR * D], F32))
        x = ctx.enter_context(nc.sbuf_tensor("pal_x", [T, D], F32))
        xT = ctx.enter_context(nc.sbuf_tensor("pal_xT", [D, T], F32))
        ta = ctx.enter_context(nc.sbuf_tensor("pal_ta", [T, BR + 1, D], F32))
        tb = ctx.enter_context(nc.sbuf_tensor("pal_tb", [T, BR + 1, D], F32))
        ip = ctx.enter_context(nc.sbuf_tensor("pal_ip", [T, 2, (BR + 1) * D], F32))
        n2 = ctx.enter_context(nc.sbuf_tensor("pal_n2", [T, 4, BR + 1], F32))
        ipT = ctx.enter_context(nc.sbuf_tensor("pal_ipT", [D, 2, (BR + 1) * T], F32))
        logits = ctx.enter_context(nc.sbuf_tensor("pal_logits", [T, BR, T], F32))
        gram = ctx.enter_context(nc.sbuf_tensor("pal_gram", [T, T], F32))
        top = ctx.enter_context(nc.sbuf_tensor("pal_top", [T, BR, KS], F32))
        at = ctx.enter_context(nc.sbuf_tensor("pal_at", [T, BR, KS], U32))
        atf = ctx.enter_context(nc.sbuf_tensor("pal_atf", [T, BR, KS], F32))
        spread = ctx.enter_context(nc.sbuf_tensor("pal_spread", [BR * KS, T * KM], BF16))
        onehot = ctx.enter_context(nc.sbuf_tensor("pal_onehot", [T, 2, SP_ * KM], F32))
        rext = ctx.enter_context(nc.sbuf_tensor("pal_rext", [T, 2, SP_, REL], F32))
        rel = ctx.enter_context(nc.sbuf_tensor("pal_rel", [RB_, 2, SW], F32))
        hid = ctx.enter_context(nc.sbuf_tensor("pal_act", [128, 2, SW], F32))
        outs = ctx.enter_context(nc.sbuf_tensor("pal_outs", [OUTS, SW], F32))
        z = ctx.enter_context(nc.sbuf_tensor("pal_z", [CB, 2, NB], F32))
        g = ctx.enter_context(nc.sbuf_tensor("pal_g", [CB, 2, NB], F32))
        mix = ctx.enter_context(nc.sbuf_tensor("pal_mix", [CB, NB], F32))
        mixT = ctx.enter_context(nc.sbuf_tensor("pal_mixT", [NB, 4, CB], F32))
        msum = ctx.enter_context(nc.sbuf_tensor("pal_msum", [NB, 3, SB], F32))
        hat = ctx.enter_context(nc.sbuf_tensor("pal_hat", [CB, 2, NB * PH], F32))
        across = ctx.enter_context(nc.sbuf_tensor("pal_across", [CB, 2, QW], F32))
        share = ctx.enter_context(nc.sbuf_tensor("pal_share", [PH, HALF * QW], F32))
        vT = ctx.enter_context(nc.sbuf_tensor("pal_vT", [D, NS], F32))
        def sem(name):
            return ctx.enter_context(nc.semaphore("pal_" + name))

        weights, set_up, zeroed = sem("weights"), sem("set_up"), sem("zeroed")
        x_staged, x_turned, xT_ready = sem("x_staged"), sem("x_turned"), sem("xT_ready")
        ip_made, ip_squared, n_ready, ip_ready = sem("ip_made"), sem("ip_squared"), sem("n_ready"), sem("ip_ready")
        ip_turned, ipT_ready, products = sem("ip_turned"), sem("ipT_ready"), sem("products")
        at_ready, at_turned, spread_ready = sem("at_ready"), sem("at_turned"), sem("spread_ready")
        keys_spread, onehot_ready, gathered, rext_ready = sem("keys_spread"), sem("onehot_ready"), sem("gathered"), sem("rext_ready")
        related, rel_ready, hidden_ready, act_ready = sem("related"), sem("rel_ready"), sem("hidden_ready"), sem("act_ready")
        outs_ready, outs_turned = sem("outs_ready"), sem("outs_turned")
        placed, z_ready, mix_ready, mix_turned = sem("placed"), sem("z_ready"), sem("mix_ready"), sem("mix_turned")
        mix_centred, mix_exp, shares_ready, shares_turned = sem("mix_centred"), sem("mix_exp"), sem("shares_ready"), sem("shares_turned")
        away, hat_ready, across_ready, crossed = sem("away"), sem("hat_ready"), sem("across_ready"), sem("crossed")
        share_copied, v_ready, vT_ready, y_ready, added = sem("share_copied"), sem("v_ready"), sem("vT_ready"), sem("y_ready"), sem("added")
        hats_ready = sem("hats_ready")
        steps, dve_gap, pe_gap = sem("steps"), sem("dve_gap"), sem("pe_gap")
        block = ctx.block()
        ps = m.ps
        BANK = [512 * k for k in range(8)]
        NCUT = BR * len(CUT)
        NSUP = NB // SUP
        loads = [(w, "pal_w"), (turn, "pal_turn"), (causal, "pal_causal"), (shift, "pal_shift"), (age, "pal_age"),
                 (key, "pal_key"), (pick, "pal_pick"), (rowsf, "pal_rows"), (own, "pal_own"), (w1, "pal_w1"),
                 (b1, "pal_b1"), (w2T, "pal_w2T"), (b2, "pal_b2"), (wcm, "pal_wcm"), (bcm, "pal_bcm"),
                 (soft, "pal_soft"), (grid, "pal_grid"), (site, "pal_site"), (palette, "pal_palette"), (wo, "pal_wo")]
        LOADED = 16 * len(loads)

        def blocks(q):
            return range(q * SUP, min((q + 1) * SUP, NBR))

        def sites(r, cut):
            lo, hi = r * T + cut[0], r * T + cut[1]
            return lo, hi, lo * KM, hi * KM

        @block.sync
        def _(sp):
            for to, name in loads:
                sp.dma_start(to[:, :], c[name]).then_inc(weights, 16)

        @block.tensor
        def _(pe):
            pe.wait_ge(weights, LOADED)
            nc.tensor.matmul(ps[0:RH, BANK[0]:BANK[0] + 3], w2T[:, :], wcm[:, :], start=True, stop=True)
            nc.tensor.matmul(ps[RH:128, BANK[0]:BANK[0] + 3], w2T[:, :], wcm[:, :], start=True, stop=True)
            nc.tensor.matmul(ps[0:CB, BANK[1]:BANK[1] + 3], b2[:, :], wcm[:, :], start=True, stop=True).then_inc(set_up, 1)
            pe.wait_ge(zeroed, 1)


            def turn_x(n):
                pe.wait_ge(x_staged, n + 1)
                pe.sem_inc(pe_gap, 1)
                nc.tensor.transpose(ps[0:D, BANK[0]:BANK[0] + T], x[:, :], m.ident[0:T, 0:T]).then_inc(x_turned, 1)

            def project(n):
                pe.wait_ge(xT_ready, n + 1)
                nc.tensor.matmul(ps[0:T, BANK[1]:BANK[1] + (BR + 1) * D], xT[:, :], w[:, :], start=True, stop=True).then_inc(ip_made, 1)

            def turn_rotated(n):
                pe.wait_ge(ip_ready, n + 1)
                pe.sem_inc(pe_gap, 1)
                for k in range(2):
                    for r in range(BR + 1):
                        ins = nc.tensor.transpose(ps[0:D, BANK[k] + r * T:BANK[k] + (r + 1) * T], ip[:, k, r * D:(r + 1) * D], m.ident[0:T, 0:T])
                ins.then_inc(ip_turned, 1)

            def key_products(n):
                pe.wait_ge(ipT_ready, n + 1)
                for r in range(BR):
                    nc.tensor.matmul(ps[0:T, BANK[0] + r * T:BANK[0] + (r + 1) * T], ipT[:, 0, r * T:(r + 1) * T], ipT[:, 0, BR * T:], start=True, stop=True)
                nc.tensor.matmul(ps[0:T, BANK[1]:BANK[1] + (BR + 1) * T], ipT[:, 1, BR * T:], ipT[:, 1, :], start=True, stop=True).then_inc(products, 1)

            def turn_indices(n):
                pe.wait_ge(at_ready, n + 1)
                pe.sem_inc(pe_gap, 1)
                nc.tensor.transpose(ps[0:BR * KS, BANK[0]:BANK[0] + T], atf[:, :, :].rearrange("t r k -> t (r k)"), m.ident[0:T, 0:T]).then_inc(at_turned, 1)

            def spread_keys(n, j):
                lo, hi = CUT[j % 3]
                if j >= 2:
                    pe.wait_ge(onehot_ready, n * NCUT + j - 1)
                nc.tensor.matmul(ps[0:T, BANK[2 + j % 2]:BANK[2 + j % 2] + (hi - lo) * KM], rows[:, (j // 3) * T:(j // 3 + 1) * T], spread[:, lo * KM:hi * KM], start=True, stop=True).then_inc(keys_spread, 1)

            def gather(n, p, j):
                _, _, a0, b0 = sites(j // 3, CUT[j % 3])
                pe.wait_ge(onehot_ready, n * NCUT + j + 1)
                if j >= 2:
                    pe.wait_ge(rext_ready, n * NCUT + j - 1)
                nc.tensor.matmul(ps[0:T, BANK[4 + j % 2]:BANK[4 + j % 2] + b0 - a0], gram[:, :], onehot[:, p, a0:b0], start=True, stop=True).then_inc(gathered, 1)

            def relate(n, p, s):
                if s >= 2:
                    pe.wait_ge(rel_ready, n * NSUP + s - 1)
                for k in range(SUP):
                    b = s * SUP + k
                    ins = nc.tensor.matmul(ps[0:RB_, BANK[6 + s % 2] + k * CB:BANK[6 + s % 2] + (k + 1) * CB], rext[:, p, b * SB:(b + 1) * SB, :].rearrange("t s f -> t (s f)"), onehot[:, p, b * CB:(b + 1) * CB], start=True, stop=True)
                ins.then_inc(related, 1)

            def hidden(n, s):
                pe.wait_ge(rel_ready, n * NSUP + s + 1)
                pair, half = s // 2, s % 2
                if s >= 4 and half == 0:
                    pe.wait_ge(act_ready, n * (NSUP // 2) + pair - 1)
                pe.sem_inc(pe_gap, 1)
                nc.tensor.matmul(ps[half * RH:(half + 1) * RH, BANK[4 + pair % 2]:BANK[4 + pair % 2] + SW], w1[:, :], rel[:, s % 2, :], start=True, stop=True).then_inc(hidden_ready, 1)

            def place(n, pair):
                pe.wait_ge(act_ready, n * (NSUP // 2) + pair + 1)
                nc.tensor.matmul(ps[0:OUTS, BANK[3]:BANK[3] + SW], heads[:, pair, :], hid[:, pair % 2, :], start=(pair == 0), stop=(pair == NSUP // 2 - 1)).then_inc(placed, 1)

            def turn_outputs(n):
                pe.wait_ge(outs_ready, n + 1)
                pe.sem_inc(pe_gap, 1)
                for k in range(SUP):
                    ins = nc.tensor.transpose(ps[0:CB, BANK[3] + k * OUTS:BANK[3] + (k + 1) * OUTS], outs[:, k * CB:(k + 1) * CB], m.ident[0:OUTS, 0:OUTS])
                ins.then_inc(outs_turned, 1)

            FRONT = {0: turn_x, 1: project, 5: turn_rotated, 7: key_products, NSUP - 1: turn_indices}

            def relations(n, p, last):
                pe.wait_ge(rext_ready, (n + 1) * NCUT)
                relate(n, p, 0)
                for s in range(NSUP):
                    if s + 1 < NSUP:
                        relate(n, p, s + 1)
                    hidden(n, s)
                    if s % 2 == 1 and s >= 3:
                        place(n, s // 2 - 1)
                    if not last and s in FRONT:
                        FRONT[s](n + 1)
                place(n, NSUP // 2 - 1)
                turn_outputs(n)

            def turn_mix(n):
                pe.wait_ge(mix_ready, n + 1)
                pe.sem_inc(pe_gap, 1)
                nc.tensor.transpose(ps[0:NB, BANK[0]:BANK[0] + CB], mix[:, :], m.ident[0:CB, 0:CB]).then_inc(mix_turned, 1)

            def turn_shares(n):
                pe.wait_ge(shares_ready, n + 1)
                pe.sem_inc(pe_gap, 1)
                nc.tensor.transpose(ps[0:CB, BANK[1]:BANK[1] + NB], mixT[:, 3, :], m.ident[0:NB, 0:NB]).then_inc(shares_turned, 1)

            def keep(n, p, before=True):
                pe.wait_ge(spread_ready, n + 1)
                spread_keys(n, 0)
                for j in range(NCUT):
                    if j == 0 and before:
                        pe.wait_ge(mix_ready, n)
                    if j + 1 < NCUT:
                        spread_keys(n, j + 1)
                    if j == 0 and before:
                        turn_mix(n - 1)
                    gather(n, p, j)
                    if j == 8 and before:
                        turn_shares(n - 1)
                pe.wait_ge(rext_ready, (n + 1) * NCUT)

            def palette_sum(n, half):
                pe.wait_ge(share_copied, n * NQ + (half + 1) * HALF)
                first, last = half * HALF * SUP * SB, min((half + 1) * HALF * SUP, NBR) * SB
                by_column = share[:, 0:(last - first) * PH].rearrange("p (s x) -> p s x", x=PH)
                for col in range(PH):
                    ins = nc.tensor.matmul(ps[0:D, BANK[2] + first:BANK[2] + last], palette[:, col * D:(col + 1) * D], by_column[:, :, col], start=(col == 0), stop=(col == PH - 1))
                ins.then_inc(v_ready, 1)

            def sample(n):
                for q in range(NQ):
                    pe.wait_ge(across_ready, n * NQ + q + 1)
                    if q >= 2:
                        pe.wait_ge(share_copied, n * NQ + q - 1)
                    for j, b in enumerate(blocks(q)):
                        at_ = BANK[4 + q % 2] + j * SB * PH
                        ins = nc.tensor.matmul(ps[0:PH, at_:at_ + SB * PH], hat[:, 1, b * PH:(b + 1) * PH], across[:, q % 2, j * SB * PH:(j + 1) * SB * PH], start=True, stop=True)
                    ins.then_inc(crossed, 1)
                    if q == HALF + 1:
                        palette_sum(n, 0)
                palette_sum(n, 1)
                pe.wait_ge(vT_ready, n + 1)
                for r in range(BR):
                    ins = nc.tensor.matmul(ps[0:T, BANK[2]:BANK[2] + D], vT[:, r * T:(r + 1) * T], wo[:, r * D:(r + 1) * D], start=(r == 0), stop=(r == BR - 1))
                ins.then_inc(y_ready, 1)

            def sequence(n, p, last=False):
                relations(n, p, last)
                if last:
                    turn_mix(n)
                    turn_shares(n)
                else:
                    keep(n + 1, 1 - p)
                sample(n)
                pe.wait_ge(added, n + 1)

            for k in sorted(FRONT):
                FRONT[k](0)
            keep(0, 0, before=False)
            with pe.Fori(0, B // 2 - 1) as i:
                for u in range(2):
                    sequence(i * 2 + u, u)
            sequence(B - 2, 0)
            sequence(B - 1, 1, last=True)

        @block.scalar
        def _(act):
            act.wait_ge(weights, LOADED)
            nc.scalar.activation(b1s[:, :], b1[:, :], ACT.Copy, scale=SILU).then_inc(set_up, 1)
            act.wait_ge(set_up, 3)

            def stage_x(n):
                nc.scalar.activation(x[:, :], m.xn[:, bass.ds(n * D, D)], ACT.Copy).then_inc(x_staged, 1)

            def take_xT(n):
                act.wait_ge(x_turned, n + 1)
                nc.scalar.activation(xT[:, :], ps[0:D, BANK[0]:BANK[0] + T], ACT.Copy).then_inc(xT_ready, 1)

            def lengths(n):
                act.wait_ge(ip_squared, n + 1)
                nc.scalar.activation(n2[:, 1, :], n2[:, 0, :], ACT.Sqrt).then_inc(n_ready, 1)

            def take_turned(n):
                act.wait_ge(ip_turned, n + 1)
                for k in range(2):
                    ins = nc.scalar.activation(ipT[:, k, :], ps[0:D, BANK[k]:BANK[k] + (BR + 1) * T], ACT.Copy)
                ins.then_inc(ipT_ready, 1)

            def take_rows(n, p, j):
                lo, hi, a0, b0 = sites(j // 3, CUT[j % 3])
                act.wait_ge(gathered, n * NCUT + j + 1)
                nc.scalar.activation(rext[:, p, lo:hi, 0:KM], ps[0:T, BANK[4 + j % 2]:BANK[4 + j % 2] + b0 - a0].rearrange("t (s k) -> t s k", k=KM), ACT.Copy).then_inc(rext_ready, 1)

            FRONT = {0: take_xT, 1: lengths, 2: take_turned}

            def activations(n, last):
                if not last:
                    stage_x(n + 1)
                for pair in range(NSUP // 2):
                    act.wait_ge(hidden_ready, n * NSUP + 2 * pair + 2)
                    if pair >= 2:
                        act.wait_ge(placed, n * (NSUP // 2) + pair - 1)
                    nc.scalar.activation(hid[:, pair % 2, :], ps[:, BANK[4 + pair % 2]:BANK[4 + pair % 2] + SW], ACT.Silu, bias=b1s[:, 0:1], scale=SILU).then_inc(act_ready, 1)
                    if not last and pair in FRONT:
                        FRONT[pair](n + 1)

            def positions(n):
                act.wait_ge(placed, (n + 1) * (NSUP // 2))
                nc.scalar.activation(outs[:, :], ps[0:OUTS, BANK[3]:BANK[3] + SW], ACT.Copy).then_inc(outs_ready, 1)
                act.wait_ge(outs_turned, n + 1)
                out = ps[0:CB, BANK[3]:BANK[3] + SUP * OUTS].rearrange("p (k q h c) -> p c q h k", k=SUP, h=2, c=3)
                for k in range(2):
                    ins = nc.scalar.activation(z[:, k, :].rearrange("p (q h k) -> p q h k", h=2, k=SUP), out[:, k], ACT.Tanh, bias=hbias[:, k:k + 1])
                ins.then_inc(z_ready, 1)
                nc.scalar.activation(mix[:, :].rearrange("p (q h k) -> p q h k", h=2, k=SUP), out[:, 2], ACT.Identity, bias=hbias[:, 2:3]).then_inc(mix_ready, 1)

            def hats(n):
                act.wait_ge(away, n + 1)
                nc.scalar.activation(hat[:, :, :], hat[:, :, :], ACT.Abs).then_inc(hat_ready, 1)
                act.wait_ge(hat_ready, 2 * n + 1)
                nc.scalar.activation(hat[:, :, :], hat[:, :, :], ACT.Relu, bias=1.0, scale=-1.0).then_inc(hat_ready, 1)

            def mix_exps(n):
                act.wait_ge(mix_centred, n + 1)
                nc.scalar.activation(mixT[:, 2, :], mixT[:, 1, :], ACT.Exp).then_inc(mix_exp, 1)

            def keep(n, p, before=True):
                for j in range(NCUT):
                    take_rows(n, p, j)
                    if j == 2 and before:
                        hats(n - 1)
                    if j == 5 and before:
                        mix_exps(n - 1)

            def sample(n):
                for q in range(NQ):
                    act.wait_ge(crossed, n * NQ + q + 1)
                    if q == HALF:
                        act.wait_ge(v_ready, 2 * n + 1)
                    w_, at_ = len(blocks(q)) * SB * PH, (q % HALF) * QW
                    nc.scalar.activation(share[:, at_:at_ + w_], ps[0:PH, BANK[4 + q % 2]:BANK[4 + q % 2] + w_], ACT.Copy).then_inc(share_copied, 1)
                act.wait_ge(v_ready, 2 * n + 2)
                nc.scalar.activation(vT[:, :], ps[0:D, BANK[2]:BANK[2] + NS], ACT.Copy).then_inc(vT_ready, 1)

            def sequence(n, p, last=False):
                activations(n, last)
                positions(n)
                if last:
                    hats(n)
                    mix_exps(n)
                else:
                    keep(n + 1, 1 - p)
                sample(n)

            stage_x(0)
            for k in sorted(FRONT):
                FRONT[k](0)
            keep(0, 0, before=False)
            with act.Fori(0, B // 2 - 1) as i:
                for u in range(2):
                    sequence(i * 2 + u, u)
            sequence(B - 2, 0)
            sequence(B - 1, 1, last=True)

        @block.vector
        def _(dve):
            step = Chain(dve, steps, dve_gap)
            dve.wait_ge(weights, LOADED)
            dve.wait_ge(set_up, 2)
            nc.vector.memset(onehot[:, :, :], 0.0)
            nc.vector.memset(rext[:, :, :, :], 0.0)
            nc.vector.memset(heads[:, :, :], 0.0)
            step(nc.vector.tensor_copy(rows[:, :], rowsf[:, :]))
            for p in range(2):
                nc.vector.tensor_copy(rext[:, p, 0:NS, KM + 1], age[:, :])
            for half in range(2):
                for pair in range(NSUP // 2):
                    nc.vector.tensor_scalar(heads[half * RH:(half + 1) * RH, pair, 6 * pair + 3 * half:6 * pair + 3 * half + 3], ps[half * RH:(half + 1) * RH, BANK[0]:BANK[0] + 3], 1.0 / SILU, None, ALU.mult)
            nc.vector.tensor_tensor(hbias[:, :], ps[0:CB, BANK[1]:BANK[1] + 3], bcm[:, :], ALU.add).then_inc(set_up, 1)
            dve.wait_ge(set_up, 3)
            step(nc.vector.memset(n2[:, 3, :], 0.0))
            dve.sem_inc(zeroed, 1)
            H = D // 2
            src = ps[0:T, BANK[1]:BANK[1] + (BR + 1) * D].rearrange("t (r d) -> t r d", d=D)
            rotated = ip[:, 0, :].rearrange("t (r d) -> t r d", d=D)
            unit = ip[:, 1, :].rearrange("t (r d) -> t r d", d=D)
            hats = hat[:, :, :].rearrange("p w (b v) -> p w b v", v=PH)
            per = lambda v: v.rearrange("b (s k) -> b s k", k=KM)

            def rotate(n, p):
                dve.wait_ge(ip_made, n + 1)
                cos2, sin = turn[:, 0:D], turn[:, D:D + H]
                nc.vector.tensor_tensor(ta[:, :, :], src, outer(cos2, BR + 1), ALU.mult)
                nc.vector.tensor_tensor(tb[:, :, 0:H], src[:, :, H:D], outer(sin, BR + 1), ALU.mult)
                step(nc.vector.tensor_tensor(tb[:, :, H:D], src[:, :, 0:H], outer(sin, BR + 1), ALU.mult))
                nc.vector.tensor_tensor(rotated[:, :, 0:H], ta[:, :, 0:H], tb[:, :, 0:H], ALU.subtract)
                step(nc.vector.tensor_tensor(rotated[:, :, H:D], ta[:, :, H:D], tb[:, :, H:D], ALU.add))
                step(nc.vector.tensor_tensor(ta[:, :, :], rotated, rotated, ALU.mult))
                nc.vector.tensor_reduce(n2[:, 0, :], ta[:, :, :], X, ALU.add).then_inc(ip_squared, 1)

            def to_unit(n, p):
                dve.wait_ge(n_ready, n + 1)
                step(nc.vector.tensor_scalar(n2[:, 2, :], n2[:, 1, :], 1e-12, None, ALU.max))
                step(nc.vector.reciprocal(n2[:, 3, :], n2[:, 2, :]))
                nc.vector.tensor_tensor(unit, rotated, inner(n2[:, 3, :], D), ALU.mult).then_inc(ip_ready, 1)

            def take_products(n, p):
                dve.wait_ge(products, n + 1)
                nc.vector.scalar_tensor_tensor(logits[:, :, :], ps[0:T, BANK[0]:BANK[0] + BR * T].rearrange("t (r s) -> t r s", s=T), D ** -0.5, outer(causal[:, :], BR), ALU.mult, ALU.add)
                nc.vector.tensor_scalar(rext[:, p, 0:NS, KM], ps[0:T, BANK[1]:BANK[1] + NS], 1.0, -1.0, ALU.min, ALU.max)
                step(nc.vector.tensor_scalar(gram[:, :], ps[0:T, BANK[1] + NS:BANK[1] + NS + T], 1.0, -1.0, ALU.min, ALU.max), gap=True)

            def best(lo):
                for r in range(BR):
                    ins = nc.vector.max(top[:, r, lo:lo + 8], logits[:, r, :])
                step(ins, gap=True)

            def where(lo):
                for r in range(BR):
                    ins = nc.vector.max_index(at[:, r, lo:lo + 8], top[:, r, lo:lo + 8], logits[:, r, :])
                step(ins, gap=True)

            def strike(n, p):
                for r in range(BR):
                    ins = nc.vector.match_replace(logits[:, r, :], top[:, r, 0:8], logits[:, r, :], GONE)
                step(ins, gap=True)

            def indices(n, p):
                where(8)
                step(nc.vector.tensor_copy(atf[:, :, :], at[:, :, :]))
                nc.vector.tensor_tensor(atf[:, :, :], atf[:, :, :], outer(shift[:, :], BR), ALU.add).then_inc(at_ready, 1)

            FRONT = {2: rotate, 4: to_unit, 8: take_products, 9: lambda n, p: best(0), 10: lambda n, p: where(0),
                     11: strike, 12: lambda n, p: best(8), 13: indices}

            def relations(n, p, last):
                for s in range(NSUP):
                    dve.wait_ge(related, n * NSUP + s + 1)
                    if s >= 2:
                        dve.wait_ge(hidden_ready, n * NSUP + s - 1)
                    nc.vector.tensor_tensor(rel[:, s % 2, :], ps[0:RB_, BANK[6 + s % 2]:BANK[6 + s % 2] + SW], own[:, :], ALU.mult).then_inc(rel_ready, 1)
                    if not last and s in FRONT:
                        FRONT[s](n + 1, 1 - p)

            def distances(n):
                dve.wait_ge(z_ready, n + 1)
                step(nc.vector.tensor_scalar(g[:, :, :], z[:, :, :], 1.0, 0.5 * (PH - 1), ALU.add, ALU.mult))
                step(nc.vector.tensor_scalar(g[:, :, :], g[:, :, :], 0.0, PH - 1.0, ALU.max, ALU.min))
                nc.vector.tensor_tensor(hat[:, :, :].rearrange("p w (b v) -> p (w b) v", v=PH), inner(g[:, :, :].rearrange("p w b -> p (w b)"), PH), outer(grid[:, :], 2 * NB), ALU.subtract).then_inc(away, 1)

            def centre_mix(n):
                dve.wait_ge(mix_turned, n + 1)
                step(nc.vector.tensor_tensor(mixT[:, 0, :], ps[0:NB, BANK[0]:BANK[0] + CB], soft[:, :], ALU.add))
                step(nc.vector.tensor_reduce(msum[:, 0, :], per(mixT[:, 0, :]), X, ALU.max))
                nc.vector.tensor_tensor(per(mixT[:, 1, :]), per(mixT[:, 0, :]), inner(msum[:, 0, :], KM), ALU.subtract).then_inc(mix_centred, 1)

            def shares(n):
                dve.wait_ge(mix_exp, n + 1)
                step(nc.vector.tensor_reduce(msum[:, 1, :], per(mixT[:, 2, :]), X, ALU.add))
                step(nc.vector.reciprocal(msum[:, 2, :], msum[:, 1, :]))
                nc.vector.tensor_tensor(per(mixT[:, 3, :]), per(mixT[:, 2, :]), inner(msum[:, 2, :], KM), ALU.mult).then_inc(shares_ready, 1)

            def keep(n, p, before=True):
                dve.wait_ge(at_turned, n + 1)
                nc.vector.tensor_tensor(spread[:, :].rearrange("r (t k) -> r t k", k=KM), inner(ps[0:BR * KS, BANK[0]:BANK[0] + T], KM), outer(pick[:, :], T), ALU.mult).then_inc(spread_ready, 1)
                for j in range(NCUT):
                    _, _, a0, b0 = sites(j // 3, CUT[j % 3])
                    dve.wait_ge(keys_spread, n * NCUT + j + 1)
                    nc.vector.tensor_scalar(onehot[:, p, a0:b0], ps[0:T, BANK[2 + j % 2]:BANK[2 + j % 2] + b0 - a0], key[:, 0:1], None, ALU.is_equal).then_inc(onehot_ready, 1)
                    if before and j == 1:
                        distances(n - 1)
                    if before and j == 3:
                        centre_mix(n - 1)
                    if before and j == 7:
                        shares(n - 1)

            def sample(n):
                dve.wait_ge(shares_turned, n + 1)
                dve.wait_ge(hat_ready, 2 * n + 2)
                ins = nc.vector.tensor_tensor(hats[:, 1], hats[:, 1], inner(ps[0:CB, BANK[1]:BANK[1] + NB], PH), ALU.mult)
                ins.then_inc(hats_ready, 1)
                dve.wait_ge(hats_ready, n + 1)
                for q in range(NQ):
                    if q >= 2:
                        dve.wait_ge(crossed, n * NQ + q - 1)
                    nb, b0 = len(blocks(q)), q * SUP
                    to = across[:, q % 2, 0:nb * SB * PH].rearrange("p (b s x) -> p b s x", s=SB, x=PH)
                    nc.vector.tensor_tensor(to, outer(hats[:, 0, b0:b0 + nb], SB, 2), outer(inner(site[:, :], PH), nb), ALU.mult).then_inc(across_ready, 1)
                dve.wait_ge(y_ready, n + 1)
                group = m.h[:, bass.ds(n * D, D)]
                nc.vector.scalar_tensor_tensor(group, ps[0:T, BANK[2]:BANK[2] + D], 1.0 / BR, group, ALU.mult, ALU.add).then_inc(added, 1)

            def sequence(n, p, last=False):
                relations(n, p, last)
                if last:
                    distances(n)
                    centre_mix(n)
                    shares(n)
                else:
                    keep(n + 1, 1 - p)
                sample(n)

            for s in sorted(FRONT):
                FRONT[s](0, 0)
            keep(0, 0, before=False)
            N = 18
            with dve.Fori(0, B // 2 - 1) as i:
                step.begin(i, 2 * N)
                for u in range(2):
                    sequence(i * 2 + u, u)
                step.end(B // 2 - 1)
            sequence(B - 2, 0)
            sequence(B - 1, 1, last=True)


class Memory:
    pass


def program(nc, c, out):
    with ExitStack() as ctx:
        h = ctx.enter_context(nc.sbuf_tensor("h", [T, F], F32))
        xn = ctx.enter_context(nc.sbuf_tensor("xn", [T, F + D], F32))
        ident = ctx.enter_context(nc.sbuf_tensor("ident", [128, 128], F32))
        ones = ctx.enter_context(nc.sbuf_tensor("ones", [1, 512], F32))
        ps = ctx.enter_context(nc.psum_tensor("ps", [128, 4096], F32))
        m = Memory()
        m.h, m.ident, m.ones, m.ps, m.xn = h, ident, ones, ps, xn
        tokens(nc, m, c)
        layer_norm(nc, m, m.h[:, :], m.h[:, :], "tok_ln", c["tok_gamma"], c["tok_beta"])
        shifted = xn[:, D:D + F]
        layer_norm(nc, m, h[:, :], shifted, "fw_ln")
        add_in(nc, h[:, :], shifted, "fw_skip")
        layer_norm(nc, m, shifted, shifted, "fw_ln2", c["fw_gain"], c["fw_shift"])
        fast_weights(nc, m, c)
        layer_norm(nc, m, h[:, :], xn[:, 0:F], "mod_ln")
        depth_ffn(nc, m, c)
        layer_norm(nc, m, h[:, :], xn[:, 0:F], "win_ln")
        window_attention(nc, m, c)
        layer_norm(nc, m, h[:, :], xn[:, 0:F], "top1_ln")
        top1_experts(nc, m, c)
        layer_norm(nc, m, h[:, :], xn[:, 0:F], "pair_ln")
        pair_attention(nc, m, c)
        layer_norm(nc, m, h[:, :], xn[:, 0:F], "gate_ln")
        gated_ffn(nc, m, c)
        layer_norm(nc, m, h[:, :], xn[:, 0:F], "pal_ln")
        palette_attention(nc, m, c)
        layer_norm(nc, m, h[:, :], xn[:, 0:F], "moe_ln")
        top2_experts(nc, m, c)
        with nc.semaphore("out_stored") as out_stored, nc.Block() as block:
            @block.sync
            def _(sp):
                sp.dma_start(out.rearrange("b t d -> t b d"), h[:, :].rearrange("t (b d) -> t b d", d=D)).then_inc(out_stored, 16)
                sp.wait_ge(out_stored, 16)


def add_in(nc, acc, more, tag):
    with nc.Block() as block:
        @block.vector
        def _(dve):
            nc.vector.tensor_tensor(acc, acc, more, ALU.add)


def laid_out(inp):
    f = {k: np.asarray(v) for k, v in inp.items()}
    a = {}
    a["ident"] = np.eye(128, dtype=np.float32)
    a["ones"] = np.ones((1, 512), np.float32)
    x = f["x"].reshape(B, -1)[:, :ROWS * PATCH_COLS].reshape(B, ROWS, PATCH_COLS)
    a["tok_rows"] = x.transpose(2, 0, 1).reshape(PATCH_COLS, B * ROWS)
    a["tok_w"] = f["L0_tok_W"].reshape(D, 2, 128).transpose(2, 1, 0).reshape(128, 2 * D)
    a["tok_b"] = f["L0_tok_b"].reshape(1, D)
    a["tok_gamma"] = f["L0_tok_gamma"].reshape(1, D)
    a["tok_beta"] = f["L0_tok_beta"].reshape(1, D)
    w = f["L0_attn_slow_W"].reshape(HEADS, 5 * DH + 2, D)
    cut = [w[:, k * DH:(k + 1) * DH].reshape(HEADS * DH, D) for k in range(5)]
    q, k, v, rk, rv = cut
    a["fw_w"] = np.concatenate([q, k, rk, v, rv, w[:, 5 * DH], w[:, 5 * DH + 1]]).T
    a["fw_w_out"] = f["L0_attn_out_W"].reshape(D, 2, 128).transpose(2, 1, 0).reshape(128, 2 * D)
    a["fw_gain"] = f["L0_attn_ln_g"].reshape(1, D)
    a["fw_shift"] = f["L0_attn_ln_b"].reshape(1, D)
    a["mod_w1"] = f["L0_ffn_w1"]
    a["mod_b1"] = f["L0_ffn_b1"].reshape(2, 128).T
    a["mod_w2"] = f["L0_ffn_w2"].reshape(2, 128, D).transpose(1, 0, 2).reshape(128, 2 * D)
    a["mod_b2"] = f["L0_ffn_b2"].reshape(1, D)
    a["mod_wr"] = f["L0_ffn_wr"].reshape(1, D)
    a["mod_br"] = f["L0_ffn_br"].reshape(1, 1)
    a["win_w"] = np.concatenate([f["L1_attn_qkv_w"], f["L1_attn_qkv_b"][None]])
    a["win_proj"] = np.concatenate([f["L1_attn_proj_w"], f["L1_attn_proj_b"][None]])
    at = np.arange(WIN)
    a["win_bias"] = f["L1_attn_rel_bias"][at[None, :] - at[:, None] + WIN - 1].transpose(2, 0, 1).reshape(1, -1)
    a["count"] = np.arange(128, dtype=np.float32)[None]
    a["top1_wr"] = np.concatenate([f["L1_ffn_router_w"].T, f["L1_ffn_router_b"][None]])
    a["top1_w1"] = np.concatenate([f["L1_ffn_W1"].transpose(1, 0, 2).reshape(D, E1 * H1), f["L1_ffn_b1"].reshape(1, -1)])
    a["top1_w2"] = f["L1_ffn_W2"].reshape(-1, 128, D).transpose(1, 0, 2).reshape(128, -1)
    a["top1_b2"] = f["L1_ffn_b2"]
    a["top1_spread"] = np.repeat(np.eye(E1, dtype=np.float32), H1, axis=1)
    v = f["L2_attn_Wv"].T.reshape(D, DG, NGRP).transpose(0, 2, 1).reshape(D, D)
    a["pair_w"] = np.concatenate([f["L2_attn_Wq"].T, f["L2_attn_Wk"].T, v], axis=1)
    mlp = np.zeros((2, NGRP, DG, 2, NGRP), np.float32)
    for s in range(2):
        for g in range(NGRP):
            mlp[s, g, :, s, g] = f["L2_attn_w_mlp"]
    a["pair_mlp"] = mlp.reshape(128, 2 * NGRP)
    a["pair_b"] = f["L2_attn_b_mlp"].reshape(1, 1)
    a["gate_w1"] = f["L2_ffn_W1"]
    a["gate_b1"] = f["L2_ffn_b1"].reshape(2, 128).T
    a["gate_wg"] = f["L2_ffn_Wg"].reshape(2, 128, E2).transpose(1, 0, 2).reshape(128, -1)
    a["gate_bg"] = f["L2_ffn_bg"].reshape(1, E2)
    a["gate_wd"] = f["L2_ffn_Wd"].reshape(E2, 2, 128, D).transpose(2, 1, 0, 3).reshape(128, -1)
    a["gate_bd"] = f["L2_ffn_bd"].reshape(1, -1)
    halves = lambda w, r: w.reshape(D, r, D // 2, 2).transpose(0, 1, 3, 2).reshape(D, r * D)
    a["pal_w"] = np.concatenate([halves(f["L3_attn_Wi"], BR), halves(f["L3_attn_Wp"], 1)], axis=1)
    angle = np.outer(np.arange(T, dtype=np.float32), 1.0 / 10000.0 ** (np.arange(0, D, 2, dtype=np.float32) / D))
    cos, sin = np.cos(angle), np.sin(angle)
    a["pal_turn"] = np.concatenate([cos, cos, sin, sin], axis=1).astype(np.float32)
    t, k = np.arange(T), np.arange(KS)
    a["pal_causal"] = np.where(t[None, :] > t[:, None], MASKED, 0.0).astype(np.float32)
    a["pal_shift"] = np.where(k[None, :] > t[:, None], 128.0, 0.0).astype(np.float32)
    q = np.arange(NS) % T
    a["pal_age"] = (np.maximum(q[None, :] - t[:, None], 0).astype(np.float32) / np.float32(T)).astype(np.float32)
    a["pal_key"] = t.astype(np.float32)[:, None]
    place = np.arange(BR * KS)
    a["pal_pick"] = (place[:, None] % KS == np.arange(KM)[None]).astype(np.float32)
    a["pal_rows"] = (place[:, None] // KS == np.arange(NS)[None] // T).astype(np.float32)
    a["pal_own"] = (np.arange(RB_)[:, None] // REL == np.arange(SW)[None] % CB // KM).astype(np.float32)
    a["pal_w1"] = np.tile(f["L3_attn_W1"], (SB, 1))
    a["pal_b1"] = np.tile(f["L3_attn_b1"], 2).reshape(2 * RH, 1)
    a["pal_w2T"] = f["L3_attn_W2"].T
    a["pal_b2"] = np.repeat(f["L3_attn_b2"][:, None], CB, axis=1)
    a["pal_wcm"] = np.concatenate([f["L3_attn_Wc"], f["L3_attn_Wm"]], axis=1)
    a["pal_bcm"] = np.repeat(np.concatenate([f["L3_attn_bc"], f["L3_attn_bm"]])[None], CB, axis=0)
    col = np.arange(CB)
    s = np.arange(NB)[:, None] * SB + col[None] // KM
    a["pal_soft"] = np.where((col[None] % KM > s % T) & (s < NS), MASKED, 0.0).astype(np.float32)
    a["pal_grid"] = np.repeat(np.arange(PH, dtype=np.float32)[None], CB, axis=0)
    a["pal_site"] = (col[:, None] // KM == np.arange(SB)[None]).astype(np.float32)
    a["pal_palette"] = f["L3_attn_palette"].reshape(D, PH, PH).transpose(1, 2, 0).reshape(PH, PH * D)
    a["pal_wo"] = f["L3_attn_Wo"].transpose(1, 0, 2).reshape(D, BR * D)
    a["moe_wg"] = np.concatenate([f["L3_ffn_Wg"], f["L3_ffn_bg"][None]])
    a["moe_w1"] = f["L3_ffn_W1"].transpose(1, 0, 2).reshape(D, -1)
    a["moe_b1"] = f["L3_ffn_b1"].reshape(2 * E2, 128).T
    a["moe_w2"] = f["L3_ffn_W2"].reshape(2 * E2, 128, D).transpose(1, 0, 2).reshape(128, -1)
    a["moe_b2"] = f["L3_ffn_b2"].reshape(1, -1)
    return {k: np.ascontiguousarray(v) for k, v in a.items()}




def kernel(**inputs):
    import concourse.bacc as bacc
    from concourse.bass_utils import run_bass_kernel_spmd

    nc = bacc.Bacc("TRN2", target_bir_lowering=False, num_devices=1)
    arrays = laid_out(inputs)
    c = {k: nc.dram_tensor(k + "_in", v.shape, mybir.dt.from_np(v.dtype), kind="ExternalInput").ap() for k, v in arrays.items()}
    out = nc.dram_tensor("out", (B, T, D), F32, kind="ExternalOutput").ap()
    program(nc, c, out)
    r = run_bass_kernel_spmd(nc, [{k + "_in": v for k, v in arrays.items()}], core_ids=[0])
    return r.results[0]["out"]
```
